# Optimizing a Trainium2 kernel written in Bass

```python
import numpy as np
import jax
import jax.numpy as jnp

def _softmax(x, axis=-1):
    return jax.nn.softmax(x, axis=axis)

def _gelu(x):
    return jax.nn.gelu(x, approximate=True)

def _silu(x):
    return jax.nn.silu(x)

def _sigmoid(x):
    return jax.nn.sigmoid(x)

def _layernorm(x, axis=-1, eps=1e-05):
    m = jnp.mean(x, axis=axis, keepdims=True)
    v = jnp.var(x, axis=axis, keepdims=True)
    return (x - m) / jnp.sqrt(v + eps)

def _scatter_add(tgt, idx, src, axis=0):
    return tgt.at[idx].add(src)

def _segment_sum(src, seg, n):
    return jax.ops.segment_sum(src, seg, n)
kernel_name = 'mk_xattn_ffn_d2_seqx_r4_265fa9'

def setup_inputs(seed: int=0):
    np.random.seed(seed)
    _w = jnp.asarray

    def _rec_inputs():
        import jax
        import jax.numpy as jnp
        _rk = jax.random.key(seed)
        x = -0.0002928 + 1 * jax.random.normal(jax.random.fold_in(_rk, 1), (2, 1024, 256), jnp.float32)
        _lenS = 1024 - jax.random.randint(jax.random.fold_in(_rk, 7), (2,), 0, max(1, 1024 // 4) + 1, jnp.int32)
        _lenS2 = 77 - jax.random.randint(jax.random.fold_in(_rk, 8), (2,), 0, max(1, 77 // 4) + 1, jnp.int32)
        _ctx_1024P = jax.random.normal(jax.random.fold_in(_rk, 11), (2, 16, 256), jnp.float32)
        _ctx_1024c = jax.random.dirichlet(jax.random.fold_in(_rk, 511), 0.3 * jnp.ones((16,), jnp.float32), (2, 77))
        _ctx_1024t = jnp.einsum('bsk,bkd->bsd', _ctx_1024c, _ctx_1024P)
        _ctx_1024t = _ctx_1024t * jax.lax.rsqrt(jnp.mean(jnp.square(_ctx_1024t)) + 1e-12) * 0.953939
        ctx_1024 = -1.39393e-06 + 0.999914 * (_ctx_1024t + 0.3 * jax.random.normal(jax.random.fold_in(_rk, 611), (2, 77, 256), jnp.float32))
        itok_BxS_0_511 = jax.random.randint(jax.random.fold_in(_rk, 12), (2, 1024), 0, 128, jnp.int32)
        return (x, ctx_1024, itok_BxS_0_511)
    x, ctx_1024, itok_BxS_0_511 = _rec_inputs()

    def _L0_xattn_setup():
        import jax, jax.numpy as jnp
        import numpy as np
        B, S, D, H = (2, 512, 256, 16)
        HD = D // H

        def _split_heads(x):
            b, s, _ = x.shape
            return x.reshape(b, s, H, HD).transpose(0, 2, 1, 3)
        key = jax.random.key(seed)
        ks = jax.random.split(key, 11)
        s = 0.02
        return {'query': jax.random.normal(ks[0], (B, S, D), jnp.float32), 'key_in': jax.random.normal(ks[1], (B, S, D), jnp.float32), 'value': jax.random.normal(ks[2], (B, S, D), jnp.float32), 'Wq': jax.random.normal(ks[3], (D, D), jnp.float32) * s, 'bq': jnp.zeros((D,), jnp.float32), 'Wk': jax.random.normal(ks[4], (D, D), jnp.float32) * s, 'bk': jnp.zeros((D,), jnp.float32), 'Wv': jax.random.normal(ks[5], (D, D), jnp.float32) * s, 'bv': jnp.zeros((D,), jnp.float32), 'Wo': jax.random.normal(ks[6], (D, D), jnp.float32) * s, 'bo': jnp.zeros((D,), jnp.float32)}
    _L0_xattn_all = _L0_xattn_setup()
    _L0_xattn_in = {k: v for k, v in _L0_xattn_all.items() if k in ('Wq', 'bq', 'Wk', 'bk', 'Wv', 'bv', 'Wo', 'bo')}
    del _L0_xattn_all

    def _L0_ffn_setup():
        import jax, jax.numpy as jnp
        import numpy as np
        K = 2
        key = jax.random.key(seed)
        ks = jax.random.split(key, 9)
        B, S, D, O, E = (4, 256, 256, 256, 8)
        sc = 0.02
        return {'x': jax.random.normal(ks[0], (B, S, D), dtype=jnp.float32), 'gate_w': jax.random.normal(ks[1], (D, E), dtype=jnp.float32) * sc, 'gate_b': jax.random.normal(ks[2], (E,), dtype=jnp.float32) * sc, 'w1': jax.random.normal(ks[3], (E, D, O), dtype=jnp.float32) * sc, 'b1': jax.random.normal(ks[4], (E, O), dtype=jnp.float32) * sc, 'w2': jax.random.normal(ks[5], (E, O, O), dtype=jnp.float32) * sc, 'b2': jax.random.normal(ks[6], (E, O), dtype=jnp.float32) * sc, 'w3': jax.random.normal(ks[7], (E, O, O), dtype=jnp.float32) * sc, 'b3': jax.random.normal(ks[8], (E, O), dtype=jnp.float32) * sc}
    _L0_ffn_all = _L0_ffn_setup()
    _L0_ffn_in = {k: v for k, v in _L0_ffn_all.items() if k in ('gate_w', 'gate_b', 'w1', 'b1', 'w2', 'b2', 'w3', 'b3')}
    del _L0_ffn_all

    def _L1_xattn_setup():
        import jax, jax.numpy as jnp
        import numpy as np
        Q_DIM, KV_DIM = (256, 256)
        H, HD, KVC, QC, R = (16, 64, 64, 96, 64)
        LOOKBACK = 2
        B, LQ, LK = (4, 512, 128)

        def _rope(x, pos):
            r = x.shape[-1]
            half = r // 2
            inv = 1.0 / 10000.0 ** (jnp.arange(half, dtype=jnp.float32) / half)
            ang = pos[..., None].astype(jnp.float32) * inv
            cos, sin = (jnp.cos(ang), jnp.sin(ang))
            x1, x2 = (x[..., :half], x[..., half:])
            return jnp.concatenate([x1 * cos - x2 * sin, x1 * sin + x2 * cos], axis=-1)
        key = jax.random.key(seed)
        ks = jax.random.split(key, 11)
        w = lambda k, shape: jax.random.normal(k, shape, jnp.float32) / np.sqrt(shape[0]).astype(np.float32)
        return {'q': jax.random.normal(ks[0], (B, LQ, Q_DIM), jnp.float32), 'kv': jax.random.normal(ks[1], (B, LK, KV_DIM), jnp.float32), 'seg_id': jnp.sort(jax.random.randint(ks[2], (B, LQ), 0, LK), axis=-1), 'w_kv_comp': w(ks[3], (KV_DIM, KVC)), 'w_q_down': w(ks[4], (Q_DIM, QC)), 'w_q_up': w(ks[5], (QC, H * HD)), 'w_q_rope': w(ks[6], (QC, H * R)), 'w_k_up': w(ks[7], (KVC, H * HD)), 'w_k_rope': w(ks[8], (KVC, R)), 'w_v_up': w(ks[9], (KVC, H * HD)), 'w_out': w(ks[10], (H * HD, Q_DIM))}
    _L1_xattn_all = _L1_xattn_setup()
    _L1_xattn_in = {k: v for k, v in _L1_xattn_all.items() if k in ('w_kv_comp', 'w_q_down', 'w_q_up', 'w_q_rope', 'w_k_up', 'w_k_rope', 'w_v_up', 'w_out')}
    del _L1_xattn_all

    def _L1_ffn_setup():
        import jax, jax.numpy as jnp
        import numpy as np
        TOP_K = 2
        key = jax.random.key(seed)
        k1, k2, k3 = jax.random.split(key, 3)
        B, S, H, E = (4, 512, 256, 8)
        hidden_states = jax.random.normal(k1, (B, S, H), dtype=jnp.float32)
        Wg = jax.random.normal(k2, (H, E), dtype=jnp.float32) * H ** (-0.5)
        We = jax.random.normal(k3, (E, H, H), dtype=jnp.float32) * H ** (-0.5)
        be = jnp.zeros((E, H), dtype=jnp.float32)
        return {'hidden_states': hidden_states, 'Wg': Wg, 'We': We, 'be': be}
    _L1_ffn_all = _L1_ffn_setup()
    _L1_ffn_in = {k: v for k, v in _L1_ffn_all.items() if k in ('Wg', 'We', 'be')}
    del _L1_ffn_all
    return {'x': x, 'ctx_1024': ctx_1024, 'itok_BxS_0_511': itok_BxS_0_511, 'L0_xattn_Wq': _L0_xattn_in['Wq'], 'L0_xattn_bq': _L0_xattn_in['bq'], 'L0_xattn_Wk': _L0_xattn_in['Wk'], 'L0_xattn_bk': _L0_xattn_in['bk'], 'L0_xattn_Wv': _L0_xattn_in['Wv'], 'L0_xattn_bv': _L0_xattn_in['bv'], 'L0_xattn_Wo': _L0_xattn_in['Wo'], 'L0_xattn_bo': _L0_xattn_in['bo'], 'L0_ffn_gate_w': _L0_ffn_in['gate_w'], 'L0_ffn_gate_b': _L0_ffn_in['gate_b'], 'L0_ffn_w1': _L0_ffn_in['w1'], 'L0_ffn_b1': _L0_ffn_in['b1'], 'L0_ffn_w2': _L0_ffn_in['w2'], 'L0_ffn_b2': _L0_ffn_in['b2'], 'L0_ffn_w3': _L0_ffn_in['w3'], 'L0_ffn_b3': _L0_ffn_in['b3'], 'L1_xattn_w_kv_comp': _L1_xattn_in['w_kv_comp'], 'L1_xattn_w_q_down': _L1_xattn_in['w_q_down'], 'L1_xattn_w_q_up': _L1_xattn_in['w_q_up'], 'L1_xattn_w_q_rope': _L1_xattn_in['w_q_rope'], 'L1_xattn_w_k_up': _L1_xattn_in['w_k_up'], 'L1_xattn_w_k_rope': _L1_xattn_in['w_k_rope'], 'L1_xattn_w_v_up': _L1_xattn_in['w_v_up'], 'L1_xattn_w_out': _L1_xattn_in['w_out'], 'L1_ffn_Wg': _L1_ffn_in['Wg'], 'L1_ffn_We': _L1_ffn_in['We'], 'L1_ffn_be': _L1_ffn_in['be']}

def reference(x, ctx_1024, itok_BxS_0_511, L0_xattn_Wq, L0_xattn_bq, L0_xattn_Wk, L0_xattn_bk, L0_xattn_Wv, L0_xattn_bv, L0_xattn_Wo, L0_xattn_bo, L0_ffn_gate_w, L0_ffn_gate_b, L0_ffn_w1, L0_ffn_b1, L0_ffn_w2, L0_ffn_b2, L0_ffn_w3, L0_ffn_b3, L1_xattn_w_kv_comp, L1_xattn_w_q_down, L1_xattn_w_q_up, L1_xattn_w_q_rope, L1_xattn_w_k_up, L1_xattn_w_k_rope, L1_xattn_w_v_up, L1_xattn_w_out, L1_ffn_Wg, L1_ffn_We, L1_ffn_be):
    import jax
    import jax.numpy as jnp

    def _L0_xattn_ref(query, key_in, value, Wq, bq, Wk, bk, Wv, bv, Wo, bo):
        import jax, jax.numpy as jnp
        import numpy as np
        B, S, D, H = (2, 512, 256, 16)
        HD = D // H

        def _split_heads(x):
            b, s, _ = x.shape
            return x.reshape(b, s, H, HD).transpose(0, 2, 1, 3)
        q = _split_heads(query @ Wq + bq)
        k = _split_heads(key_in @ Wk + bk)
        v = _split_heads(value @ Wv + bv)
        scores = jnp.einsum('bhqd,bhkd->bhqk', q, k) / jnp.sqrt(jnp.float32(HD))
        weights = jax.nn.softmax(scores, axis=-1)
        ctx = jnp.einsum('bhqk,bhkd->bhqd', weights, v)
        ctx = ctx.transpose(0, 2, 1, 3).reshape(query.shape[0], -1, D)
        return ctx @ Wo + bo

    def _L0_ffn_ref(x, gate_w, gate_b, w1, b1, w2, b2, w3, b3):
        import jax, jax.numpy as jnp
        import numpy as np
        K = 2
        E = gate_w.shape[-1]
        logits = jnp.einsum('bsd,de->bse', x, gate_w) + gate_b
        probs = jax.nn.softmax(logits, axis=1)
        vals, idx = jax.lax.top_k(probs, K)
        h = jax.nn.relu(jnp.einsum('bsd,edo->ebso', x, w1) + b1[:, None, None, :])
        h = jax.nn.relu(jnp.einsum('ebso,eop->ebsp', h, w2) + b2[:, None, None, :])
        y = jax.nn.relu(jnp.einsum('ebso,eop->ebsp', h, w3) + b3[:, None, None, :])
        onehot = jax.nn.one_hot(idx, E, dtype=x.dtype)
        w_tok = jnp.einsum('bske,bsk->bse', onehot, vals)
        ind = onehot.max(axis=2)
        v = jnp.einsum('ebso,bse->eo', y, w_tok)
        out = jnp.einsum('bse,eo->bso', ind, v)
        return out

    def _L1_xattn_ref(q, kv, seg_id, w_kv_comp, w_q_down, w_q_up, w_q_rope, w_k_up, w_k_rope, w_v_up, w_out):
        import jax, jax.numpy as jnp
        import numpy as np
        Q_DIM, KV_DIM = (256, 256)
        H, HD, KVC, QC, R = (16, 64, 64, 96, 64)
        LOOKBACK = 2
        B, LQ, LK = (4, 512, 128)

        def _rope(x, pos):
            r = x.shape[-1]
            half = r // 2
            inv = 1.0 / 10000.0 ** (jnp.arange(half, dtype=jnp.float32) / half)
            ang = pos[..., None].astype(jnp.float32) * inv
            cos, sin = (jnp.cos(ang), jnp.sin(ang))
            x1, x2 = (x[..., :half], x[..., half:])
            return jnp.concatenate([x1 * cos - x2 * sin, x1 * sin + x2 * cos], axis=-1)
        b, lq, _ = q.shape
        lk = kv.shape[1]
        kv_c = kv @ w_kv_comp
        qc = q @ w_q_down
        q_nope = (qc @ w_q_up).reshape(b, lq, H, HD)
        q_rope = (qc @ w_q_rope).reshape(b, lq, H, R)
        q_rope = _rope(q_rope, jnp.arange(lq)[None, :, None])
        k_nope = (kv_c @ w_k_up).reshape(b, lk, H, HD)
        k_rope = _rope(kv_c @ w_k_rope, jnp.arange(lk)[None, :])
        v = (kv_c @ w_v_up).reshape(b, lk, H, HD)
        scale = 1.0 / np.sqrt(HD + R).astype(np.float32)
        scores = (jnp.einsum('bqhd,bkhd->bhqk', q_nope, k_nope) + jnp.einsum('bqhr,bkr->bhqk', q_rope, k_rope)) * scale
        k_idx = jnp.arange(lk)[None, None, :]
        q_seg = seg_id[:, :, None]
        good = (k_idx <= q_seg) & (k_idx >= q_seg - LOOKBACK)
        neg = jnp.finfo(scores.dtype).min
        scores = jnp.where(good[:, None, :, :], scores, neg)
        attn = jax.nn.softmax(scores, axis=-1)
        out = jnp.einsum('bhqk,bkhd->bqhd', attn, v).reshape(b, lq, H * HD)
        return out @ w_out

    def _L1_ffn_ref(hidden_states, Wg, We, be):
        import jax, jax.numpy as jnp
        import numpy as np
        TOP_K = 2
        B, S, H = hidden_states.shape
        T = B * S
        x = hidden_states.reshape(T, H)
        probs = jax.nn.softmax(x @ Wg, axis=-1)
        top_vals, top_idx = jax.lax.top_k(probs, TOP_K)
        gates = top_vals / jnp.sum(top_vals, axis=-1, keepdims=True)
        expert_out = jnp.einsum('th,ehd->etd', x, We) + be[:, None, :]
        tok = jnp.arange(T)[:, None]
        sel = expert_out[top_idx, tok, :]
        out = jnp.sum(gates[..., None] * sel, axis=1)
        return out.reshape(B, S, H)
    x = x + _L0_xattn_ref(_layernorm(x, axis=-1), ctx_1024, ctx_1024, L0_xattn_Wq, L0_xattn_bq, L0_xattn_Wk, L0_xattn_bk, L0_xattn_Wv, L0_xattn_bv, L0_xattn_Wo, L0_xattn_bo)
    x = x + _L0_ffn_ref(_layernorm(x, axis=-1), L0_ffn_gate_w, L0_ffn_gate_b, L0_ffn_w1, L0_ffn_b1, L0_ffn_w2, L0_ffn_b2, L0_ffn_w3, L0_ffn_b3)
    x = x + _L1_xattn_ref(_layernorm(x, axis=-1), ctx_1024, itok_BxS_0_511, L1_xattn_w_kv_comp, L1_xattn_w_q_down, L1_xattn_w_q_up, L1_xattn_w_q_rope, L1_xattn_w_k_up, L1_xattn_w_k_rope, L1_xattn_w_v_up, L1_xattn_w_out)
    x = x + _L1_ffn_ref(_layernorm(x, axis=-1), L1_ffn_Wg, L1_ffn_We, L1_ffn_be)
    return x

_drawn_inputs = setup_inputs


def setup_inputs(seed=0):
    import zlib

    import numpy as np

    out = dict(_drawn_inputs(seed))
    spreads = {'L0_xattn_bq': (0.0, 0.558),
     'L0_xattn_bk': (0.0, 0.8),
     'L0_xattn_bv': (0.0, 0.1),
     'L0_xattn_bo': (0.0, 0.1),
     'L1_ffn_be': (0.0, 0.1)}
    factors = {'L0_xattn_Wq': 4.137,
     'L0_xattn_Wk': 3.059,
     'L0_ffn_gate_b': 8.0,
     'L0_ffn_w1': 8.0,
     'L0_ffn_b1': 8.0,
     'L0_ffn_w2': 3.037,
     'L0_ffn_b2': 4.254}
    for name, (base, spread) in spreads.items():
        noise = np.random.default_rng([zlib.crc32(name.encode()), seed]).standard_normal(out[name].shape)
        drawn = base * np.exp(spread * noise) if base else spread * noise
        out[name] = jnp.asarray(drawn.astype(out[name].dtype))
    for name, factor in factors.items():
        out[name] = (out[name] * factor).astype(out[name].dtype)
    return out
```

```python
import numpy as np
import concourse.bass as bass
from concourse import mybir
from contextlib import ExitStack

P = 128
B = 2
S = 1024
D = 256
DK = D // P
TPB = S // P
NT = B * TPB
LK = 77
H = 16
HC = H // 2
UK = HC * LK
NJ = -(-UK // P)
HD = D // H
E = 8
NL = 3
TOP = 2
NCH = (TOP * B * S + E * (P - 1)) // P
NSTR = 3
NIT = NCH // NSTR
DQ = 96
DC = 64
RD = 64
NP2 = H // 2
SCALE = float(np.float32(1.0) / np.float32(np.sqrt(np.float32(2 * RD))))
FMIN = float(np.finfo(np.float32).min)
PAD = P + 2 * LK + P
VW1 = HD + 1


def rows(j):
    return min(P, UK - P * j)


def heads_of(j):
    h0 = P * j // LK
    return h0, (P * j + rows(j) - 1) // LK - h0 + 1


def v_unit(q):
    return q // (2 * NJ), q // NJ % 2, q % NJ


def bcast(ap, axis, n):
    u = ap.unsqueeze(axis)
    shape = list(u.shape)
    shape[axis] = n
    return u.broadcast_to(shape)


def build(nc, io):
    F32 = mybir.dt.float32
    I32 = mybir.dt.int32
    ALU = mybir.AluOpType
    ACT = mybir.ActivationFunctionType
    AX = mybir.AxisListType

    with ExitStack() as st:
        def sb(name, shape, dt=F32):
            return st.enter_context(nc.sbuf_tensor(name, shape, dt))

        def sem(name):
            return st.enter_context(nc.semaphore(name))

        ps = st.enter_context(nc.psum_tensor("ps", [P, 8, 512], F32))

        x = sb("x", [P, B, TPB, D])
        ident = sb("ident", [P, P])
        stats = sb("stats", [P, 2, 6])
        st_all = sb("st_all", [P, B, TPB, 6])
        xs = sb("xs", [P, 2, D])
        mv = sb("mv", [P, B, TPB, 2])
        rstd = sb("rstd", [P, B, TPB])
        epsv = sb("epsv", [P, B, TPB])
        power = sb("power", [P, B, TPB])
        xn = sb("xn", [P, 2, D])
        xnT = sb("xnT", [P, 2, DK, P])
        w0 = sb("w0", [P, E, NL, DK, D])
        b0 = sb("b0", [P, E, NL, D])
        wqd = sb("wqd", [P, DK, DQ])
        wr2 = sb("wr2", [DQ, H, 2 * RD])
        trig = sb("trig", [P, S])
        negm = sb("negm", [P, NT, LK])
        seg_i = sb("seg_i", [P, NT], I32)
        seg = sb("seg", [P, 2, NT])
        iok = sb("iok", [P, LK])
        anope = sb("anope", [DQ, B, H, LK])
        kr2 = sb("kr2", [P, B, LK])
        vw = sb("vw", [P, B, 2, NJ, D])
        knT = vw[:].rearrange("p b c j d -> p (b c j d)")[:, 0:NP2 * B * LK].rearrange("p (q b k) -> p q b k", q=NP2, b=B)
        room = b0[:].rearrange("p e l d -> p (e l d)")
        at = [0]

        def carve(cols):
            at[0] += cols
            return room[:, at[0] - cols:at[0]]

        wkup = carve(H * RD)[0:DC]
        wvup = carve(H * RD)[0:DC]
        wqupT = carve(NP2 * DQ).rearrange("p (q c) -> p q c", q=NP2)
        wout = carve(NP2 * D).rearrange("p (q d) -> p q d", q=NP2)
        wkvc = carve(DK * DC).rearrange("p (k c) -> p k c", k=DK)
        wkr = carve(2 * 2 * RD).rearrange("p (v r) -> p v r", v=2)[0:DC]
        kvcT = carve(B * LK)[0:DC]
        krt = carve(2 * LK).rearrange("p (v k) -> p v k", v=2)
        kruv = carve(2 * B * LK).rearrange("p (v b k) -> p v b k", v=2, b=B)
        gw = sb("gw", [P, DK, E])
        gb = sb("gb", [E, 1])
        ctxT = sb("ctxT", [P, DK, B, LK])
        phase = ExitStack()

        def sb(name, shape, dt=F32):
            return phase.enter_context(nc.sbuf_tensor(name, shape, dt))

        wq = sb("wq", [P, DK, D])
        wk = sb("wk", [P, DK, D])
        wv = sb("wv", [P, DK, D])
        wo = sb("wo", [P, DK, D])
        bq = sb("bq", [P, 2])
        bk = sb("bk", [P, 2])
        bv = sb("bv", [P, D])
        bo = sb("bo", [P, D])
        kmask = sb("kmask", [P, HC])
        vmask = sb("vmask", [P, NJ, HC])
        ctx = sb("ctx", [LK, B, D])
        ctx_rep = sb("ctx_rep", [P, DK, B, HC, LK])
        kT = sb("kT", [P, 2, B, LK])
        kbd = sb("kbd", [P, B, 2, HC, LK])
        vbd = sb("vbd", [P, B, 2, NJ, HC, VW1])
        vtmp = sb("vtmp", [P, 2, 4, P])
        qT = sb("qT", [P, 2, 2, P])
        pr = sb("pr", [P, 2, HC, LK])
        prT = sb("prT", [P, 2, NJ, P])
        nmax = sb("nmax", [P, 2, HC])
        rsum = sb("rsum", [P, 2, HC])
        on = sb("on", [P, 2, HC, HD])
        oT = sb("oT", [P, 2, P])

        phase.close()
        phase = ExitStack()
        lg = sb("lg", [E, B, S])
        gmax = sb("gmax", [E, B])
        gsum = sb("gsum", [E, B])
        prob = sb("prob", [P, NT, E])
        top = sb("top", [P, TOP, NT])
        key = sb("key", [P, NT, E])
        kmax = sb("kmax", [P, NT])
        oneh = sb("oneh", [P, TOP, NT, E])
        sel = sb("sel", [P, NT, E])
        prob2 = sb("prob2", [P, NT, E])
        cmp16 = sb("cmp16", [P, E, NT])
        nch = sb("nch", [P, E])
        tri8 = sb("tri8", [P, E, E])
        cend = sb("cend", [P, E])
        base = sb("base", [P, E])
        pos = sb("pos", [P, NT, E])
        slot = sb("slot", [P, TOP * NT])
        slot_i = sb("slot_i", [P, 3, TOP * NT], I32)
        rc = sb("rc", [P, 2, TOP * NT])
        rowhot = sb("rowhot", [P, 2, 8, P])
        chhot = sb("chhot", [P, TOP * NT, NCH])
        payload = sb("payload", [P, TOP * NT, 2, NCH])
        cmp8 = sb("cmp8", [P, NCH, E])
        ce = sb("ce", [P, NCH])
        ce_i = sb("ce_i", [P, NCH], I32)
        tok_i = sb("tok_i", [P, NCH], I32)
        wslot = sb("wslot", [P, NCH])
        wexp = sb("wexp", [P, NCH, E])
        indT = sb("indT", [E, NT, P])
        tri = sb("tri", [P, P])
        ones = sb("ones", [P, P])
        iot = sb("iot", [P, P])
        rev8 = sb("rev8", [P, E])
        tokid = sb("tokid", [P, NT])
        work0 = sb("work0", [P, NP2 * PAD])
        vbdT = work0[:].rearrange("p (q c) -> p q c", q=NP2)
        w_ = lambda q: work0[:, NSTR * D * q:NSTR * D * (q + 1)].rearrange("p (s d) -> p s d", s=NSTR)
        g0 = w_(0)
        hT = w_(1).rearrange("p s (k q) -> p s k q", k=DK)
        h0 = w_(2)
        y0 = w_(3)
        vT = sb("vT", [P, DK, E])
        v0 = sb("v0", [E, D])
        phase.close()
        phase = ExitStack()
        qc = sb("qc", [DQ, 2, P])
        rot = sb("rot", [P, 4, 4, P])
        pc = sb("pc", [P, 2, HC, LK])
        pcT = sb("pcT", [P, 2, NJ, P])
        pmax = sb("pmax", [P, 2, HC])
        psm = sb("psm", [P, 2, HC])
        wg = sb("wg", [P, DK, E])
        be = sb("be", [E, D])
        lt = sb("lt", [P, 2, E])
        lmax = sb("lmax", [P, 2, E])
        lidx = sb("lidx", [P, 2, E], mybir.dt.uint32)
        lidf = sb("lidf", [P, 2, TOP])
        gt = sb("gt", [P, 2, TOP])
        gd = sb("gd", [P, 2, 2])
        goh = sb("goh", [P, 2, TOP, E])
        gates = sb("gates", [P, 2, E])
        gatesT = sb("gatesT", [E, 2, P])
        acc = sb("acc", [P, 2, 2, D])
        y = sb("y", [P, 2, D])
        iot8 = sb("iot8", [P, E])
        phase.close()
        we = w0[:].rearrange("p e l k d -> p (e l k d)")[:, 0:DK * E * D].rearrange("p (k n) -> p k n", k=DK)

        S_ = lambda c: ps[:, 2 * c:2 * c + 2, 0:4 * LK].rearrange("p a (h k) -> p a h k", h=4)
        PTA = ps[:, 4, 0:3 * P].rearrange("p (j q) -> p j q", j=3)
        PTB = ps[:, 5, 0:2 * P].rearrange("p (j q) -> p j q", j=2)
        XT = ps[:, 6, 0:D].rearrange("p (k q) -> p k q", k=DK)
        QT = ps[:, 6, D:2 * D].rearrange("p (c q) -> p c q", c=2)
        O_ = ps[:, 7, 0:2 * HC * VW1].rearrange("p (c h v) -> p c h v", c=2, h=HC)
        OT = ps[:, 7, 0:2 * P].rearrange("p (c q) -> p c q", c=2)
        OUT = ps[:, 7, D:2 * D]

        x_in = [sem(f"x_in{g}") for g in range(2)]
        k_in = sem("k_in")
        v_in = sem("v_in")
        q_in = sem("q_in")
        g_in = sem("g_in")
        c_in = sem("c_in")
        w0_in = sem("w0_in")
        const_set = sem("const_set")
        sA = {n: sem("a_" + n) for n in (
            "stats aggr rstd kv_ps kv_sb kbd_ready vbd_ready ctxT_ps ctxT_sb rep_ready "
            "xn_ready xT_ps xT_sb q_ps q_ready s_ps max_done sub_done exp_done pta_ps ptb_ps pta_ev ptb_ev "
            "o_ps rsum_done on_ready oT_ps oT_sb out_ps x1_ready aggr2 stats2 xo_ready x1_kept stats_kept").split()}

        sB = {n: sem("b_" + n) for n in (
            "const rstd xn_ready xT_ps xT_sb lg_ps lg_sb chain gexp pT_ps ind_ps ind_sb rank_ps payload rowhot rowhot_used "
            "tok_ready route_ready tp_ps tp_sb l_ps l_sb y_ready v_ps vT_sb v_tp v_sb o_ps x2_ready stats aggr").split()}
        stored = [sem(f"b_stored{u}") for u in range(2)]
        gathered = [sem(f"b_gathered{s}") for s in range(NSTR)]

        sC = {n: sem("c_" + n) for n in (
            "mask set kvc_ps kvc_sb kn_ps kn_sb v_ps v_sb a_ps a_sb kr_ps kr_sb kr_mul vw_ps vw_sb zero work_free "
            "aggr rstd xn_ready xT_ps xT_sb qc_ps qc_sb rope_ps rot_ready s_ps mask_done max_done sub_done exp_done sum_done rsum_done norm_done "
            "pta_ps ptb_ps pta_ev ptb_ev out_ps x_ready x_kept stats stats_kept").split()}
        sD = {n: sem("d_" + n) for n in (
            "w_in aggr rstd xn_ready xT_ps xT_sb lg_ps chain diff exp gates gT_ps gT_sb be_ps e_ps accA accB y_ready").split()}
        written = [sem(f"d_written{u}") for u in range(2)]
        c_w = sem("c_w")

        block = st.enter_context(nc.Block())

        def wait(eng, s, n):
            if not isinstance(n, int) or n > 0:
                eng.wait_ge(s, n)

        def tile_at(i, s):
            return s % 2, i + s // 2

        def pipeline(eng, body):
            body(-1, 1)
            body(0, 0)
            body(0, 1)
            with eng.Fori(1, TPB - 1) as i:
                body(i, 0)
                body(i, 1)
            body(TPB - 1, 0)
            body(TPB - 1, 1)
            body(TPB, 0)

        def live(i, s):
            return not isinstance(i, int) or 0 <= 2 * i + s < NT

        @block.sync
        def _(sp):
            sp.dma_start(ctx[:], io["ctx_1024"].rearrange("b k d -> k b d")).then_inc(c_in, 16)
            sp.dma_start(ident[:], io["c_ident"]).then_inc(c_in, 16)
            sp.dma_start(wk[:], io["L0_xattn_Wk"].rearrange("(k p) n -> p k n", p=P)).then_inc(k_in, 16)
            sp.dma_start(bk[:], io["L0_xattn_bk"]).then_inc(k_in, 16)
            sp.dma_start(kmask[:], io["c_kmask"]).then_inc(k_in, 16)
            sp.dma_start(wv[:], io["L0_xattn_Wv"].rearrange("(k p) n -> p k n", p=P)).then_inc(v_in, 16)
            sp.dma_start(bv[:], io["L0_xattn_bv"].partition_broadcast(P)).then_inc(v_in, 16)
            sp.dma_start(vmask[:], io["c_vmask"]).then_inc(v_in, 16)
            sp.dma_start(wq[:], io["L0_xattn_Wq"].rearrange("(k p) n -> p k n", p=P)).then_inc(q_in, 16)
            sp.dma_start(bq[:], io["L0_xattn_bq"]).then_inc(q_in, 16)
            sp.dma_start(wo[:], io["L0_xattn_Wo"].rearrange("(k p) n -> p k n", p=P)).then_inc(q_in, 16)
            sp.dma_start(bo[:], io["L0_xattn_bo"].partition_broadcast(P)).then_inc(q_in, 16)
            sp.dma_start(gw[:], io["L0_ffn_gate_w"].rearrange("(k p) e -> p k e", p=P)).then_inc(g_in, 16)
            sp.dma_start(gb[:], io["L0_ffn_gate_b"]).then_inc(g_in, 16)
            for l, n in enumerate(("L0_ffn_w1", "L0_ffn_w2", "L0_ffn_w3")):
                for k in range(DK):
                    sp.dma_start(w0[:, :, l, k, :], io[n][:, P * k:P * k + P, :].rearrange("e p o -> p e o")).then_inc(w0_in, 16)
            for dst, n in ((wkup, "L1_xattn_w_k_up"), (wvup, "L1_xattn_w_v_up"), (wqupT, "L1_xattn_w_q_up"), (trig[:], "c_trig"),
                           (seg_i[:], "itok_BxS_0_511"), (krt, "c_ktrig"), (iok[:], "c_iok")):
                sp.dma_start(dst, io[n]).then_inc(c_w, 16)
            sp.dma_start(wout, io["L1_xattn_w_out"].rearrange("(q p) n -> p q n", p=P)).then_inc(c_w, 16)
            sp.dma_start(wkvc, io["L1_xattn_w_kv_comp"].rearrange("(k p) n -> p k n", p=P)).then_inc(c_w, 16)
            sp.dma_start(wqd[:], io["L1_xattn_w_q_down"].rearrange("(k p) n -> p k n", p=P)).then_inc(c_w, 16)
            half = RD // 2
            wqr = io["L1_xattn_w_q_rope"].rearrange("c (h r) -> c h r", h=H)
            for dst, src in ((wr2[:, :, 0:RD], wqr), (wr2[:, :, RD:RD + half], wqr[:, :, half:RD]), (wr2[:, :, RD + half:], wqr[:, :, 0:half])):
                sp.dma_start(dst, src).then_inc(c_w, 16)
            for a in range(2):
                sp.dma_start(wkr[:, 0, RD * a:RD * a + RD], io["L1_xattn_w_k_rope"]).then_inc(c_w, 16)
                sp.dma_start(wkr[:, 1, RD * a:RD * a + half], io["L1_xattn_w_k_rope"][:, half:RD]).then_inc(c_w, 16)
                sp.dma_start(wkr[:, 1, RD * a + half:RD * a + RD], io["L1_xattn_w_k_rope"][:, 0:half]).then_inc(c_w, 16)
            sp.wait_ge(sA["x1_ready"], NT)
            for dst, n in ((tri, "c_tri"), (ones, "c_ones"), (iot, "c_iota"), (rev8, "c_rev8"), (tri8, "c_tri8"), (tokid, "c_tokid")):
                sp.dma_start(dst[:], io[n]).then_inc(sB["const"], 16)
            for n in range(NT):
                b, j = tile_at(0, n)
                sp.wait_ge(sB["xn_ready"], n + 1)
                sp.dma_start(io["xn_dram"][P * (TPB * b + j):P * (TPB * b + j + 1), :], xn[:, b, :]).then_inc(stored[b], 16)
            sp.wait_ge(sC["vw_ps"], 2 * NJ)
            sp.wait_ge(sC["kr_mul"], 3)
            for l, n in enumerate(("L0_ffn_b1", "L0_ffn_b2", "L0_ffn_b3")):
                sp.dma_start(b0[:, :, l, :], io[n].partition_broadcast(P)).then_inc(w0_in, 16)
            sp.wait_ge(sB["l_sb"], NL * NCH)
            for k in range(DK):
                sp.dma_start(we[:, k, :].rearrange("p (e d) -> p e d", e=E), io["L1_ffn_We"][:, P * k:P * k + P, :].rearrange("e p d -> p e d")).then_inc(sD["w_in"], 16)
            sp.wait_ge(sB["x2_ready"], NT // 2)
            sp.dma_start(wg[:], io["L1_ffn_Wg"].rearrange("(k p) e -> p k e", p=P)).then_inc(sD["w_in"], 16)
            sp.dma_start(be[:], io["L1_ffn_be"]).then_inc(sD["w_in"], 16)
            sp.dma_start(iot8[:], io["c_iota"][:, 0:E]).then_inc(sD["w_in"], 16)
            for n in range(NT):
                b, j = tile_at(0, n)
                sp.wait_ge(sD["y_ready"], n + 1)
                sp.dma_start(io["out"][b, P * j:P * j + P, :], y[:, b, :]).then_inc(written[b], 16)
            for b in range(B):
                sp.wait_ge(written[b], 16 * TPB)
        @block.gpsimd
        def _(pool):
            nc.gpsimd.memset(epsv[:], 1e-5).then_inc(const_set, 1)
            nc.gpsimd.memset(power[:], -0.5).then_inc(const_set, 1)
            pool.wait_ge(const_set, 2)
            pool.wait_ge(sA["aggr"], NT)
            nc.gpsimd.tensor_tensor(rstd[:], mv[:, :, :, 1], epsv[:], ALU.add).then_inc(sA["rstd"], 1)
            pool.wait_ge(sA["rstd"], 1)
            nc.gpsimd.tensor_tensor(rstd[:], rstd[:], power[:], ALU.pow).then_inc(sA["rstd"], 1)
            pool.wait_ge(q_in, 64)

            def body(i, u):
                if live(i, u):
                    b, j = tile_at(i, u)
                    jj = bass.ds(j, 1)
                    wait(pool, sA["xn_ready"], 2 * i + u + 1)
                    nc.gpsimd.tensor_tensor(x[:, b, jj, :].squeeze(1), x[:, b, jj, :].squeeze(1), bo[:], ALU.add).then_inc(sA["xo_ready"], 1)

            pipeline(pool, body)

            pool.wait_ge(sA["stats_kept"], NT)
            nc.gpsimd.memset(work0[:], 0.0).then_inc(sC["zero"], 1)
            pool.wait_ge(sA["aggr2"], NT)
            nc.gpsimd.tensor_tensor(rstd[:], mv[:, :, :, 1], epsv[:], ALU.add).then_inc(sB["rstd"], 1)
            pool.wait_ge(sB["rstd"], 1)
            nc.gpsimd.tensor_tensor(rstd[:], rstd[:], power[:], ALU.pow).then_inc(sB["rstd"], 1)
            pool.wait_ge(sC["kr_sb"], 1)
            for v in range(2):
                last = nc.gpsimd.tensor_tensor(kruv[:, v], kruv[:, v], bcast(krt[:, v], 1, B), ALU.mult)
                last.then_inc(sC["kr_mul"], 1)
            pool.wait_ge(sC["kr_mul"], 2)
            nc.gpsimd.tensor_tensor(kr2[:], kruv[:, 0], kruv[:, 1], ALU.add).then_inc(sC["kr_mul"], 1)
            for u in range(2):
                pool.wait_ge(stored[u], 16 * TPB)
            pool.wait_ge(sB["tok_ready"], 1)
            pool.wait_ge(sC["vw_ps"], 2 * NJ)
            for c in range(NCH):
                it, s = c // NSTR, c % NSTR
                if it:
                    pool.wait_ge(sB["tp_ps"], NL * NSTR * (it - 1) + s + 1)
                pool.indirect_dma_start(out=g0[:, s, :], out_offset=None, in_=io["xn_dram"],
                                        in_offset=bass.IndirectOffsetOnAxis(ap=tok_i[:, c:c + 1], axis=0)).then_inc(gathered[s], 16)
            def rstd_of(done, s):
                pool.wait_ge(done, NT)
                nc.gpsimd.tensor_tensor(rstd[:], mv[:, :, :, 1], epsv[:], ALU.add).then_inc(s, 1)
                pool.wait_ge(s, 1)
                nc.gpsimd.tensor_tensor(rstd[:], rstd[:], power[:], ALU.pow).then_inc(s, 1)

            pool.wait_ge(sB["aggr"], NT // 2)
            nc.gpsimd.tensor_tensor(rstd[:], mv[:, :, :, 1], epsv[:], ALU.add).then_inc(sC["rstd"], 1)
            pool.wait_ge(sC["rstd"], 1)
            nc.gpsimd.tensor_tensor(rstd[:], rstd[:], power[:], ALU.pow).then_inc(sC["rstd"], 1)

            def body(i, u):
                n = 2 * i + u

                def norm(m, c):
                    wait(pool, sC["rsum_done"], 2 * m + c + 1)
                    nc.gpsimd.tensor_tensor(pc[:, c], pc[:, c], bcast(psm[:, c], 2, LK), ALU.mult).then_inc(sC["norm_done"], 1)

                def sub(m, c):
                    wait(pool, sC["max_done"], 2 * m + c + 1)
                    nc.gpsimd.tensor_tensor(pc[:, c], pc[:, c], bcast(pmax[:, c], 2, LK), ALU.subtract).then_inc(sC["sub_done"], 1)

                if live(i, u):
                    norm(n, 1)
                if live(i, u + 1):
                    sub(n + 1, 0)
                    norm(n + 1, 0)
                    sub(n + 1, 1)

            pipeline(pool, body)
            rstd_of(sD["aggr"], sD["rstd"])

        @block.scalar
        def _(act):
            for g in range(2):
                for b in range(B):
                    act.dma_start(x[:, b, 4 * g:4 * g + 4, :], io["x"][b, 512 * g:512 * g + 512, :].rearrange("(j p) d -> p j d", p=P)).then_inc(x_in[g], 16)
            act.wait_ge(q_in, 64)

            def body(i, u):
                n = 2 * i + u
                if live(i, u + 1):
                    wait(act, sA["xT_ps"], n + 2)
                    wait(act, sA["q_ps"], n)
                    nc.scalar.activation(xnT[:, 1 - u], XT, ACT.Copy).then_inc(sA["xT_sb"], 1)

                def weights(c):
                    wait(act, sA["pta_ps"], 2 * n + c + 1)
                    wait(act, sA["o_ps"], n)
                    nc.scalar.activation(prT[:, c, 0:3, :], PTA, ACT.Copy).then_inc(sA["pta_ev"], 1)
                    wait(act, sA["ptb_ps"], 2 * n + c + 1)
                    nc.scalar.activation(prT[:, c, 3, :], PTB[:, 0], ACT.Copy)
                    nc.scalar.activation(prT[0:rows(4), c, 4, :], PTB[0:rows(4), 1], ACT.Copy).then_inc(sA["ptb_ev"], 1)

                if live(i, u):
                    weights(0)
                if live(i, u - 1):
                    wait(act, sA["oT_ps"], n)
                    wait(act, sA["out_ps"], n - 1)
                    nc.scalar.activation(oT[:], OT, ACT.Copy).then_inc(sA["oT_sb"], 1)
                if live(i, u + 1):
                    wait(act, sA["q_ps"], n + 2)
                    wait(act, sA["s_ps"], 2 * n)
                    for c in range(2):
                        last = nc.scalar.activation(qT[:, 1 - u, c, :], QT[:, c], ACT.Identity, bias=bq[:, c:c + 1])
                    last.then_inc(sA["q_ready"], 1)
                if live(i, u):
                    weights(1)
                if live(i, u + 1):
                    for c in range(2):
                        wait(act, sA["sub_done"], 2 * n + 3 + c)
                        nc.scalar.activation(pr[:, c], pr[:, c], ACT.Exp).then_inc(sA["exp_done"], 1)

            pipeline(act, body)

            def body(i):
                for u in range(2):
                    n = 2 * i + u
                    act.wait_ge(sB["xT_ps"], n + 1)
                    wait(act, sB["lg_ps"], n - 1)
                    nc.scalar.activation(xnT[:, u], ps[:, u, 0:D].rearrange("p (k q) -> p k q", k=DK), ACT.Copy).then_inc(sB["xT_sb"], 1)

            body(0)
            with act.Fori(1, TPB) as i:
                body(i)
            act.wait_ge(sB["chain"], 1)
            for b in range(B):
                nc.scalar.activation(lg[:, b], lg[:, b], ACT.Exp, bias=gmax[:, b:b + 1], accum_out=gsum[:, b:b + 1]).then_inc(sB["gexp"], 1)
            def copies(ps_sem, k, dst, src, sb_sem, scale=1.0):
                act.wait_ge(ps_sem, k)
                nc.scalar.activation(dst, src, ACT.Copy, scale=scale).then_inc(sb_sem, 1)

            copies(sC["kvc_ps"], 1, kvcT, ps[0:DC, 7, 0:B * LK], sC["kvc_sb"])
            for g, (q0, nq) in enumerate(((0, 3), (3, 3), (6, 2))):
                copies(sC["kn_ps"], g + 1, knT[:, q0:q0 + nq].rearrange("p q b k -> p (q b k)"), ps[:, g, 0:nq * B * LK], sC["kn_sb"])
            copies(sC["kr_ps"], 1, kruv.rearrange("p v b k -> p (v b k)"), ps[:, 3, 0:2 * B * LK], sC["kr_sb"], scale=SCALE)
            for g in range(6):
                q0, a = 3 * (g // 2), g % 2
                nh = min(3, NP2 - q0)
                copies(sC["a_ps"], g + 1, anope[:].rearrange("p b (q a) k -> p a q b k", a=2)[:, a, q0:q0 + nh],
                       ps[0:DQ, g % 2, 0:nh * B * LK].rearrange("p (h b k) -> p h b k", h=nh, b=B), sC["a_sb"], scale=SCALE)
            act.wait_ge(sC["zero"], 1)
            for b in range(B):
                if b:
                    act.wait_ge(sC["vw_ps"], NJ)
                act.wait_ge(sC["v_ps"], 3)
                for q in range(NP2):
                    for a in range(2):
                        r = slice(RD * a, RD * a + RD)
                        last = nc.scalar.activation(vbdT[r, q, P + LK * a:P + LK * a + LK], ps[r, 2 + q // 3, (q % 3) * B * LK + b * LK:(q % 3) * B * LK + (b + 1) * LK], ACT.Copy)
                last.then_inc(sC["v_sb"], 1)
                for m in range(NJ):
                    act.wait_ge(sC["vw_ps"], NJ * b + m + 1)
                    for a in range(2):
                        c, j = (2 * m + a) // NJ, (2 * m + a) % NJ
                        last = nc.scalar.activation(vw[0:rows(j), b, c, j, :], ps[0:rows(j), 5 + m % 2, D * a:D * a + D], ACT.Copy)
                    last.then_inc(sC["vw_sb"], 1)
            act.wait_ge(sB["ind_ps"], 1)
            for g in range(4):
                last = nc.scalar.activation(indT[:, 4 * g:4 * g + 4, :], ps[0:E, g, :].rearrange("e (t q) -> e t q", q=P), ACT.Copy)
            last.then_inc(sB["ind_sb"], 1)

            def chunks(it):
                for l in range(NL):
                    for s in range(NSTR):
                        act.wait_ge(sB["tp_ps"], NL * NSTR * it + NSTR * l + s + 1)
                        nc.scalar.activation(hT[:, s], ps[:, s, 0:D].rearrange("p (k q) -> p k q", k=DK),
                                             ACT.Relu if l else ACT.Copy).then_inc(sB["tp_sb"], 1)
                for s in range(NSTR):
                    act.wait_ge(sB["l_sb"], NL * NSTR * it + NSTR * (NL - 1) + s + 1)
                    wait(act, sB["v_ps"], NSTR * (it - 1) + s + 1)
                    nc.scalar.activation(y0[:, s], h0[:, s], ACT.Relu).then_inc(sB["y_ready"], 1)

            chunks(0)
            with act.Fori(1, NIT) as it:
                chunks(it)
            act.wait_ge(sB["v_tp"], 1)
            nc.scalar.activation(v0[:], ps[0:E, 5, 0:D], ACT.Copy).then_inc(sB["v_sb"], 1)

            def evac_xT(i, s):
                m = 2 * i + s
                wait(act, sC["xT_ps"], m + 1)
                nc.scalar.activation(xnT[:, s % 2], ps[:, 6, 0:D].rearrange("p (k q) -> p k q", k=DK), ACT.Copy).then_inc(sC["xT_sb"], 1)

            def evac_qc(i, s):
                m = 2 * i + s
                wait(act, sC["qc_ps"], m + 1)
                wait(act, sC["s_ps"], 2 * m - 2)
                nc.scalar.activation(qc[:, s % 2, :], ps[0:DQ, 6, D:D + P], ACT.Copy).then_inc(sC["qc_sb"], 1)

            evac_xT(0, 0)
            evac_qc(0, 0)

            def body(i, u):
                n = 2 * i + u

                def weights(c):
                    wait(act, sC["pta_ps"], 2 * n + c + 1)
                    wait(act, sC["out_ps"], n)
                    nc.scalar.activation(pcT[:, c, 0:3, :], PTA, ACT.Copy).then_inc(sC["pta_ev"], 1)
                    wait(act, sC["ptb_ps"], 2 * n + c + 1)
                    nc.scalar.activation(pcT[:, c, 3, :], PTB[:, 0], ACT.Copy)
                    nc.scalar.activation(pcT[0:rows(4), c, 4, :], PTB[0:rows(4), 1], ACT.Copy).then_inc(sC["ptb_ev"], 1)

                def exponentials(c):
                    wait(act, sC["sub_done"], 2 * n + 3 + c)
                    nc.scalar.activation(pc[:, c], pc[:, c], ACT.Exp).then_inc(sC["exp_done"], 1)

                if live(i, u):
                    weights(0)
                    weights(1)
                if live(i, u + 1):
                    exponentials(0)
                if live(i, u + 2):
                    evac_xT(i, u + 2)
                    evac_qc(i, u + 2)
                if live(i, u + 1):
                    exponentials(1)

            pipeline(act, body)

            def body(i, u):
                n = 2 * i + u
                if live(i, u + 1):
                    wait(act, sD["xT_ps"], n + 2)
                    wait(act, sD["e_ps"], 4 * n)
                    nc.scalar.activation(xnT[:, 1 - u], ps[:, 4, 0:D].rearrange("p (k q) -> p k q", k=DK), ACT.Copy).then_inc(sD["xT_sb"], 1)
                    wait(act, sD["diff"], n + 2)
                    nc.scalar.activation(gd[:, 1 - u, 1:2], gd[:, 1 - u, 0:1], ACT.Exp).then_inc(sD["exp"], 1)
                    wait(act, sD["gT_ps"], n + 2)
                    wait(act, sD["be_ps"], n)
                    nc.scalar.activation(gatesT[:, 1 - u, :], ps[0:E, 6, 0:P], ACT.Copy).then_inc(sD["gT_sb"], 1)

            pipeline(act, body)

        @block.vector
        def _(dve):
            dve.wait_ge(sA["ctxT_ps"], 1)
            nc.vector.tensor_copy(ctxT[:], ps[:, 6, 0:DK * B * LK].rearrange("p (k b q) -> p k b q", k=DK, b=B)).then_inc(sA["ctxT_sb"], 1)
            dve.wait_ge(sA["ctxT_sb"], 1)
            for k in range(DK):
                last = nc.vector.tensor_copy(ctx_rep[:, k], bcast(ctxT[:, k], 2, HC))
            last.then_inc(sA["rep_ready"], 1)
            dve.wait_ge(k_in, 48)
            dve.wait_ge(sA["kv_ps"], 1)
            for c in range(2):
                last = nc.vector.tensor_scalar(kT[:, c], ps[:, 7, 2 * LK * c:2 * LK * (c + 1)].rearrange("p (b k) -> p b k", b=B),
                                               bk[:, c:c + 1], HD ** -0.5, ALU.add, ALU.mult)
            last.then_inc(sA["kv_sb"], 1)
            dve.wait_ge(sA["kv_sb"], 1)
            for c in range(2):
                for b in range(B):
                    last = nc.vector.tensor_tensor(kbd[:, b, c], bcast(kT[:, c, b], 1, HC), bcast(kmask[:], 2, LK), ALU.mult)
            last.then_inc(sA["kbd_ready"], 1)
            for j in range(TPB):
                for b in range(B):
                    t = B * j + b
                    dve.wait_ge(x_in[j // 4], 32)
                    nc.vector.bn_stats(stats[:, t % 2], x[:, b, j, :]).then_inc(sA["stats"], 1)
                    dve.wait_ge(sA["stats"], t + 1)
                    nc.vector.bn_aggr(mv[:, b, j], stats[:, t % 2]).then_inc(sA["aggr"], 1)
            dve.wait_ge(v_in, 48)
            for g in range(5):
                dve.wait_ge(sA["kv_ps"], g + 2)
                if g >= 2:
                    dve.wait_ge(sA["vbd_ready"], g - 1)
                dve_src = ps[:, g % 4, :].rearrange("p (n d) -> p n d", n=4)
                for q in range(4):
                    b, c, j = v_unit(4 * g + q)
                    last = nc.vector.tensor_tensor(vtmp[0:rows(j), g % 2, q], dve_src[0:rows(j), q], bv[0:rows(j), P * c:P * c + P], ALU.add)
                last.then_inc(sA["kv_sb"], 1)
                dve.wait_ge(sA["kv_sb"], g + 2)
                for q in range(4):
                    b, c, j = v_unit(4 * g + q)
                    r = rows(j)
                    nc.vector.tensor_tensor(vbd[0:r, b, c, j, :, 0:HD], vtmp[0:r, g % 2, q].rearrange("p (h d) -> p h d", h=HC),
                                            bcast(vmask[0:r, j], 2, HD), ALU.mult)
                    last = nc.vector.tensor_copy(vbd[0:r, b, c, j, :, HD:VW1], vmask[0:r, j].unsqueeze(2))
                last.then_inc(sA["vbd_ready"], 1)

            def normalise(i, s):
                b, j = tile_at(i, s)
                n = 2 * i + s
                wait(dve, sA["xT_ps"], n - 1)
                jj = bass.ds(j, 1)
                nc.vector.tensor_scalar(xn[:, b], x[:, b, jj, :], mv[:, b, jj, 0:1], rstd[:, b, jj],
                                        ALU.subtract, ALU.mult).then_inc(sA["xn_ready"], 1)

            dve.wait_ge(sA["rstd"], 2)
            normalise(0, 0)

            def body(i, u):
                n = 2 * i + u
                if live(i, u - 1):
                    wait(dve, sA["o_ps"], n)
                    nc.vector.reciprocal(rsum[:], O_[:, :, :, HD]).then_inc(sA["rsum_done"], 1)
                    wait(dve, sA["rsum_done"], n)
                    wait(dve, sA["oT_ps"], n - 1)
                    nc.vector.tensor_tensor(on[:], O_[:, :, :, 0:HD], bcast(rsum[:], 3, HD), ALU.mult).then_inc(sA["on_ready"], 1)
                if live(i, u + 2):
                    normalise(i, u + 2)
                if live(i, u - 1):
                    b, j = tile_at(i, u - 1)
                    jj = bass.ds(j, 1)
                    wait(dve, sA["out_ps"], n)
                    wait(dve, sA["xo_ready"], n)
                    wait(dve, sA["x1_kept"], n - 1)
                    nc.vector.tensor_tensor(xs[:, b], x[:, b, jj, :].squeeze(1), OUT, ALU.add).then_inc(sA["x1_ready"], 1)
                for c in range(2):
                    if live(i, u + 1):
                        wait(dve, sA["s_ps"], 2 * n + 3 + c)
                        nc.vector.tensor_reduce(nmax[:, c], S_(c), AX.X, ALU.max).then_inc(sA["max_done"], 1)
                        wait(dve, sA["max_done"], 2 * n + 3 + c)
                        wait(dve, sA["ptb_ps"], 2 * n + 1 + c)
                        if c == 1 and live(i, u - 1):
                            wait(dve, sA["stats2"], n)
                        nc.vector.tensor_tensor(pr[:, c].rearrange("p (a h) k -> p a h k", a=2), S_(c),
                                                bcast(nmax[:, c].rearrange("p (a h) -> p a h", a=2), 3, LK),
                                                ALU.subtract).then_inc(sA["sub_done"], 1)
                    if live(i, u - 1):
                        if c == 0:
                            wait(dve, sA["x1_ready"], n)
                            nc.vector.bn_stats(stats[:, b], xs[:, b]).then_inc(sA["stats2"], 1)
                            nc.vector.tensor_copy(x[:, b, jj, :].squeeze(1), xs[:, b]).then_inc(sA["x1_kept"], 1)
                        else:
                            if not live(i, u + 1):
                                wait(dve, sA["stats2"], n)
                            nc.vector.tensor_copy(st_all[:, b, jj, :].squeeze(1), stats[:, b]).then_inc(sA["stats_kept"], 1)

            pipeline(dve, body)

            dve.wait_ge(sA["stats_kept"], NT)
            for b in range(B):
                for j in range(TPB):
                    nc.vector.bn_aggr(mv[:, b, j], st_all[:, b, j]).then_inc(sA["aggr2"], 1)

            def normalise2(i, u):
                n = 2 * i + u
                jj = bass.ds(i, 1)
                wait(dve, sB["xT_ps"], n - 1)
                wait(dve, stored[u], 16 * i)
                nc.vector.tensor_scalar(xn[:, u], x[:, u, jj, :], mv[:, u, jj, 0:1], rstd[:, u, jj],
                                        ALU.subtract, ALU.mult).then_inc(sB["xn_ready"], 1)

            def logits(i, u):
                n = 2 * i + u
                wait(dve, sB["lg_ps"], n + 1)
                nc.vector.tensor_scalar(lg[:, u, bass.ds(P * i, P)], ps[0:E, 2 + u, 0:P], gb[:, 0:1], None, ALU.add).then_inc(sB["lg_sb"], 1)

            dve.wait_ge(g_in, 32)
            dve.wait_ge(sB["rstd"], 2)
            normalise2(0, 0)
            normalise2(0, 1)
            with dve.Fori(1, TPB) as i:
                normalise2(i, 0)
                logits(i - 1, 0)
                normalise2(i, 1)
                logits(i - 1, 1)
            logits(TPB - 1, 0)
            logits(TPB - 1, 1)
            links = [0]

            def then(ins):
                links[0] += 1
                ins.then_inc(sB["chain"], 1)
                dve.wait_ge(sB["chain"], links[0])

            dve.wait_ge(sB["lg_sb"], NT)
            then(nc.vector.tensor_reduce(gmax[:], lg[:], AX.X, ALU.max, negate=True))
            dve.wait_ge(sB["gexp"], 2)
            then(nc.vector.reciprocal(gsum[:], gsum[:]))
            for b in range(B):
                last = nc.vector.tensor_scalar(lg[:, b], lg[:, b], gsum[:, b:b + 1], None, ALU.mult)
            then(last)
            dve.wait_ge(sB["const"], 96)
            dve.wait_ge(sB["pT_ps"], 1)
            then(nc.vector.tensor_copy(prob[:], ps[:, 4, 0:NT * E].rearrange("p (t e) -> p t e", e=E)))
            src = prob
            for k in range(TOP):
                then(nc.vector.tensor_reduce(top[:, k], src[:], AX.X, ALU.max))
                then(nc.vector.tensor_tensor(key[:], src[:], bcast(top[:, k], 2, E), ALU.is_equal))
                then(nc.vector.tensor_tensor(key[:], key[:], bcast(rev8[:], 1, NT), ALU.mult))
                then(nc.vector.tensor_reduce(kmax[:], key[:], AX.X, ALU.max))
                then(nc.vector.tensor_tensor(oneh[:, k], bcast(rev8[:], 1, NT), bcast(kmax[:], 2, E), ALU.is_equal))
                if k == 0:
                    then(nc.vector.scalar_tensor_tensor(prob2[:], oneh[:, 0], -2.0, prob[:], ALU.mult, ALU.add))
                    src = prob2
            nc.vector.tensor_tensor(sel[:], oneh[:, 0], oneh[:, 1], ALU.add).then_inc(sB["route_ready"], 1)
            dve.wait_ge(sB["rank_ps"], 1)
            rank = ps[:, 5, 0:(NT + 1) * E].rearrange("p (t e) -> p t e", e=E)
            then(nc.vector.tensor_copy(base[:], rank[:, NT, :]))
            then(nc.vector.tensor_scalar(cmp16[:, 0], iot[:, 0:NT], float(P), None, ALU.mult))
            then(nc.vector.tensor_copy(kmax[:], cmp16[:, 0]))
            then(nc.vector.tensor_tensor(cmp16[:], bcast(base[:], 2, NT), bcast(kmax[:], 1, E), ALU.is_gt))
            then(nc.vector.tensor_reduce(nch[:], cmp16[:], AX.X, ALU.add))
            then(nc.vector.tensor_tensor(tri8[:], tri8[:], bcast(nch[:], 1, E), ALU.mult))
            then(nc.vector.tensor_reduce(cend[:], tri8[:], AX.X, ALU.add))
            then(nc.vector.tensor_tensor(base[:], cend[:], nch[:], ALU.subtract))
            then(nc.vector.tensor_scalar(base[:], base[:], float(P), None, ALU.mult))
            then(nc.vector.tensor_tensor(pos[:], rank[:, 0:NT, :], bcast(base[:], 1, NT), ALU.add))
            for k in range(TOP):
                then(nc.vector.tensor_tensor(key[:], oneh[:, k], pos[:], ALU.mult))
                then(nc.vector.tensor_reduce(slot[:, NT * k:NT * k + NT], key[:], AX.X, ALU.add))
            then(nc.vector.tensor_copy(slot_i[:, 0], slot[:]))
            nc.vector.tensor_scalar(slot_i[:, 1], slot_i[:, 0], P - 1, None, ALU.bitwise_and)
            then(nc.vector.tensor_scalar(slot_i[:, 2], slot_i[:, 0], P.bit_length() - 1, None, ALU.logical_shift_right))
            then(nc.vector.tensor_copy(rc[:], slot_i[:, 1:3]))
            then(nc.vector.tensor_tensor(chhot[:], bcast(rc[:, 1], 2, NCH), bcast(iot[:, 0:NCH], 1, TOP * NT), ALU.is_equal))
            hot = chhot[:].rearrange("p (k t) c -> p k t c", k=TOP)
            pay = payload[:].rearrange("p (k t) v c -> p k t v c", k=TOP)
            for k in range(TOP):
                nc.vector.tensor_tensor(pay[:, k, :, 0, :], hot[:, k], bcast(tokid[:], 2, NCH), ALU.mult)
                nc.vector.tensor_tensor(pay[:, k, :, 1, :], hot[:, k], bcast(top[:, k], 2, NCH), ALU.mult).then_inc(sB["payload"], 1)
            for g in range(4):
                a = slice(8 * g, 8 * g + 8)
                if g >= 2:
                    dve.wait_ge(sB["rowhot_used"], g - 1)
                nc.vector.tensor_tensor(rowhot[:, g % 2], bcast(rc[:, 0, a], 2, P), bcast(iot[:], 1, 8), ALU.is_equal).then_inc(sB["rowhot"], 1)
            then(nc.vector.tensor_tensor(cmp8[:], bcast(iot[:, 0:NCH], 2, E), bcast(cend[:], 1, NCH), ALU.is_ge))
            then(nc.vector.tensor_reduce(ce[:], cmp8[:], AX.X, ALU.add))
            then(nc.vector.tensor_scalar(ce[:], ce[:], float(E - 1), None, ALU.min))
            then(nc.vector.tensor_copy(ce_i[:], ce[:]))
            then(nc.vector.tensor_tensor(cmp8[:], bcast(ce[:], 2, E), bcast(iot[:, 0:E], 1, NCH), ALU.is_equal))
            dve.wait_ge(sB["rowhot_used"], 4)
            nc.vector.tensor_copy(tok_i[:], ps[:, 6, 0:NCH]).then_inc(sB["tok_ready"], 1)
            then(nc.vector.tensor_copy(wslot[:], ps[:, 6, NCH:2 * NCH]))
            nc.vector.tensor_tensor(wexp[:], cmp8[:], bcast(wslot[:], 2, E), ALU.mult).then_inc(sB["route_ready"], 1)
            dve.wait_ge(w0_in, 144)

            dve.wait_ge(c_w, 19 * 16)
            tmp = payload[:].rearrange("p t v c -> p (t v c)")[:, 0:NT * LK].rearrange("p (t k) -> p t k", t=NT)
            then(nc.vector.tensor_copy(seg[:, 0], seg_i[:]))
            then(nc.vector.tensor_scalar(seg[:, 1], seg[:, 0], 2.0, None, ALU.subtract))
            nc.vector.tensor_tensor(negm[:], bcast(iok[:], 1, NT), bcast(seg[:, 0], 2, LK), ALU.is_gt)
            then(nc.vector.tensor_tensor(tmp, bcast(iok[:], 1, NT), bcast(seg[:, 1], 2, LK), ALU.is_lt))
            then(nc.vector.tensor_tensor(negm[:], negm[:], tmp, ALU.add))
            then(nc.vector.tensor_scalar(negm[:], negm[:], FMIN, None, ALU.mult))

            def chunks(it):
                e = [nc.vector.value_load(ce_i[0:1, bass.ds(NSTR * it + s, 1)], min_val=0, max_val=E - 1) for s in range(NSTR)]
                for l in range(NL):
                    for s in range(NSTR):
                        dve.wait_ge(sB["l_ps"], NL * NSTR * it + NSTR * l + s + 1)
                        if l == 0:
                            wait(dve, sB["y_ready"], NSTR * (it - 1) + s + 1)
                        nc.vector.tensor_tensor(h0[:, s], ps[:, s, D:2 * D], b0[:, bass.ds(e[s], 1), l, :].squeeze(1), ALU.add).then_inc(sB["l_sb"], 1)

            chunks(0)
            with dve.Fori(1, NIT) as it:
                chunks(it)
            dve.wait_ge(sB["v_ps"], NCH)
            nc.vector.tensor_copy(vT[:], ps[:, 3:5, 0:E]).then_inc(sB["vT_sb"], 1)
            for m in range(NT // 2):
                b, j = 2 * m // TPB, 2 * m % TPB
                dve.wait_ge(sB["o_ps"], m + 1)
                nc.vector.tensor_tensor(x[:, b, j:j + 2, :], x[:, b, j:j + 2, :], ps[:, m % 4, :].rearrange("p (t d) -> p t d", t=2), ALU.add).then_inc(sB["x2_ready"], 1)
                dve.wait_ge(sB["x2_ready"], m + 1)
                for q in range(2):
                    last = nc.vector.bn_stats(stats[:, q], x[:, b, j + q, :])
                last.then_inc(sB["stats"], 1)
                dve.wait_ge(sB["stats"], m + 1)
                for q in range(2):
                    last = nc.vector.bn_aggr(mv[:, b, j + q], stats[:, q])
                last.then_inc(sB["aggr"], 1)

            def normalise3(i, s):
                n = 2 * i + s
                b, j = tile_at(i, s)
                jj = bass.ds(j, 1)
                wait(dve, sC["xT_ps"], n - 1)
                nc.vector.tensor_scalar(xn[:, b], x[:, b, jj, :], mv[:, b, jj, 0:1], rstd[:, b, jj],
                                        ALU.subtract, ALU.mult).then_inc(sC["xn_ready"], 1)

            dve.wait_ge(sC["rstd"], 2)
            normalise3(0, 0)

            def body(i, u):
                n = 2 * i + u

                def rotate(g):
                    b, j = tile_at(i, u + 1)
                    wait(dve, sC["rope_ps"], 4 * (n + 1) + g + 1)
                    wait(dve, sC["s_ps"], 2 * n + 1 + g // 2)
                    nc.vector.tensor_tensor(rot[:, g], ps[:, 6, :].rearrange("p (h q) -> p h q", h=4),
                                            bcast(trig[:, bass.ds(P * j, P)], 1, 4), ALU.mult).then_inc(sC["rot_ready"], 1)

                def mask(c):
                    b, j = tile_at(i, u + 1)
                    m = 2 * (n + 1) + c + 1
                    wait(dve, sC["s_ps"], m)
                    wait(dve, sC["ptb_ps"], m - 2)
                    nc.vector.tensor_tensor(pc[:, c].rearrange("p (a h) k -> p a h k", a=2), S_(c),
                                            negm[:, bass.ds(TPB * b + j, 1), :].unsqueeze(1).broadcast_to([P, 2, 4, LK]),
                                            ALU.add).then_inc(sC["mask_done"], 1)
                    wait(dve, sC["mask_done"], m)
                    nc.vector.tensor_reduce(pmax[:, c], pc[:, c], AX.X, ALU.max).then_inc(sC["max_done"], 1)

                def total(m, c):
                    k = 2 * m + c + 1
                    wait(dve, sC["exp_done"], k)
                    wait(dve, sC["norm_done"], k - 2)
                    nc.vector.tensor_reduce(psm[:, c], pc[:, c], AX.X, ALU.add).then_inc(sC["sum_done"], 1)
                    wait(dve, sC["sum_done"], k)
                    nc.vector.reciprocal(psm[:, c], psm[:, c]).then_inc(sC["rsum_done"], 1)

                if live(i, u + 1):
                    rotate(0)
                if live(i, u + 2):
                    normalise3(i, u + 2)
                if live(i, u + 1):
                    rotate(1)
                    rotate(2)
                    mask(0)
                    rotate(3)
                    total(n + 1, 0)
                    mask(1)
                if live(i, u - 1):
                    bb, j = tile_at(i, u - 1)
                    jb = bass.ds(j, 1)
                    wait(dve, sC["x_ready"], n)
                    wait(dve, sC["stats_kept"], n - 2)
                    nc.vector.bn_stats(stats[:, bb], xs[:, bb]).then_inc(sC["stats"], 1)
                    nc.vector.tensor_copy(x[:, bb, jb, :].squeeze(1), xs[:, bb]).then_inc(sC["x_kept"], 1)
                if live(i, u + 1):
                    total(n + 1, 1)
                if live(i, u):
                    b, j = tile_at(i, u)
                    jj = bass.ds(j, 1)
                    wait(dve, sC["out_ps"], n + 1)
                    wait(dve, sC["x_kept"], n - 1)
                    wait(dve, sC["stats"], n)
                    nc.vector.tensor_tensor(xs[:, b], x[:, b, jj, :].squeeze(1), ps[:, 7, 0:D], ALU.add).then_inc(sC["x_ready"], 1)
                if live(i, u - 1):
                    if not live(i, u):
                        wait(dve, sC["stats"], n)
                    nc.vector.tensor_copy(st_all[:, bb, jb, :].squeeze(1), stats[:, bb]).then_inc(sC["stats_kept"], 1)

            pipeline(dve, body)
            dve.wait_ge(sC["stats_kept"], NT)
            for b in range(B):
                for j in range(TPB):
                    nc.vector.bn_aggr(mv[:, b, j], st_all[:, b, j]).then_inc(sD["aggr"], 1)

            def normalise4(i, s):
                n = 2 * i + s
                b, j = tile_at(i, s)
                jj = bass.ds(j, 1)
                wait(dve, sD["xT_ps"], n - 1)
                nc.vector.tensor_scalar(xn[:, b], x[:, b, jj, :], mv[:, b, jj, 0:1], rstd[:, b, jj],
                                        ALU.subtract, ALU.mult).then_inc(sD["xn_ready"], 1)

            dve.wait_ge(sD["rstd"], 2)
            dve.wait_ge(sD["w_in"], 80)
            normalise4(0, 0)
            LINKS = 10

            def body(i, u):
                n = 2 * i + u
                if live(i, u + 1):
                    v = 1 - u
                    step = [0]

                    def link(ins):
                        step[0] += 1
                        ins.then_inc(sD["chain"], 1)
                        wait(dve, sD["chain"], LINKS * (n + 1) + step[0])

                    wait(dve, sD["lg_ps"], n + 2)
                    link(nc.vector.tensor_copy(lt[:, v], ps[:, 5, 0:E]))
                if live(i, u + 2):
                    normalise4(i, u + 2)
                if live(i, u + 1):
                    link(nc.vector.max(lmax[:, v], lt[:, v]))
                    nc.vector.tensor_tensor(gd[:, v, 0:1], lmax[:, v, 1:2], lmax[:, v, 0:1], ALU.subtract).then_inc(sD["diff"], 1)
                    link(nc.vector.max_index(lidx[:, v], lmax[:, v], lt[:, v]))
                    link(nc.vector.tensor_copy(lidf[:, v], lidx[:, v, 0:TOP]))
                    link(nc.vector.tensor_tensor(goh[:, v], bcast(iot8[:], 1, TOP), bcast(lidf[:, v], 2, E), ALU.is_equal))
                    wait(dve, sD["exp"], n + 2)
                    link(nc.vector.tensor_scalar(gt[:, v, 0:1], gd[:, v, 1:2], 1.0, None, ALU.add))
                    link(nc.vector.reciprocal(gt[:, v, 0:1], gt[:, v, 0:1]))
                    link(nc.vector.tensor_tensor(gt[:, v, 1:2], gt[:, v, 0:1], gd[:, v, 1:2], ALU.mult))
                    link(nc.vector.tensor_tensor(goh[:, v], goh[:, v], bcast(gt[:, v], 2, E), ALU.mult))
                    wait(dve, sD["gT_ps"], n)
                    link(nc.vector.tensor_tensor(gates[:, v], goh[:, v, 0], goh[:, v, 1], ALU.add))
                if live(i, u):
                    b, j = tile_at(i, u)
                    jj = bass.ds(j, 1)
                    wait(dve, sD["be_ps"], n + 1)
                    wait(dve, sD["y_ready"], n - 1)
                    nc.vector.tensor_tensor(acc[:, u, 0], x[:, b, jj, :].squeeze(1), ps[:, 7, 0:D], ALU.add).then_inc(sD["accA"], 1)
                    for e in range(E):
                        wait(dve, sD["e_ps"], 4 * n + e // 2 + 1)
                        src = ps[:, e // 2, D * (e % 2):D * (e % 2) + D]
                        if e == 1:
                            nc.vector.tensor_scalar(acc[:, u, 1], src, gates[:, u, e:e + 1], None, ALU.mult).then_inc(sD["accB"], 1)
                            continue
                        side = sD["accB"] if e % 2 else sD["accA"]
                        wait(dve, side, (4 * n + e // 2) if e % 2 else (5 * n + e // 2 + 1))
                        nc.vector.scalar_tensor_tensor(acc[:, u, e % 2], src, gates[:, u, e:e + 1], acc[:, u, e % 2], ALU.mult, ALU.add).then_inc(side, 1)
                    wait(dve, sD["accA"], 5 * n + 5)
                    wait(dve, sD["accB"], 4 * n + 4)
                    wait(dve, written[u], 16 * i)
                    nc.vector.tensor_tensor(y[:, u], acc[:, u, 0], acc[:, u, 1], ALU.add).then_inc(sD["y_ready"], 1)

            pipeline(dve, body)

        @block.tensor
        def _(pe):
            pe.wait_ge(c_in, 32)
            for k in range(DK):
                for b in range(B):
                    last = nc.tensor.transpose(ps[:, 6, (2 * k + b) * LK:(2 * k + b + 1) * LK], ctx[:, b, P * k:P * k + P], ident[0:LK, 0:LK])
            last.then_inc(sA["ctxT_ps"], 1)
            pe.wait_ge(sA["ctxT_sb"], 1)
            pe.wait_ge(k_in, 48)
            for c in range(2):
                for k in range(DK):
                    last = nc.tensor.matmul(ps[:, 7, 2 * LK * c:2 * LK * (c + 1)], wk[:, k, P * c:P * c + P], ctxT[:, k],
                                            start=k == 0, stop=k == DK - 1)
            last.then_inc(sA["kv_ps"], 1)
            pe.wait_ge(sA["rep_ready"], 1)
            pe.wait_ge(v_in, 48)
            for g in range(5):
                if g >= 4:
                    pe.wait_ge(sA["kv_sb"], g - 2)
                for q in range(4):
                    b, c, j = v_unit(4 * g + q)
                    for k in range(DK):
                        last = nc.tensor.matmul(ps[0:rows(j), g % 4, P * q:P * q + P],
                                                ctx_rep[:, k, b].rearrange("p h k -> p (h k)")[:, P * j:P * j + rows(j)],
                                                wv[:, k, P * c:P * c + P], start=k == 0, stop=k == DK - 1)
                last.then_inc(sA["kv_ps"], 1)
            pe.wait_ge(sA["kbd_ready"], 1)
            pe.wait_ge(sA["vbd_ready"], 5)
            pe.wait_ge(q_in, 64)

            def body(i, u):
                n = 2 * i + u
                if live(i, u + 1):
                    wait(pe, sA["xn_ready"], n + 2)
                    wait(pe, sA["q_ready"], n + 1)
                    for k in range(DK):
                        last = nc.tensor.transpose(XT[:, k], xn[:, 1 - u, P * k:P * k + P], ident[:])
                    last.then_inc(sA["xT_ps"], 1)

                def transpose_weights(c):
                    flat = pr[:, c].rearrange("p h k -> p (h k)")
                    wait(pe, sA["exp_done"], 2 * n + c + 1)
                    wait(pe, sA["pta_ev"], 2 * n + c)
                    for j in range(3):
                        last = nc.tensor.transpose(PTA[:, j], flat[:, P * j:P * j + P], ident[:])
                    last.then_inc(sA["pta_ps"], 1)
                    wait(pe, sA["ptb_ev"], 2 * n + c)
                    nc.tensor.transpose(PTB[:, 0], flat[:, 3 * P:4 * P], ident[:])
                    nc.tensor.transpose(PTB[0:rows(4), 1], flat[:, 4 * P:UK], ident[:]).then_inc(sA["ptb_ps"], 1)

                def apply_weights(c):
                    wait(pe, sA["ptb_ev"], 2 * n + c + 1)
                    for j in range(NJ):
                        h0, nh = heads_of(j)
                        last = nc.tensor.matmul(O_[:, c, h0:h0 + nh, :].rearrange("p h v -> p (h v)"), prT[0:rows(j), c, j, :],
                                                vbd[0:rows(j), u, c, j, h0:h0 + nh, :].rearrange("p h v -> p (h v)"),
                                                start=j == 0 and c == 0, stop=j == NJ - 1, skip_group_check=True)
                    return last

                def scores(c):
                    wait(pe, sA["sub_done"], 2 * n + c + 1)
                    for a in range(2):
                        last = nc.tensor.matmul(ps[:, 2 * c + a, 0:4 * LK], qT[:, 1 - u, c, :],
                                                kbd[:, 1 - u, c, 4 * a:4 * a + 4, :].rearrange("p h k -> p (h k)"), start=True, stop=True)
                    last.then_inc(sA["s_ps"], 1)

                if live(i, u):
                    transpose_weights(0)
                if live(i, u - 1):
                    wait(pe, sA["on_ready"], n)
                    for c in range(2):
                        last = nc.tensor.transpose(OT[:, c], on[:, c].rearrange("p h d -> p (h d)"), ident[:])
                    last.then_inc(sA["oT_ps"], 1)
                if live(i, u + 1):
                    wait(pe, sA["xT_sb"], n + 2)
                    for c in range(2):
                        for k in range(DK):
                            last = nc.tensor.matmul(QT[:, c], wq[:, k, P * c:P * c + P], xnT[:, 1 - u, k, :], start=k == 0, stop=k == DK - 1)
                    last.then_inc(sA["q_ps"], 1)
                if live(i, u - 1):
                    wait(pe, sA["oT_sb"], n)
                    for c in range(2):
                        last = nc.tensor.matmul(OUT, oT[:, c, :], wo[:, c, :], start=c == 0, stop=c == 1)
                    last.then_inc(sA["out_ps"], 1)
                if live(i, u):
                    transpose_weights(1)
                if live(i, u + 1):
                    wait(pe, sA["q_ready"], n + 2)
                    scores(0)
                if live(i, u):
                    wait(pe, sA["x1_ready"], n)
                    apply_weights(0)
                if live(i, u + 1):
                    scores(1)
                if live(i, u):
                    apply_weights(1).then_inc(sA["o_ps"], 1)

            pipeline(pe, body)

            pe.wait_ge(g_in, 32)
            def transpose_tile(i, u):
                n = 2 * i + u
                wait(pe, sB["xn_ready"], n + 1)
                wait(pe, sB["xT_sb"], n - 1)
                for k in range(DK):
                    last = nc.tensor.transpose(ps[:, u, P * k:P * k + P], xn[:, u, P * k:P * k + P], ident[:])
                last.then_inc(sB["xT_ps"], 1)

            def gate(i, u):
                n = 2 * i + u
                wait(pe, sB["xT_sb"], n + 1)
                wait(pe, sB["lg_sb"], n - 1)
                for k in range(DK):
                    last = nc.tensor.matmul(ps[0:E, 2 + u, 0:P], gw[:, k, :], xnT[:, u, k, :], start=k == 0, stop=k == DK - 1)
                last.then_inc(sB["lg_ps"], 1)

            transpose_tile(0, 0)
            transpose_tile(0, 1)
            gate(0, 0)
            with pe.Fori(1, TPB) as i:
                transpose_tile(i, 0)
                gate(i - 1, 1)
                transpose_tile(i, 1)
                gate(i, 0)
            gate(TPB - 1, 1)
            pe.wait_ge(sB["chain"], 3)
            for t in range(NT):
                b, j = t // TPB, t % TPB
                last = nc.tensor.transpose(ps[:, 4, E * t:E * t + E], lg[:, b, P * j:P * j + P], ident[0:E, 0:E])
            last.then_inc(sB["pT_ps"], 1)
            pe.wait_ge(c_w, 19 * 16)
            for k in range(DK):
                last = nc.tensor.matmul(ps[0:DC, 7, 0:B * LK], wkvc[:, k, :], ctxT[:, k], start=k == 0, stop=k == DK - 1)
            last.then_inc(sC["kvc_ps"], 1)
            pe.wait_ge(sC["kvc_sb"], 1)
            for q in range(NP2):
                last = nc.tensor.matmul(ps[:, q // 3, (q % 3) * B * LK:(q % 3 + 1) * B * LK], wkup[:, P * q:P * q + P], kvcT, start=True, stop=True)
                if q % 3 == 2 or q == NP2 - 1:
                    last.then_inc(sC["kn_ps"], 1)
            for v in range(2):
                last = nc.tensor.matmul(ps[:, 3, v * B * LK:(v + 1) * B * LK], wkr[:, v, :], kvcT, start=True, stop=True)
            last.then_inc(sC["kr_ps"], 1)
            for g in range(6):
                pe.wait_ge(sC["kn_sb"], 3)
                if g >= 2:
                    pe.wait_ge(sC["a_sb"], g - 1)
                r = slice(RD * (g % 2), RD * (g % 2) + RD)
                for q in range(3 * (g // 2), min(3 * (g // 2) + 3, NP2)):
                    last = nc.tensor.matmul(ps[0:DQ, g % 2, (q % 3) * B * LK:(q % 3 + 1) * B * LK], wqupT[r, q, :],
                                            knT[r, q].rearrange("p b k -> p (b k)"), start=True, stop=True)
                last.then_inc(sC["a_ps"], 1)
            pe.wait_ge(sB["route_ready"], 1)
            pe.wait_ge(sC["kr_sb"], 1)
            for q in range(NP2):
                last = nc.tensor.matmul(ps[:, 2 + q // 3, (q % 3) * B * LK:(q % 3 + 1) * B * LK], wvup[:, P * q:P * q + P], kvcT, start=True, stop=True)
                if q % 3 == 2 or q == NP2 - 1:
                    last.then_inc(sC["v_ps"], 1)
            for b in range(B):
                pe.wait_ge(sC["v_sb"], b + 1)
                for m in range(NJ):
                    wait(pe, sC["vw_sb"], NJ * b + m - 1)
                    for a in range(2):
                        c, j = (2 * m + a) // NJ, (2 * m + a) % NJ
                        pairs = [q for q in range(4) if -rows(j) < P * j - 2 * LK * q < 2 * LK]
                        for q in pairs:
                            w0_ = P + P * j - 2 * LK * q
                            last = nc.tensor.matmul(ps[0:rows(j), 5 + m % 2, D * a:D * a + D], vbdT[:, 4 * c + q, w0_:w0_ + rows(j)],
                                                    wout[:, 4 * c + q, :], start=q == pairs[0], stop=q == pairs[-1])
                    last.then_inc(sC["vw_ps"], 1)
            pe.wait_ge(sC["vw_sb"], 2 * NJ)
            pe.wait_ge(sB["route_ready"], 1)
            pe.wait_ge(sB["const"], 96)
            flat = sel[:].rearrange("p t e -> p (t e)")
            nc.tensor.matmul(ps[:, 5, 0:NT * E], tri[:], flat, start=True, stop=False, skip_group_check=True)
            for t in range(NT):
                last = nc.tensor.matmul(ps[:, 5, E * (t + 1):E * (NT + 1)].rearrange("p (a e) -> p a e", e=E), ones[:],
                                        bcast(sel[:, t], 1, NT - t), start=False, stop=t == NT - 1, skip_group_check=True)
            last.then_inc(sB["rank_ps"], 1)
            pe.wait_ge(sB["payload"], 2)
            for q in range(TOP * NT):
                pe.wait_ge(sB["rowhot"], q // 8 + 1)
                last = nc.tensor.matmul(ps[:, 6, 0:2 * NCH], rowhot[:, q // 8 % 2, q % 8], payload[:, q].rearrange("p v c -> p (v c)"),
                                        start=q == 0, stop=q == TOP * NT - 1)
                if q % 8 == 7:
                    last.then_inc(sB["rowhot_used"], 1)
            for t in range(NT):
                last = nc.tensor.transpose(ps[0:E, t // 4, P * (t % 4):P * (t % 4) + P], sel[:, t, :], ident[:])
            last.then_inc(sB["ind_ps"], 1)
            pe.wait_ge(sB["route_ready"], 2)
            pe.wait_ge(sB["ind_sb"], 1)
            pe.wait_ge(w0_in, 144)

            def values(it, s):
                pe.wait_ge(sB["y_ready"], NSTR * it + s + 1)
                first = isinstance(it, int) and it == 0 and s == 0
                final = isinstance(it, int) and it == NIT - 1 and s == NSTR - 1
                for m in range(DK):
                    last = nc.tensor.matmul(ps[:, 3 + m, 0:E], y0[:, s, P * m:P * m + P], wexp[:, bass.ds(NSTR * it + s, 1), :].squeeze(1),
                                            start=first, stop=final)
                last.then_inc(sB["v_ps"], 1)

            def chunks(it):
                e = [nc.tensor.value_load(ce_i[0:1, bass.ds(NSTR * it + s, 1)], min_val=0, max_val=E - 1) for s in range(NSTR)]
                for l in range(NL):
                    for s in range(NSTR):
                        if l == 0:
                            pe.wait_ge(gathered[s], 16 * (it + 1))
                            wait(pe, sB["l_sb"], NL * NSTR * (it - 1) + NSTR * (NL - 1) + s + 1)
                        else:
                            pe.wait_ge(sB["l_sb"], NL * NSTR * it + NSTR * (l - 1) + s + 1)
                        src = h0 if l else g0
                        for k in range(DK):
                            last = nc.tensor.transpose(ps[:, s, P * k:P * k + P], src[:, s, P * k:P * k + P], ident[:])
                        last.then_inc(sB["tp_ps"], 1)
                    for s in range(NSTR):
                        pe.wait_ge(sB["tp_sb"], NL * NSTR * it + NSTR * l + s + 1)
                        for k in range(DK):
                            last = nc.tensor.matmul(ps[:, s, D:2 * D], hT[:, s, k, :], w0[:, bass.ds(e[s], 1), l, k, :].squeeze(1),
                                                    start=k == 0, stop=k == DK - 1)
                        last.then_inc(sB["l_ps"], 1)
                    if l == 0 and (not isinstance(it, int) or it > 0):
                        for s in range(NSTR):
                            values(it - 1, s)

            chunks(0)
            chunks(1)
            with pe.Fori(2, NIT) as it:
                chunks(it)
            for s in range(NSTR):
                values(NIT - 1, s)
            pe.wait_ge(sB["vT_sb"], 1)
            for m in range(DK):
                last = nc.tensor.transpose(ps[0:E, 5, P * m:P * m + P], vT[:, m, :], ident[:])
            last.then_inc(sB["v_tp"], 1)
            pe.wait_ge(sB["v_sb"], 1)
            for m in range(NT // 2):
                if m >= 4:
                    pe.wait_ge(sB["x2_ready"], m - 3)
                for q in range(2):
                    last = nc.tensor.matmul(ps[:, m % 4, D * q:D * q + D], indT[:, 2 * m + q, :], v0[:], start=True, stop=True)
                last.then_inc(sB["o_ps"], 1)
            pe.wait_ge(sB["x2_ready"], NT // 2)

            def transpose_tile(i, s):
                m = 2 * i + s
                wait(pe, sC["xn_ready"], m + 1)
                wait(pe, sC["rot_ready"], 4 * m)
                for k in range(DK):
                    last = nc.tensor.transpose(ps[:, 6, P * k:P * k + P], xn[:, s % 2, P * k:P * k + P], ident[:])
                last.then_inc(sC["xT_ps"], 1)

            def latents(i, s):
                wait(pe, sC["xT_sb"], 2 * i + s + 1)
                for k in range(DK):
                    last = nc.tensor.matmul(ps[0:DQ, 6, D:D + P], wqd[:, k, :], xnT[:, s % 2, k, :], start=k == 0, stop=k == DK - 1)
                last.then_inc(sC["qc_ps"], 1)

            transpose_tile(0, 0)
            latents(0, 0)

            def body(i, u):
                n = 2 * i + u
                v = 1 - u

                def transpose_weights(c):
                    flat = pc[:, c].rearrange("p h k -> p (h k)")
                    wait(pe, sC["norm_done"], 2 * n + c + 1)
                    wait(pe, sC["pta_ev"], 2 * n + c)
                    for j in range(3):
                        last = nc.tensor.transpose(PTA[:, j], flat[:, P * j:P * j + P], ident[:])
                    last.then_inc(sC["pta_ps"], 1)
                    wait(pe, sC["ptb_ev"], 2 * n + c)
                    nc.tensor.transpose(PTB[:, 0], flat[:, 3 * P:4 * P], ident[:])
                    nc.tensor.transpose(PTB[0:rows(4), 1], flat[:, 4 * P:UK], ident[:]).then_inc(sC["ptb_ps"], 1)

                def apply_weights(c):
                    wait(pe, sC["ptb_ev"], 2 * n + c + 1)
                    for j in range(NJ):
                        last = nc.tensor.matmul(ps[:, 7, 0:D], pcT[0:rows(j), c, j, :], vw[0:rows(j), u, c, j, :],
                                                start=c == 0 and j == 0, stop=c == 1 and j == NJ - 1)
                    return last

                def project(g):
                    wait(pe, sC["rot_ready"], 4 * (n + 1) + g)
                    for h in range(4 * g, 4 * g + 4):
                        last = nc.tensor.matmul(ps[:, 6, P * (h % 4):P * (h % 4) + P], wr2[:, h, :], qc[:, v, :], start=True, stop=True)
                    last.then_inc(sC["rope_ps"], 1)

                def nope(g):
                    wait(pe, sC["mask_done"], 2 * n + 1 + g // 2)
                    nc.tensor.matmul(ps[:, g, 0:4 * LK], qc[:, v, :], anope[:, v, 4 * g:4 * g + 4, :].rearrange("p h k -> p (h k)"),
                                     start=True, stop=False, skip_group_check=True)

                def rope(g):
                    wait(pe, sC["rot_ready"], 4 * (n + 1) + g + 1)
                    for h in range(4):
                        last = nc.tensor.matmul(ps[:, g, LK * h:LK * h + LK], rot[:, g, h, :], kr2[:, v, :],
                                                start=False, stop=h == 3, skip_group_check=True)
                    if g % 2:
                        last.then_inc(sC["s_ps"], 1)

                if live(i, u + 1):
                    wait(pe, sC["qc_sb"], n + 2)
                    project(0)
                    nope(0)
                if live(i, u):
                    transpose_weights(0)
                if live(i, u + 1):
                    project(1)
                    nope(1)
                    rope(0)
                    project(2)
                    rope(1)
                    nope(2)
                if live(i, u):
                    transpose_weights(1)
                if live(i, u + 1):
                    project(3)
                    nope(3)
                    rope(2)
                if live(i, u + 2):
                    transpose_tile(i, u + 2)
                if live(i, u + 1):
                    rope(3)
                if live(i, u):
                    wait(pe, sC["x_ready"], n)
                    apply_weights(0)
                if live(i, u + 2):
                    latents(i, u + 2)
                if live(i, u):
                    last = apply_weights(1)
                    last.then_inc(sC["out_ps"], 1)

            pipeline(pe, body)
            pe.wait_ge(sC["x_ready"], NT)
            pe.wait_ge(sC["ptb_ev"], 2 * NT)
            pe.wait_ge(sC["mask_done"], 2 * NT)
            pe.wait_ge(sD["w_in"], 80)

            def body(i, u):
                n = 2 * i + u
                v = 1 - u

                def experts(g):
                    wait(pe, sD["accB"], 4 * (n - 1) + g + 1)
                    wait(pe, sD["accA"], 5 * (n - 1) + g + 2)
                    for k in range(DK):
                        last = nc.tensor.matmul(ps[:, g, :], xnT[:, u, k, :], we[:, k, 2 * D * g:2 * D * g + 2 * D], start=k == 0, stop=k == DK - 1)
                    last.then_inc(sD["e_ps"], 1)

                if live(i, u + 1):
                    wait(pe, sD["xn_ready"], n + 2)
                    wait(pe, sD["xT_sb"], n + 1)
                    for k in range(DK):
                        last = nc.tensor.transpose(ps[:, 4, P * k:P * k + P], xn[:, v, P * k:P * k + P], ident[:])
                    last.then_inc(sD["xT_ps"], 1)
                if live(i, u):
                    experts(0)
                if live(i, u + 1):
                    wait(pe, sD["xT_sb"], n + 2)
                    wait(pe, sD["chain"], 10 * n + 1)
                    for k in range(DK):
                        last = nc.tensor.matmul(ps[:, 5, 0:E], xnT[:, v, k, :], wg[:, k, :], start=k == 0, stop=k == DK - 1)
                    last.then_inc(sD["lg_ps"], 1)
                if live(i, u):
                    experts(1)
                    experts(2)
                    experts(3)
                if live(i, u + 1):
                    wait(pe, sD["chain"], 10 * (n + 2))
                    wait(pe, sD["gT_sb"], n + 1)
                    nc.tensor.transpose(ps[0:E, 6, 0:P], gates[:, v, :], ident[:]).then_inc(sD["gT_ps"], 1)
                    wait(pe, sD["gT_sb"], n + 2)
                    wait(pe, sD["accA"], 5 * n + 1)
                    nc.tensor.matmul(ps[:, 7, 0:D], gatesT[:, v, :], be[:], start=True, stop=True).then_inc(sD["be_ps"], 1)

            pipeline(pe, body)


_INS = ['x', 'ctx_1024', 'L0_xattn_Wq', 'L0_xattn_bq', 'L0_xattn_Wk', 'L0_xattn_bk', 'L0_xattn_Wv', 'L0_xattn_bv',
        'L0_xattn_Wo', 'L0_xattn_bo', 'L0_ffn_gate_w', 'L0_ffn_gate_b', 'L0_ffn_w1', 'L0_ffn_b1', 'L0_ffn_w2', 'L0_ffn_b2',
        'L0_ffn_w3', 'L0_ffn_b3', 'itok_BxS_0_511', 'L1_xattn_w_kv_comp', 'L1_xattn_w_q_down', 'L1_xattn_w_q_up', 'L1_xattn_w_q_rope',
        'L1_xattn_w_k_up', 'L1_xattn_w_k_rope', 'L1_xattn_w_v_up', 'L1_xattn_w_out', 'L1_ffn_Wg', 'L1_ffn_We', 'L1_ffn_be']


def constants():
    import numpy as np
    f = np.float32
    row = np.arange(P)
    c = {"c_ident": np.eye(P, dtype=f)}
    c["c_tri"] = (row[:, None] < row[None]).astype(f)
    c["c_ones"] = np.ones((P, P), f)
    c["c_iota"] = np.tile(row.astype(f), (P, 1))
    c["c_rev8"] = np.tile(np.arange(E, 0, -1).astype(f), (P, 1))
    c["c_tri8"] = np.tile(np.tril(np.ones((E, E), f)), (P, 1, 1))
    c["c_tokid"] = (np.arange(NT)[None] * P + row[:, None]).astype(f)
    half = RD // 2
    inv = (f(1.0) / f(10000.0) ** (np.arange(half, dtype=f) / f(half))).astype(f)
    ang = np.arange(S, dtype=f)[None] * inv[:, None]
    cos, sin = np.cos(ang).astype(f), np.sin(ang).astype(f)
    c["c_trig"] = np.concatenate([cos, cos, -sin, sin])
    kc, ks = np.concatenate([cos, cos])[:, :LK], np.concatenate([-sin, sin])[:, :LK]
    c["c_ktrig"] = np.stack([np.concatenate([kc, kc]), np.concatenate([ks, ks])], 1)
    c["c_iok"] = np.tile(np.arange(LK, dtype=f), (P, 1))
    c["c_kmask"] = (row[:, None] // HD == np.arange(HC)[None]).astype(f)
    i = np.arange(NJ)[None, :] * P + row[:, None]
    c["c_vmask"] = ((i // LK)[:, :, None] == np.arange(HC)).astype(f)
    return c


def kernel(**inputs):
    import numpy as np
    import concourse.bacc as bacc
    from concourse import mybir as mb
    from concourse.bass_utils import run_bass_kernel_spmd as run
    nc = bacc.Bacc("TRN2", target_bir_lowering=False, num_devices=1)
    arrays, io = {}, {}
    data = {n: np.ascontiguousarray(inputs[n]) for n in _INS}
    for n in ('L0_xattn_bq', 'L0_xattn_bk'):
        data[n] = np.ascontiguousarray(data[n].reshape(2, P).T)
    data['itok_BxS_0_511'] = np.ascontiguousarray(data['itok_BxS_0_511'].reshape(NT, P).T)
    data['L1_xattn_w_q_up'] = np.ascontiguousarray(data['L1_xattn_w_q_up'].reshape(DQ, NP2, P).transpose(2, 1, 0))
    data['L0_ffn_gate_b'] = data['L0_ffn_gate_b'].reshape(E, 1)
    data.update(constants())
    for name, a in data.items():
        arrays[f"in_{name}"] = a
        io[name] = nc.dram_tensor(f"in_{name}", a.shape, mb.dt.from_np(a.dtype), kind="ExternalInput").ap()
    io["out"] = nc.dram_tensor("out_0", (B, S, D), mb.dt.float32, kind="ExternalOutput").ap()
    io["xn_dram"] = nc.dram_tensor("xn_dram", (B * S, D), mb.dt.float32).ap()
    build(nc, io)
    r = run(nc, [arrays], core_ids=[0])
    return r.results[0]["out_0"]
```

```python
import numpy as np
import concourse.bass as bass
from concourse import mybir
from contextlib import ExitStack

P = 128
B = 2
S = 1024
D = 256
DK = D // P
TPB = S // P
NT = B * TPB
LK = 77
H = 16
HC = H // 2
UK = HC * LK
NJ = -(-UK // P)
HD = D // H
E = 8
EA = 2
LINKS = 8
ACCS = E - EA + 1
NL = 3
TOP = 2
NCH = (TOP * B * S + E * (P - 1)) // P
NSTR = 3
NIT = NCH // NSTR
STEPS = NL * NSTR
RING = 4
DQ = 96
DC = 64
RD = 64
NP2 = H // 2
SCALE = float(np.float32(1.0) / np.float32(np.sqrt(np.float32(2 * RD))))
FMIN = float(np.finfo(np.float32).min)
PAD = P + 2 * LK + P
VW1 = HD + 1


def rows(j):
    return min(P, UK - P * j)


def heads_of(j):
    h0 = P * j // LK
    return h0, (P * j + rows(j) - 1) // LK - h0 + 1


def v_unit(q):
    return q // (2 * NJ), q // NJ % 2, q % NJ


def bcast(ap, axis, n):
    u = ap.unsqueeze(axis)
    shape = list(u.shape)
    shape[axis] = n
    return u.broadcast_to(shape)


def build(nc, io):
    F32 = mybir.dt.float32
    F32R = mybir.dt.float32r
    I32 = mybir.dt.int32
    ALU = mybir.AluOpType
    ACT = mybir.ActivationFunctionType
    AX = mybir.AxisListType

    with ExitStack() as st:
        def sb(name, shape, dt=F32):
            return st.enter_context(nc.sbuf_tensor(name, shape, dt))

        def sem(name):
            return st.enter_context(nc.semaphore(name))

        ps = st.enter_context(nc.psum_tensor("ps", [P, 8, 512], F32))

        x = sb("x", [P, B, TPB, D])
        ident = sb("ident", [P, P])
        stats = sb("stats", [P, 2, 6])
        st_all = sb("st_all", [P, B, TPB, 6])
        xs = sb("xs", [P, 2, D])
        mv = sb("mv", [P, B, TPB, 2])
        rstd = sb("rstd", [P, B, TPB])
        epsv = sb("epsv", [P, B, TPB])
        power = sb("power", [P, B, TPB])
        xn = sb("xn", [P, 2, D])
        xnT = sb("xnT", [P, 2, DK, P])
        b0 = sb("b0", [P, E, NL, D])
        wqd = sb("wqd", [P, DK, DQ])
        wr2 = sb("wr2", [DQ, H, 2 * RD])
        trig = sb("trig", [P, S])
        negm = sb("negm", [P, NT, LK])
        seg_i = sb("seg_i", [P, NT], I32)
        seg = sb("seg", [P, 2, NT])
        iok = sb("iok", [P, LK])
        anope = sb("anope", [DQ, B, H, LK])
        kr2 = sb("kr2", [P, B, LK])
        vw = sb("vw", [P, B, 2, NJ, D])
        knT = vw[:].rearrange("p b c j d -> p (b c j d)")[:, 0:NP2 * B * LK].rearrange("p (q b k) -> p q b k", q=NP2, b=B)
        room = b0[:].rearrange("p e l d -> p (e l d)")
        at = [0]

        def carve(cols):
            at[0] += cols
            return room[:, at[0] - cols:at[0]]

        wkup = carve(H * RD)[0:DC]
        wvup = carve(H * RD)[0:DC]
        wqupT = carve(NP2 * DQ).rearrange("p (q c) -> p q c", q=NP2)
        wout = carve(NP2 * D).rearrange("p (q d) -> p q d", q=NP2)
        wkvc = carve(DK * DC).rearrange("p (k c) -> p k c", k=DK)
        wkr = carve(2 * 2 * RD).rearrange("p (v r) -> p v r", v=2)[0:DC]
        kvcT = carve(B * LK)[0:DC]
        krt = carve(2 * LK).rearrange("p (v k) -> p v k", v=2)
        kruv = carve(2 * B * LK).rearrange("p (v b k) -> p v b k", v=2, b=B)
        gw = sb("gw", [P, DK, E])
        gb = sb("gb", [E, 1])
        ctxT = sb("ctxT", [P, DK, B, LK])
        experts0 = ExitStack()
        w0 = experts0.enter_context(nc.sbuf_tensor("w0", [P, E, NL, DK, D], F32))
        phase = ExitStack()

        def sb(name, shape, dt=F32):
            return phase.enter_context(nc.sbuf_tensor(name, shape, dt))

        wq = sb("wq", [P, DK, D])
        wk = sb("wk", [P, DK, D])
        wv = sb("wv", [P, DK, D])
        wo = sb("wo", [P, DK, D])
        bq = sb("bq", [P, 2])
        bk = sb("bk", [P, 2])
        bv = sb("bv", [P, D])
        bo = sb("bo", [P, D])
        kmask = sb("kmask", [P, HC])
        vmask = sb("vmask", [P, NJ, HC])
        ctx = sb("ctx", [LK, B, D])
        ctx_rep = sb("ctx_rep", [P, DK, B, HC, LK])
        kT = sb("kT", [P, 2, B, LK])
        kbd = sb("kbd", [P, B, 2, HC, LK])
        vbd = sb("vbd", [P, B, 2, NJ, HC, VW1])
        vtmp = sb("vtmp", [P, 2, 4, P])
        qT = sb("qT", [P, 2, 2, P])
        pr = sb("pr", [P, 2, HC, LK])
        prT = sb("prT", [P, 2, NJ, P])
        flat_prT = prT[:].rearrange("p c j q -> p (c j q)")
        VTMP = [vtmp[:, 0], vtmp[:, 1]] + [t.rearrange("p (q d) -> p q d", q=4) for t in (
            pr[:, 1].rearrange("p h k -> p (h k)")[:, 0:4 * P], flat_prT[:, 0:4 * P], flat_prT[:, 4 * P:8 * P])]
        nmax = sb("nmax", [P, 2, HC])
        rsum = sb("rsum", [P, 2, HC])
        on = sb("on", [P, 2, HC, HD])
        oT = sb("oT", [P, 2, P])

        phase.close()
        phase = ExitStack()
        lg = sb("lg", [E, B, S])
        gmax = sb("gmax", [E, B])
        gsum = sb("gsum", [E, B])
        prob = sb("prob", [P, NT, E])
        top = sb("top", [P, TOP, NT])
        key = sb("key", [P, NT, E])
        kmax = sb("kmax", [P, NT])
        oneh = sb("oneh", [P, TOP, NT, E])
        sel = sb("sel", [P, NT, E])
        prob2 = sb("prob2", [P, NT, E])
        cmp16 = sb("cmp16", [P, E, NT])
        nch = sb("nch", [P, E])
        tri8 = sb("tri8", [P, E, E])
        cend = sb("cend", [P, E])
        base = sb("base", [P, E])
        pos = sb("pos", [P, NT, E])
        slot = sb("slot", [P, TOP * NT])
        slot_i = sb("slot_i", [P, 3, TOP * NT], I32)
        rc = sb("rc", [P, 2, TOP * NT])
        rowhot = sb("rowhot", [P, 2, 8, P])
        chhot = sb("chhot", [P, TOP * NT, NCH])
        payload = sb("payload", [P, TOP * NT, 2, NCH])
        xng = payload[:].rearrange("p t v c -> p (t v c)")[:, 0:RING * D].rearrange("p (r d) -> p r d", r=RING)
        cmp8 = sb("cmp8", [P, NCH, E])
        ce = sb("ce", [P, NCH])
        ce_i = sb("ce_i", [P, NCH], I32)
        tok_i = sb("tok_i", [P, NCH], I32)
        wslot = sb("wslot", [P, NCH])
        wexp = sb("wexp", [P, NCH, E])
        indT = sb("indT", [E, NT, P])
        tri = sb("tri", [P, P])
        ones = sb("ones", [P, P])
        iot = sb("iot", [P, P])
        rev8 = sb("rev8", [P, E])
        tokid = sb("tokid", [P, NT])
        work0 = sb("work0", [P, NP2 * PAD])
        vbdT = work0[:].rearrange("p (q c) -> p q c", q=NP2)
        w_ = lambda q: work0[:, NSTR * D * q:NSTR * D * (q + 1)].rearrange("p (s d) -> p s d", s=NSTR)
        g0 = w_(0)
        hT = w_(1).rearrange("p s (k q) -> p s k q", k=DK)
        h0 = w_(2)
        y0 = w_(3)
        vT = sb("vT", [P, DK, E])
        v0 = sb("v0", [E, D])
        phase.close()
        experts0.close()
        phase = ExitStack()
        NW = DK * E * D
        WCOLS = NW // NT
        we = sb("we", [P, NW])
        we_hi = sb("we_hi", [P, NW], F32R)
        we_lo = sb("we_lo", [P, NW], F32R)
        qc = sb("qc", [DQ, 2, P])
        rot = sb("rot", [P, 4, 4, P])
        pc = sb("pc", [P, 2, HC, LK])
        pcT = sb("pcT", [P, 2, NJ, P])
        pmax = sb("pmax", [P, 2, HC])
        psm = sb("psm", [P, 2, HC])
        wg = sb("wg", [P, DK, E])
        be = sb("be", [E, D])
        lt = sb("lt", [P, 2, E])
        lmax = sb("lmax", [P, 2, E])
        lidx = sb("lidx", [P, 2, E], mybir.dt.uint32)
        lidf = sb("lidf", [P, 2, TOP])
        gt = sb("gt", [P, 2, TOP])
        gd = sb("gd", [P, 2, 2])
        goh = sb("goh", [P, 2, TOP, E])
        gates = sb("gates", [P, 2, E])
        gatesT = sb("gatesT", [E, 2, P])
        acc = sb("acc", [P, 2, D])
        part = sb("part", [P, 2, EA, D])
        xhi = sb("xhi", [P, 2, DK, P], F32R)
        xlo = sb("xlo", [P, 2, DK, P], F32R)
        y = sb("y", [P, 2, D])
        iot8 = sb("iot8", [P, E])
        phase.close()
        by_k = lambda t: t.rearrange("p (k n) -> p k n", k=DK)

        S_ = lambda c: ps[:, 2 * c:2 * c + 2, 0:4 * LK].rearrange("p a (h k) -> p a h k", h=4)
        PTA = ps[:, 4, 0:3 * P].rearrange("p (j q) -> p j q", j=3)
        PTB = ps[:, 5, 0:2 * P].rearrange("p (j q) -> p j q", j=2)
        XT = ps[:, 6, 0:D].rearrange("p (k q) -> p k q", k=DK)
        QT = ps[:, 6, 0:D].rearrange("p (c q) -> p c q", c=2)
        O_ = ps[:, 7, 0:2 * HC * VW1].rearrange("p (c h v) -> p c h v", c=2, h=HC)
        OT = ps[:, 6, D:2 * D].rearrange("p (c q) -> p c q", c=2)
        OUT = ps[:, 7, 0:D]

        x_in = [sem(f"x_in{g}") for g in range(2)]
        k_in = sem("k_in")
        v_in = sem("v_in")
        q_in = sem("q_in")
        g_in = sem("g_in")
        c_in = sem("c_in")
        w0_in = sem("w0_in")
        const_set = sem("const_set")
        sA = {n: sem("a_" + n) for n in (
            "stats aggr rstd ones_ready kv_ps kv_sb kbd_ready vbd_ready ctxT_ps ctxT_sb rep_ready "
            "xn_ready xT_ps xT_sb q_ps q_ready s_ps max_done sub_done exp_done pta_ps ptb_ps pta_ev ptb_ev "
            "o_ps rsum_done on_ready oT_ps oT_sb out_ps x1_ready aggr2 stats2 xo_ready x1_kept stats_kept").split()}

        sB = {n: sem("b_" + n) for n in (
            "const rstd xn_ready xT_ps xT_sb lg_ps lg_sb chain gexp pT_ps ind_ps ind_sb rank_ps payload rowhot rowhot_used "
            "tok_ready route_ready tp_ps tp_sb l_ps l_sb y_ready v_ps vT_sb v_tp v_sb o_ps x2_ready stats aggr").split()}
        stored = [sem(f"b_stored{r}") for r in range(RING)]
        gathered = [sem(f"b_gathered{s}") for s in range(NSTR)]

        sC = {n: sem("c_" + n) for n in (
            "mask set kvc_ps kvc_sb kn_ps kn_sb v_ps v_sb a_ps a_sb kr_ps kr_sb kr_mul vw_ps vw_sb zero work_free "
            "aggr rstd xn_ready xT_ps xT_sb qc_ps qc_sb rope_ps rot_ready s_ps mask_done max_done sub_done exp_done sum_done rsum_done norm_done "
            "pta_ps ptb_ps pta_ev ptb_ev out_ps x_ready x_kept stats stats_kept").split()}
        sD = {n: sem("d_" + n) for n in (
            "we_in we_hi we_lo hi lo scaled summed acc w_in aggr rstd xn_ready xT_ps xT_sb lg_ps chain diff exp gates gT_ps gT_sb be_ps e_ps chain2 y_ready").split()}
        written = [sem(f"d_written{u}") for u in range(2)]
        c_w = sem("c_w")

        VBANK = (2, 3, 7)

        block = st.enter_context(nc.Block())

        def wait(eng, s, n):
            if not isinstance(n, int) or n > 0:
                eng.wait_ge(s, n)

        def tile_at(i, s):
            return s % 2, i + s // 2

        def pipeline(eng, body):
            body(-1, 1)
            body(0, 0)
            body(0, 1)
            with eng.Fori(1, TPB - 1) as i:
                body(i, 0)
                body(i, 1)
            body(TPB - 1, 0)
            body(TPB - 1, 1)
            body(TPB, 0)

        def live(i, s):
            return not isinstance(i, int) or 0 <= 2 * i + s < NT

        @block.sync
        def _(sp):
            sp.dma_start(ctx[:], io["ctx_1024"].rearrange("b k d -> k b d")).then_inc(c_in, 16)
            sp.dma_start(ident[:], io["c_ident"]).then_inc(c_in, 16)
            sp.dma_start(wk[:], io["L0_xattn_Wk"].rearrange("(k p) n -> p k n", p=P)).then_inc(k_in, 16)
            sp.dma_start(bk[:], io["L0_xattn_bk"]).then_inc(k_in, 16)
            sp.dma_start(kmask[:], io["c_kmask"]).then_inc(k_in, 16)
            sp.dma_start(wv[:], io["L0_xattn_Wv"].rearrange("(k p) n -> p k n", p=P)).then_inc(v_in, 16)
            sp.dma_start(bv[:], io["L0_xattn_bv"].partition_broadcast(P)).then_inc(v_in, 16)
            sp.dma_start(vmask[:], io["c_vmask"]).then_inc(v_in, 16)
            sp.dma_start(wq[:], io["L0_xattn_Wq"].rearrange("(k p) n -> p k n", p=P)).then_inc(q_in, 16)
            sp.dma_start(bq[:], io["L0_xattn_bq"]).then_inc(q_in, 16)
            sp.dma_start(wo[:], io["L0_xattn_Wo"].rearrange("(k p) n -> p k n", p=P)).then_inc(q_in, 16)
            sp.dma_start(bo[:], io["L0_xattn_bo"].partition_broadcast(P)).then_inc(q_in, 16)
            sp.dma_start(gw[:], io["L0_ffn_gate_w"].rearrange("(k p) e -> p k e", p=P)).then_inc(g_in, 16)
            sp.dma_start(gb[:], io["L0_ffn_gate_b"]).then_inc(g_in, 16)
            for l, n in enumerate(("L0_ffn_w1", "L0_ffn_w2", "L0_ffn_w3")):
                for k in range(DK):
                    sp.dma_start(w0[:, :, l, k, :], io[n][:, P * k:P * k + P, :].rearrange("e p o -> p e o")).then_inc(w0_in, 16)
            for dst, n in ((wkup, "L1_xattn_w_k_up"), (wvup, "L1_xattn_w_v_up"), (wqupT, "L1_xattn_w_q_up"), (trig[:], "c_trig"),
                           (seg_i[:], "itok_BxS_0_511"), (krt, "c_ktrig"), (iok[:], "c_iok")):
                sp.dma_start(dst, io[n]).then_inc(c_w, 16)
            sp.dma_start(wout, io["L1_xattn_w_out"].rearrange("(q p) n -> p q n", p=P)).then_inc(c_w, 16)
            sp.dma_start(wkvc, io["L1_xattn_w_kv_comp"].rearrange("(k p) n -> p k n", p=P)).then_inc(c_w, 16)
            sp.dma_start(wqd[:], io["L1_xattn_w_q_down"].rearrange("(k p) n -> p k n", p=P)).then_inc(c_w, 16)
            half = RD // 2
            wqr = io["L1_xattn_w_q_rope"].rearrange("c (h r) -> c h r", h=H)
            for dst, src in ((wr2[:, :, 0:RD], wqr), (wr2[:, :, RD:RD + half], wqr[:, :, half:RD]), (wr2[:, :, RD + half:], wqr[:, :, 0:half])):
                sp.dma_start(dst, src).then_inc(c_w, 16)
            for a in range(2):
                sp.dma_start(wkr[:, 0, RD * a:RD * a + RD], io["L1_xattn_w_k_rope"]).then_inc(c_w, 16)
                sp.dma_start(wkr[:, 1, RD * a:RD * a + half], io["L1_xattn_w_k_rope"][:, half:RD]).then_inc(c_w, 16)
                sp.dma_start(wkr[:, 1, RD * a + half:RD * a + RD], io["L1_xattn_w_k_rope"][:, 0:half]).then_inc(c_w, 16)
            sp.wait_ge(sA["x1_ready"], NT)
            for dst, n in ((tri, "c_tri"), (ones, "c_ones"), (iot, "c_iota"), (rev8, "c_rev8"), (tri8, "c_tri8"), (tokid, "c_tokid")):
                sp.dma_start(dst[:], io[n]).then_inc(sB["const"], 16)
            for n in range(NT):
                b, j = tile_at(0, n)
                sp.wait_ge(sB["xn_ready"], n + 1)
                sp.dma_start(io["xn_dram"][P * (TPB * b + j):P * (TPB * b + j + 1), :], xng[:, n % RING, :]).then_inc(stored[n % RING], 16)
            sp.wait_ge(sC["vw_ps"], 2 * NJ)
            sp.wait_ge(sC["kr_mul"], 3)
            for l, n in enumerate(("L0_ffn_b1", "L0_ffn_b2", "L0_ffn_b3")):
                sp.dma_start(b0[:, :, l, :], io[n].partition_broadcast(P)).then_inc(w0_in, 16)
            sp.wait_ge(sB["l_sb"], NL * NCH)
            for k in range(DK):
                sp.dma_start(by_k(we)[:, k, :].rearrange("p (e d) -> p e d", e=E), io["L1_ffn_We"][:, P * k:P * k + P, :].rearrange("e p d -> p e d")).then_inc(sD["we_in"], 16)
            sp.wait_ge(sB["x2_ready"], NT // 2)
            sp.dma_start(wg[:], io["L1_ffn_Wg"].rearrange("(k p) e -> p k e", p=P)).then_inc(sD["w_in"], 16)
            sp.dma_start(be[:], io["L1_ffn_be"]).then_inc(sD["w_in"], 16)
            sp.dma_start(iot8[:], io["c_iota"][:, 0:E]).then_inc(sD["w_in"], 16)
            for n in range(NT):
                b, j = tile_at(0, n)
                sp.wait_ge(sD["y_ready"], n + 1)
                sp.dma_start(io["out"][b, P * j:P * j + P, :], y[:, b, :]).then_inc(written[b], 16)
            for b in range(B):
                sp.wait_ge(written[b], 16 * TPB)
        @block.gpsimd
        def _(pool):
            nc.gpsimd.memset(epsv[:], 1e-5).then_inc(const_set, 1)
            nc.gpsimd.memset(power[:], -0.5).then_inc(const_set, 1)
            pool.wait_ge(const_set, 2)
            pool.wait_ge(sA["aggr"], 1)
            nc.gpsimd.tensor_tensor(rstd[:], mv[:, :, :, 1], epsv[:], ALU.add).then_inc(sA["rstd"], 1)
            pool.wait_ge(sA["rstd"], 1)
            nc.gpsimd.tensor_tensor(rstd[:], rstd[:], power[:], ALU.pow).then_inc(sA["rstd"], 1)
            pool.wait_ge(v_in, 48)
            for g in range(5):
                pool.wait_ge(sA["kv_sb"], g + 2)
                for q in range(4):
                    b, c, j = v_unit(4 * g + q)
                    r = rows(j)
                    last = nc.gpsimd.tensor_tensor(vbd[0:r, b, c, j, :, 0:HD], VTMP[g][0:r, q].rearrange("p (h d) -> p h d", h=HC),
                                                   bcast(vmask[0:r, j], 2, HD), ALU.mult)
                last.then_inc(sA["vbd_ready"], 1)
            pool.wait_ge(q_in, 64)

            def body(i, u):
                if live(i, u):
                    b, j = tile_at(i, u)
                    jj = bass.ds(j, 1)
                    wait(pool, sA["xn_ready"], 2 * i + u + 1)
                    nc.gpsimd.tensor_tensor(x[:, b, jj, :].squeeze(1), x[:, b, jj, :].squeeze(1), bo[:], ALU.add).then_inc(sA["xo_ready"], 1)

            pipeline(pool, body)

            pool.wait_ge(sA["stats_kept"], NT)
            nc.gpsimd.memset(work0[:], 0.0).then_inc(sC["zero"], 1)
            pool.wait_ge(sA["aggr2"], NT)
            nc.gpsimd.tensor_tensor(rstd[:], mv[:, :, :, 1], epsv[:], ALU.add).then_inc(sB["rstd"], 1)
            pool.wait_ge(sB["rstd"], 1)
            nc.gpsimd.tensor_tensor(rstd[:], rstd[:], power[:], ALU.pow).then_inc(sB["rstd"], 1)
            pool.wait_ge(sC["kr_sb"], 1)
            for v in range(2):
                last = nc.gpsimd.tensor_tensor(kruv[:, v], kruv[:, v], bcast(krt[:, v], 1, B), ALU.mult)
                last.then_inc(sC["kr_mul"], 1)
            pool.wait_ge(sC["kr_mul"], 2)
            nc.gpsimd.tensor_tensor(kr2[:], kruv[:, 0], kruv[:, 1], ALU.add).then_inc(sC["kr_mul"], 1)
            for r in range(RING):
                pool.wait_ge(stored[r], 16 * NT // RING)
            pool.wait_ge(sB["tok_ready"], 1)
            pool.wait_ge(sC["vw_ps"], 2 * NJ)
            for c in range(NCH):
                it, s = c // NSTR, c % NSTR
                if it:
                    pool.wait_ge(sB["tp_ps"], NL * NSTR * (it - 1) + s + 1)
                pool.indirect_dma_start(out=g0[:, s, :], out_offset=None, in_=io["xn_dram"],
                                        in_offset=bass.IndirectOffsetOnAxis(ap=tok_i[:, c:c + 1], axis=0)).then_inc(gathered[s], 16)
            def rstd_of(done, s):
                pool.wait_ge(done, NT)
                nc.gpsimd.tensor_tensor(rstd[:], mv[:, :, :, 1], epsv[:], ALU.add).then_inc(s, 1)
                pool.wait_ge(s, 1)
                nc.gpsimd.tensor_tensor(rstd[:], rstd[:], power[:], ALU.pow).then_inc(s, 1)

            pool.wait_ge(sB["aggr"], NT // 2)
            nc.gpsimd.tensor_tensor(rstd[:], mv[:, :, :, 1], epsv[:], ALU.add).then_inc(sC["rstd"], 1)
            pool.wait_ge(sC["rstd"], 1)
            nc.gpsimd.tensor_tensor(rstd[:], rstd[:], power[:], ALU.pow).then_inc(sC["rstd"], 1)

            def body(i, u):
                n = 2 * i + u

                def norm(m, c):
                    wait(pool, sC["rsum_done"], 2 * m + c + 1)
                    nc.gpsimd.tensor_tensor(pc[:, c], pc[:, c], bcast(psm[:, c], 2, LK), ALU.mult).then_inc(sC["norm_done"], 1)

                def sub(m, c):
                    wait(pool, sC["max_done"], 2 * m + c + 1)
                    nc.gpsimd.tensor_tensor(pc[:, c], pc[:, c], bcast(pmax[:, c], 2, LK), ALU.subtract).then_inc(sC["sub_done"], 1)

                if live(i, u):
                    norm(n, 1)
                if live(i, u + 1):
                    sub(n + 1, 0)
                    norm(n + 1, 0)
                    sub(n + 1, 1)
                if live(i, u):
                    wait(pool, sD["we_hi"], n + 1)
                    cols = bass.ds(2 * WCOLS * i + WCOLS * u, WCOLS)
                    nc.gpsimd.tensor_tensor(we_lo[:, cols], we[:, cols], we_hi[:, cols], ALU.subtract).then_inc(sD["we_lo"], 1)

            pipeline(pool, body)
            rstd_of(sD["aggr"], sD["rstd"])

            def split_tile(i, s):
                m = 2 * i + s
                wait(pool, sD["hi"], m + 1)
                wait(pool, sD["e_ps"], 4 * m - 4)
                nc.gpsimd.tensor_tensor(xlo[:, s % 2], xnT[:, s % 2], xhi[:, s % 2], ALU.subtract).then_inc(sD["lo"], 1)

            def body(i, u):
                n = 2 * i + u
                if live(i, u + 2):
                    split_tile(i, u + 2)
                if live(i, u):
                    wait(pool, sD["scaled"], n + 1)
                    wait(pool, sD["y_ready"], n - 1)
                    nc.gpsimd.tensor_tensor(part[:, u, 0], part[:, u, 0], part[:, u, 1], ALU.add).then_inc(sD["summed"], 1)

            split_tile(0, 0)
            pipeline(pool, body)

        @block.scalar
        def _(act):
            for g in range(2):
                for b in range(B):
                    act.dma_start(x[:, b, 4 * g:4 * g + 4, :], io["x"][b, 512 * g:512 * g + 512, :].rearrange("(j p) d -> p j d", p=P)).then_inc(x_in[g], 16)
            act.wait_ge(v_in, 48)
            for b in range(B):
                for c in range(2):
                    last = nc.scalar.activation(vbd[:, b, c, :, :, HD], vmask[:], ACT.Copy)
            last.then_inc(sA["ones_ready"], 1)
            act.wait_ge(q_in, 64)

            def evac_xT(i, s):
                m = 2 * i + s
                wait(act, sA["xT_ps"], m + 1)
                wait(act, sA["q_ps"], m - 1)
                nc.scalar.activation(xnT[:, s % 2], XT, ACT.Copy).then_inc(sA["xT_sb"], 1)

            def evac_q(i, s):
                m = 2 * i + s
                wait(act, sA["q_ps"], m + 1)
                wait(act, sA["s_ps"], 2 * m - 2)
                for c in range(2):
                    last = nc.scalar.activation(qT[:, s % 2, c, :], QT[:, c], ACT.Identity, bias=bq[:, c:c + 1])
                last.then_inc(sA["q_ready"], 1)

            evac_xT(0, 0)
            evac_q(0, 0)

            def body(i, u):
                n = 2 * i + u
                if isinstance(i, int) and n == 0:
                    act.wait_ge(sA["vbd_ready"], 5)

                def weights(c):
                    wait(act, sA["pta_ps"], 2 * n + c + 1)
                    wait(act, sA["o_ps"], n)
                    nc.scalar.activation(prT[:, c, 0:3, :], PTA, ACT.Copy).then_inc(sA["pta_ev"], 1)
                    wait(act, sA["ptb_ps"], 2 * n + c + 1)
                    nc.scalar.activation(prT[:, c, 3, :], PTB[:, 0], ACT.Copy)
                    nc.scalar.activation(prT[0:rows(4), c, 4, :], PTB[0:rows(4), 1], ACT.Copy).then_inc(sA["ptb_ev"], 1)

                def exponentials(c):
                    wait(act, sA["sub_done"], 2 * n + 3 + c)
                    nc.scalar.activation(pr[:, c], pr[:, c], ACT.Exp).then_inc(sA["exp_done"], 1)

                if live(i, u):
                    weights(0)
                if live(i, u - 1):
                    wait(act, sA["oT_ps"], n)
                    wait(act, sA["out_ps"], n - 1)
                    nc.scalar.activation(oT[:], OT, ACT.Copy).then_inc(sA["oT_sb"], 1)
                if live(i, u + 2):
                    evac_xT(i, u + 2)
                if live(i, u + 1):
                    exponentials(0)
                if live(i, u):
                    weights(1)
                if live(i, u + 1):
                    exponentials(1)
                if live(i, u + 2):
                    evac_q(i, u + 2)

            pipeline(act, body)

            def copies(ps_sem, k, dst, src, sb_sem, scale=1.0):
                act.wait_ge(ps_sem, k)
                nc.scalar.activation(dst, src, ACT.Copy, scale=scale).then_inc(sb_sem, 1)

            copies(sC["kvc_ps"], 1, kvcT, ps[0:DC, 7, 0:B * LK], sC["kvc_sb"])
            for g, (q0, nq) in enumerate(((0, 3), (3, 3), (6, 2))):
                copies(sC["kn_ps"], g + 1, knT[:, q0:q0 + nq].rearrange("p q b k -> p (q b k)"), ps[:, g, 0:nq * B * LK], sC["kn_sb"])
            copies(sC["kr_ps"], 1, kruv.rearrange("p v b k -> p (v b k)"), ps[:, 3, 0:2 * B * LK], sC["kr_sb"], scale=SCALE)
            def body(i):
                for r in range(RING):
                    n = RING * i + r
                    act.wait_ge(sB["xT_ps"], n + 1)
                    wait(act, sB["lg_ps"], n - 1)
                    nc.scalar.activation(xnT[:, r % 2], ps[:, r, 0:D].rearrange("p (k q) -> p k q", k=DK), ACT.Copy).then_inc(sB["xT_sb"], 1)

            body(0)
            with act.Fori(1, NT // RING) as i:
                body(i)
            for g in range(6):
                if g == 3:
                    act.wait_ge(sB["chain"], 3)
                    for b in range(B):
                        nc.scalar.activation(lg[:, b], lg[:, b], ACT.Exp, bias=gmax[:, b:b + 1], accum_out=gsum[:, b:b + 1]).then_inc(sB["gexp"], 1)
                q0, a = 3 * (g // 2), g % 2
                nh = min(3, NP2 - q0)
                copies(sC["a_ps"], g + 1, anope[:].rearrange("p b (q a) k -> p a q b k", a=2)[:, a, q0:q0 + nh],
                       ps[0:DQ, g % 2, 0:nh * B * LK].rearrange("p (h b k) -> p h b k", h=nh, b=B), sC["a_sb"], scale=SCALE)
            act.wait_ge(sC["zero"], 1)
            for b in range(B):
                if b:
                    act.wait_ge(sC["vw_ps"], NJ)
                act.wait_ge(sC["v_ps"], 3)
                for q in range(NP2):
                    for a in range(2):
                        r = slice(RD * a, RD * a + RD)
                        last = nc.scalar.activation(vbdT[r, q, P + LK * a:P + LK * a + LK], ps[r, VBANK[q // 3], (q % 3) * B * LK + b * LK:(q % 3) * B * LK + (b + 1) * LK], ACT.Copy)
                last.then_inc(sC["v_sb"], 1)
                for m in range(NJ):
                    act.wait_ge(sC["vw_ps"], NJ * b + m + 1)
                    for a in range(2):
                        c, j = (2 * m + a) // NJ, (2 * m + a) % NJ
                        last = nc.scalar.activation(vw[0:rows(j), b, c, j, :], ps[0:rows(j), m % 2, D * a:D * a + D], ACT.Copy)
                    last.then_inc(sC["vw_sb"], 1)
            act.wait_ge(sB["ind_ps"], 1)
            for g in range(4):
                last = nc.scalar.activation(indT[:, 4 * g:4 * g + 4, :], ps[0:E, g, :].rearrange("e (t q) -> e t q", q=P), ACT.Copy)
            last.then_inc(sB["ind_sb"], 1)

            def evac(it, k):
                l, s = k // NSTR, k % NSTR
                act.wait_ge(sB["tp_ps"], STEPS * it + k + 1)
                nc.scalar.activation(hT[:, s], ps[:, s, 0:D].rearrange("p (k q) -> p k q", k=DK),
                                     ACT.Relu if l else ACT.Copy).then_inc(sB["tp_sb"], 1)

            def outputs(it, s):
                act.wait_ge(sB["l_sb"], STEPS * it + STEPS - NSTR + s + 1)
                wait(act, sB["v_ps"], NSTR * (it - 1) + s + 1)
                nc.scalar.activation(y0[:, s], h0[:, s], ACT.Relu).then_inc(sB["y_ready"], 1)

            def chunks(it, first=False):
                for k in range(STEPS):
                    evac(it, k)
                    if k < NSTR - 1 and not first:
                        outputs(it - 1, k + 1)
                outputs(it, 0)

            chunks(0, first=True)
            chunks(1)
            with act.Fori(2, NIT) as it:
                chunks(it)
            for s in range(1, NSTR):
                outputs(NIT - 1, s)
            act.wait_ge(sB["v_tp"], 1)
            nc.scalar.activation(v0[:], ps[0:E, 5, 0:D], ACT.Copy).then_inc(sB["v_sb"], 1)

            def evac_xT(i, s):
                m = 2 * i + s
                wait(act, sC["xT_ps"], m + 1)
                nc.scalar.activation(xnT[:, s % 2], ps[:, 6, 0:D].rearrange("p (k q) -> p k q", k=DK), ACT.Copy).then_inc(sC["xT_sb"], 1)

            def evac_qc(i, s):
                m = 2 * i + s
                wait(act, sC["qc_ps"], m + 1)
                wait(act, sC["s_ps"], 2 * m - 2)
                nc.scalar.activation(qc[:, s % 2, :], ps[0:DQ, 6, D:D + P], ACT.Copy).then_inc(sC["qc_sb"], 1)

            evac_xT(0, 0)
            evac_qc(0, 0)

            def body(i, u):
                n = 2 * i + u

                def weights(c):
                    wait(act, sC["pta_ps"], 2 * n + c + 1)
                    wait(act, sC["out_ps"], n)
                    nc.scalar.activation(pcT[:, c, 0:3, :], PTA, ACT.Copy).then_inc(sC["pta_ev"], 1)
                    wait(act, sC["ptb_ps"], 2 * n + c + 1)
                    nc.scalar.activation(pcT[:, c, 3, :], PTB[:, 0], ACT.Copy)
                    nc.scalar.activation(pcT[0:rows(4), c, 4, :], PTB[0:rows(4), 1], ACT.Copy).then_inc(sC["ptb_ev"], 1)

                def exponentials(c):
                    wait(act, sC["sub_done"], 2 * n + 3 + c)
                    nc.scalar.activation(pc[:, c], pc[:, c], ACT.Exp).then_inc(sC["exp_done"], 1)

                if live(i, u):
                    weights(0)
                    weights(1)
                if live(i, u + 1):
                    exponentials(0)
                if live(i, u + 2):
                    evac_xT(i, u + 2)
                    evac_qc(i, u + 2)
                if live(i, u + 1):
                    exponentials(1)
                if isinstance(i, int) and n == 0:
                    act.wait_ge(sD["we_in"], 32)
                if live(i, u):
                    cols = bass.ds(2 * WCOLS * i + WCOLS * u, WCOLS)
                    nc.scalar.activation(we_hi[:, cols], we[:, cols], ACT.Copy).then_inc(sD["we_hi"], 1)

            pipeline(act, body)

            def evac_xT(i, s):
                m = 2 * i + s
                wait(act, sD["xT_ps"], m + 1)
                wait(act, sD["lg_ps"], m - 1)
                wait(act, sD["lo"], m - 1)
                nc.scalar.activation(xnT[:, s % 2], ps[:, 4, 0:D].rearrange("p (k q) -> p k q", k=DK), ACT.Copy).then_inc(sD["xT_sb"], 1)
                wait(act, sD["xT_sb"], m + 1)
                wait(act, sD["e_ps"], 4 * m - 4)
                nc.scalar.activation(xhi[:, s % 2], xnT[:, s % 2], ACT.Copy).then_inc(sD["hi"], 1)

            evac_xT(0, 0)

            def body(i, u):
                n = 2 * i + u
                if live(i, u + 1):
                    wait(act, sD["diff"], n + 2)
                    nc.scalar.activation(gd[:, 1 - u, 1:2], gd[:, 1 - u, 0:1], ACT.Exp).then_inc(sD["exp"], 1)
                if live(i, u + 2):
                    evac_xT(i, u + 2)
                if live(i, u):
                    wait(act, sD["e_ps"], 4 * n + 4)
                    wait(act, sD["y_ready"], n - 1)
                    for a in range(EA):
                        e = E - EA + a
                        last = nc.scalar.activation(part[:, u, a], ps[:, e // 2, D * (e % 2):D * (e % 2) + D], ACT.Copy, scale=gates[:, u, e:e + 1])
                    last.then_inc(sD["scaled"], 1)
                if live(i, u + 1):
                    wait(act, sD["gT_ps"], n + 2)
                    wait(act, sD["be_ps"], n)
                    nc.scalar.activation(gatesT[:, 1 - u, :], ps[0:E, 6, 0:P], ACT.Copy).then_inc(sD["gT_sb"], 1)

            pipeline(act, body)

        @block.vector
        def _(dve):
            dve.wait_ge(sA["ctxT_ps"], 1)
            nc.vector.tensor_copy(ctxT[:], ps[:, 6, 0:DK * B * LK].rearrange("p (k b q) -> p k b q", k=DK, b=B)).then_inc(sA["ctxT_sb"], 1)
            dve.wait_ge(sA["ctxT_sb"], 1)
            for k in range(DK):
                last = nc.vector.tensor_copy(ctx_rep[:, k], bcast(ctxT[:, k], 2, HC))
            last.then_inc(sA["rep_ready"], 1)
            def normalise(i, s):
                b, j = tile_at(i, s)
                n = 2 * i + s
                wait(dve, sA["xT_ps"], n - 1)
                jj = bass.ds(j, 1)
                nc.vector.tensor_scalar(xn[:, b], x[:, b, jj, :], mv[:, b, jj, 0:1], rstd[:, b, jj],
                                        ALU.subtract, ALU.mult).then_inc(sA["xn_ready"], 1)

            def keep_stats(i, s):
                b, j = tile_at(i, s)
                nc.vector.tensor_copy(st_all[:, b, bass.ds(j, 1), :].squeeze(1), stats[:, b]).then_inc(sA["stats_kept"], 1)

            def input_stats(g):
                dve.wait_ge(x_in[g], 32)
                for j in range(4 * g, 4 * g + 4):
                    for b in range(B):
                        last = nc.vector.bn_stats(st_all[:, b, j], x[:, b, j, :])
                last.then_inc(sA["stats"], 1)

            def add_value_bias(g):
                dve.wait_ge(sA["kv_ps"], g + 2)
                for q in range(4):
                    b, c, j = v_unit(4 * g + q)
                    last = nc.vector.tensor_tensor(VTMP[g][0:rows(j), q], ps[0:rows(j), g, P * q:P * q + P], bv[0:rows(j), P * c:P * c + P], ALU.add)
                last.then_inc(sA["kv_sb"], 1)

            input_stats(0)
            dve.wait_ge(k_in, 48)
            dve.wait_ge(sA["kv_ps"], 1)
            for c in range(2):
                last = nc.vector.tensor_scalar(kT[:, c], ps[:, 7, 2 * LK * c:2 * LK * (c + 1)].rearrange("p (b k) -> p b k", b=B),
                                               bk[:, c:c + 1], HD ** -0.5, ALU.add, ALU.mult)
            last.then_inc(sA["kv_sb"], 1)
            dve.wait_ge(sA["kv_sb"], 1)
            for c in range(2):
                for b in range(B):
                    last = nc.vector.tensor_tensor(kbd[:, b, c], bcast(kT[:, c, b], 1, HC), bcast(kmask[:], 2, LK), ALU.mult)
            last.then_inc(sA["kbd_ready"], 1)
            input_stats(1)
            dve.wait_ge(sA["stats"], 2)
            for j in range(TPB):
                for b in range(B):
                    last = nc.vector.bn_aggr(mv[:, b, j], st_all[:, b, j])
            last.then_inc(sA["aggr"], 1)
            dve.wait_ge(v_in, 48)
            add_value_bias(0)
            add_value_bias(1)
            dve.wait_ge(sA["rstd"], 2)
            normalise(0, 0)
            for g in range(2, 5):
                add_value_bias(g)
            dve.wait_ge(sA["vbd_ready"], 3)

            def body(i, u):
                n = 2 * i + u
                def maximum(c):
                    wait(dve, sA["s_ps"], 2 * n + 3 + c)
                    nc.vector.tensor_reduce(nmax[:, c], S_(c), AX.X, ALU.max).then_inc(sA["max_done"], 1)

                def subtract(c):
                    wait(dve, sA["max_done"], 2 * n + 3 + c)
                    wait(dve, sA["ptb_ps"], 2 * n + 1 + c)
                    nc.vector.tensor_tensor(pr[:, c].rearrange("p (a h) k -> p a h k", a=2), S_(c),
                                            bcast(nmax[:, c].rearrange("p (a h) -> p a h", a=2), 3, LK),
                                            ALU.subtract).then_inc(sA["sub_done"], 1)

                if live(i, u - 1):
                    wait(dve, sA["o_ps"], n)
                    wait(dve, sA["stats2"], n - 1)
                    nc.vector.reciprocal(rsum[:], O_[:, :, :, HD]).then_inc(sA["rsum_done"], 1)
                    wait(dve, sA["rsum_done"], n)
                    wait(dve, sA["oT_ps"], n - 1)
                    nc.vector.tensor_tensor(on[:], O_[:, :, :, 0:HD], bcast(rsum[:], 3, HD), ALU.mult).then_inc(sA["on_ready"], 1)
                if live(i, u - 2):
                    keep_stats(i, u - 2)
                if live(i, u + 2):
                    normalise(i, u + 2)
                if live(i, u + 1):
                    maximum(0)
                    subtract(0)
                    maximum(1)
                if live(i, u - 1):
                    b, j = tile_at(i, u - 1)
                    jj = bass.ds(j, 1)
                    wait(dve, sA["out_ps"], n)
                    wait(dve, sA["xo_ready"], n)
                    wait(dve, sA["x1_kept"], n - 1)
                    nc.vector.tensor_tensor(xs[:, b], x[:, b, jj, :].squeeze(1), OUT, ALU.add).then_inc(sA["x1_ready"], 1)
                if live(i, u + 1):
                    subtract(1)
                if live(i, u - 1):
                    wait(dve, sA["x1_ready"], n)
                    wait(dve, sA["stats_kept"], n - 2)
                    nc.vector.bn_stats(stats[:, b], xs[:, b]).then_inc(sA["stats2"], 1)
                    nc.vector.tensor_copy(x[:, b, jj, :].squeeze(1), xs[:, b]).then_inc(sA["x1_kept"], 1)

            pipeline(dve, body)

            dve.wait_ge(sA["stats2"], NT)
            keep_stats(TPB - 1, 1)
            dve.wait_ge(sA["stats_kept"], NT)
            for b in range(B):
                for j in range(TPB):
                    nc.vector.bn_aggr(mv[:, b, j], st_all[:, b, j]).then_inc(sA["aggr2"], 1)

            links = [0]

            def then(ins):
                links[0] += 1
                ins.then_inc(sB["chain"], 1)
                dve.wait_ge(sB["chain"], links[0])

            dve.wait_ge(c_w, 19 * 16)
            tmp = chhot[:].rearrange("p t c -> p (t c)")[:, 0:NT * LK].rearrange("p (t k) -> p t k", t=NT)
            then(nc.vector.tensor_copy(seg[:, 0], seg_i[:]))
            nc.vector.tensor_tensor(negm[:], bcast(iok[:], 1, NT), bcast(seg[:, 0], 2, LK), ALU.is_gt)
            then(nc.vector.tensor_scalar(seg[:, 1], seg[:, 0], 2.0, None, ALU.subtract))

            def normalise2(i, r):
                n = RING * i + r
                u, j = r % 2, (RING // 2) * i + r // 2
                jj = bass.ds(j, 1)
                wait(dve, sB["xT_ps"], n - RING + 1)
                wait(dve, stored[r], 16 * i)
                nc.vector.tensor_scalar(xng[:, r], x[:, u, jj, :], mv[:, u, jj, 0:1], rstd[:, u, jj],
                                        ALU.subtract, ALU.mult).then_inc(sB["xn_ready"], 1)

            def logits(i, r):
                n = RING * i + r
                u, j = r % 2, (RING // 2) * i + r // 2
                wait(dve, sB["lg_ps"], n + 1)
                nc.vector.tensor_scalar(lg[:, u, bass.ds(P * j, P)], ps[0:E, 4 + u, 0:P], gb[:, 0:1], None, ALU.add).then_inc(sB["lg_sb"], 1)

            dve.wait_ge(g_in, 32)
            dve.wait_ge(sB["rstd"], 2)
            for r in range(RING):
                normalise2(0, r)
            with dve.Fori(1, NT // RING) as i:
                for r in range(RING):
                    logits(i - 1, r)
                    normalise2(i, r)
            for r in range(RING):
                logits(NT // RING - 1, r)
            dve.wait_ge(sB["lg_sb"], NT)
            then(nc.vector.tensor_reduce(gmax[:], lg[:], AX.X, ALU.max, negate=True))
            then(nc.vector.tensor_tensor(tmp, bcast(iok[:], 1, NT), bcast(seg[:, 1], 2, LK), ALU.is_lt))
            dve.wait_ge(sB["gexp"], 2)
            then(nc.vector.reciprocal(gsum[:], gsum[:]))
            for b in range(B):
                last = nc.vector.tensor_scalar(lg[:, b], lg[:, b], gsum[:, b:b + 1], None, ALU.mult)
            then(last)
            dve.wait_ge(sB["const"], 96)
            dve.wait_ge(sB["pT_ps"], 1)
            then(nc.vector.tensor_copy(prob[:], ps[:, 4, 0:NT * E].rearrange("p (t e) -> p t e", e=E)))
            src = prob
            for k in range(TOP):
                then(nc.vector.tensor_reduce(top[:, k], src[:], AX.X, ALU.max))
                then(nc.vector.tensor_tensor(key[:], src[:], bcast(top[:, k], 2, E), ALU.is_equal))
                then(nc.vector.tensor_tensor(key[:], key[:], bcast(rev8[:], 1, NT), ALU.mult))
                then(nc.vector.tensor_reduce(kmax[:], key[:], AX.X, ALU.max))
                then(nc.vector.tensor_tensor(oneh[:, k], bcast(rev8[:], 1, NT), bcast(kmax[:], 2, E), ALU.is_equal))
                if k == 0:
                    then(nc.vector.scalar_tensor_tensor(prob2[:], oneh[:, 0], -2.0, prob[:], ALU.mult, ALU.add))
                    src = prob2
            nc.vector.tensor_tensor(sel[:], oneh[:, 0], oneh[:, 1], ALU.add).then_inc(sB["route_ready"], 1)
            then(nc.vector.tensor_tensor(negm[:], negm[:], tmp, ALU.add))
            nc.vector.tensor_scalar(negm[:], negm[:], FMIN, None, ALU.mult)
            dve.wait_ge(sB["rank_ps"], 1)
            rank = ps[:, 5, 0:(NT + 1) * E].rearrange("p (t e) -> p t e", e=E)
            then(nc.vector.tensor_copy(base[:], rank[:, NT, :]))
            then(nc.vector.tensor_scalar(cmp16[:, 0], iot[:, 0:NT], float(P), None, ALU.mult))
            then(nc.vector.tensor_copy(kmax[:], cmp16[:, 0]))
            then(nc.vector.tensor_tensor(cmp16[:], bcast(base[:], 2, NT), bcast(kmax[:], 1, E), ALU.is_gt))
            then(nc.vector.tensor_reduce(nch[:], cmp16[:], AX.X, ALU.add))
            then(nc.vector.tensor_tensor(tri8[:], tri8[:], bcast(nch[:], 1, E), ALU.mult))
            then(nc.vector.tensor_reduce(cend[:], tri8[:], AX.X, ALU.add))
            then(nc.vector.tensor_tensor(base[:], cend[:], nch[:], ALU.subtract))
            then(nc.vector.tensor_scalar(base[:], base[:], float(P), None, ALU.mult))
            then(nc.vector.tensor_tensor(pos[:], rank[:, 0:NT, :], bcast(base[:], 1, NT), ALU.add))
            for k in range(TOP):
                then(nc.vector.tensor_tensor(key[:], oneh[:, k], pos[:], ALU.mult))
                then(nc.vector.tensor_reduce(slot[:, NT * k:NT * k + NT], key[:], AX.X, ALU.add))
            then(nc.vector.tensor_copy(slot_i[:, 0], slot[:]))
            nc.vector.tensor_scalar(slot_i[:, 1], slot_i[:, 0], P - 1, None, ALU.bitwise_and)
            then(nc.vector.tensor_scalar(slot_i[:, 2], slot_i[:, 0], P.bit_length() - 1, None, ALU.logical_shift_right))
            then(nc.vector.tensor_copy(rc[:], slot_i[:, 1:3]))
            then(nc.vector.tensor_tensor(chhot[:], bcast(rc[:, 1], 2, NCH), bcast(iot[:, 0:NCH], 1, TOP * NT), ALU.is_equal))
            hot = chhot[:].rearrange("p (k t) c -> p k t c", k=TOP)
            pay = payload[:].rearrange("p (k t) v c -> p k t v c", k=TOP)
            for r in range(RING):
                dve.wait_ge(stored[r], 16 * NT // RING)
            for k in range(TOP):
                nc.vector.tensor_tensor(pay[:, k, :, 0, :], hot[:, k], bcast(tokid[:], 2, NCH), ALU.mult)
                nc.vector.tensor_tensor(pay[:, k, :, 1, :], hot[:, k], bcast(top[:, k], 2, NCH), ALU.mult).then_inc(sB["payload"], 1)
            for g in range(4):
                a = slice(8 * g, 8 * g + 8)
                if g >= 2:
                    dve.wait_ge(sB["rowhot_used"], g - 1)
                nc.vector.tensor_tensor(rowhot[:, g % 2], bcast(rc[:, 0, a], 2, P), bcast(iot[:], 1, 8), ALU.is_equal).then_inc(sB["rowhot"], 1)
            then(nc.vector.tensor_tensor(cmp8[:], bcast(iot[:, 0:NCH], 2, E), bcast(cend[:], 1, NCH), ALU.is_ge))
            then(nc.vector.tensor_reduce(ce[:], cmp8[:], AX.X, ALU.add))
            then(nc.vector.tensor_scalar(ce[:], ce[:], float(E - 1), None, ALU.min))
            then(nc.vector.tensor_copy(ce_i[:], ce[:]))
            then(nc.vector.tensor_tensor(cmp8[:], bcast(ce[:], 2, E), bcast(iot[:, 0:E], 1, NCH), ALU.is_equal))
            dve.wait_ge(sB["rowhot_used"], 4)
            nc.vector.tensor_copy(tok_i[:], ps[:, 6, 0:NCH]).then_inc(sB["tok_ready"], 1)
            then(nc.vector.tensor_copy(wslot[:], ps[:, 6, NCH:2 * NCH]))
            nc.vector.tensor_tensor(wexp[:], cmp8[:], bcast(wslot[:], 2, E), ALU.mult).then_inc(sB["route_ready"], 1)
            dve.wait_ge(w0_in, 144)

            def expert_of(it, s):
                return nc.vector.value_load(ce_i[0:1, bass.ds(NSTR * it + s, 1)], min_val=0, max_val=E - 1)

            def add_bias(it, k, e):
                l, s = k // NSTR, k % NSTR
                dve.wait_ge(sB["l_ps"], STEPS * it + k + 1)
                if l == 0:
                    wait(dve, sB["y_ready"], NSTR * (it - 1) + s + 1)
                nc.vector.tensor_tensor(h0[:, s], ps[:, s, D:2 * D], b0[:, bass.ds(e, 1), l, :].squeeze(1), ALU.add).then_inc(sB["l_sb"], 1)

            def chunks(it):
                e = []
                for k in range(STEPS):
                    if k < NSTR:
                        e.append(expert_of(it, k))
                    add_bias(it, k, e[k % NSTR])

            chunks(0)
            with dve.Fori(1, NIT) as it:
                chunks(it)
            dve.wait_ge(sB["v_ps"], NCH)
            nc.vector.tensor_copy(vT[:], ps[:, 3:5, 0:E]).then_inc(sB["vT_sb"], 1)
            for m in range(NT // 2):
                b, j = 2 * m // TPB, 2 * m % TPB
                dve.wait_ge(sB["o_ps"], m + 1)
                nc.vector.tensor_tensor(x[:, b, j:j + 2, :], x[:, b, j:j + 2, :], ps[:, m % 4, :].rearrange("p (t d) -> p t d", t=2), ALU.add).then_inc(sB["x2_ready"], 1)
                dve.wait_ge(sB["x2_ready"], m + 1)
                for q in range(2):
                    last = nc.vector.bn_stats(stats[:, q], x[:, b, j + q, :])
                last.then_inc(sB["stats"], 1)
                dve.wait_ge(sB["stats"], m + 1)
                for q in range(2):
                    last = nc.vector.bn_aggr(mv[:, b, j + q], stats[:, q])
                last.then_inc(sB["aggr"], 1)

            def normalise3(i, s):
                n = 2 * i + s
                b, j = tile_at(i, s)
                jj = bass.ds(j, 1)
                wait(dve, sC["xT_ps"], n - 1)
                nc.vector.tensor_scalar(xn[:, b], x[:, b, jj, :], mv[:, b, jj, 0:1], rstd[:, b, jj],
                                        ALU.subtract, ALU.mult).then_inc(sC["xn_ready"], 1)

            dve.wait_ge(sC["rstd"], 2)
            normalise3(0, 0)

            def body(i, u):
                n = 2 * i + u

                def rotate(g):
                    b, j = tile_at(i, u + 1)
                    wait(dve, sC["rope_ps"], 4 * (n + 1) + g + 1)
                    wait(dve, sC["s_ps"], 2 * n + 1 + g // 2)
                    nc.vector.tensor_tensor(rot[:, g], ps[:, 6, :].rearrange("p (h q) -> p h q", h=4),
                                            bcast(trig[:, bass.ds(P * j, P)], 1, 4), ALU.mult).then_inc(sC["rot_ready"], 1)

                def mask(c):
                    b, j = tile_at(i, u + 1)
                    m = 2 * (n + 1) + c + 1
                    wait(dve, sC["s_ps"], m)
                    wait(dve, sC["ptb_ps"], m - 2)
                    nc.vector.tensor_tensor(pc[:, c].rearrange("p (a h) k -> p a h k", a=2), S_(c),
                                            negm[:, bass.ds(TPB * b + j, 1), :].unsqueeze(1).broadcast_to([P, 2, 4, LK]),
                                            ALU.add).then_inc(sC["mask_done"], 1)
                    wait(dve, sC["mask_done"], m)
                    nc.vector.tensor_reduce(pmax[:, c], pc[:, c], AX.X, ALU.max).then_inc(sC["max_done"], 1)

                def total(m, c):
                    k = 2 * m + c + 1
                    wait(dve, sC["exp_done"], k)
                    wait(dve, sC["norm_done"], k - 2)
                    nc.vector.tensor_reduce(psm[:, c], pc[:, c], AX.X, ALU.add).then_inc(sC["sum_done"], 1)
                    wait(dve, sC["sum_done"], k)
                    nc.vector.reciprocal(psm[:, c], psm[:, c]).then_inc(sC["rsum_done"], 1)

                if live(i, u + 1):
                    rotate(0)
                if live(i, u + 2):
                    normalise3(i, u + 2)
                if live(i, u + 1):
                    rotate(1)
                    rotate(2)
                    mask(0)
                    rotate(3)
                    total(n + 1, 0)
                    mask(1)
                if live(i, u - 1):
                    bb, j = tile_at(i, u - 1)
                    jb = bass.ds(j, 1)
                    wait(dve, sC["x_ready"], n)
                    wait(dve, sC["stats_kept"], n - 2)
                    nc.vector.bn_stats(stats[:, bb], xs[:, bb]).then_inc(sC["stats"], 1)
                    nc.vector.tensor_copy(x[:, bb, jb, :].squeeze(1), xs[:, bb]).then_inc(sC["x_kept"], 1)
                if live(i, u + 1):
                    total(n + 1, 1)
                if live(i, u):
                    b, j = tile_at(i, u)
                    jj = bass.ds(j, 1)
                    wait(dve, sC["out_ps"], n + 1)
                    wait(dve, sC["x_kept"], n - 1)
                    wait(dve, sC["stats"], n)
                    nc.vector.tensor_tensor(xs[:, b], x[:, b, jj, :].squeeze(1), ps[:, 7, 0:D], ALU.add).then_inc(sC["x_ready"], 1)
                if live(i, u - 1):
                    if not live(i, u):
                        wait(dve, sC["stats"], n)
                    nc.vector.tensor_copy(st_all[:, bb, jb, :].squeeze(1), stats[:, bb]).then_inc(sC["stats_kept"], 1)

            pipeline(dve, body)
            dve.wait_ge(sC["stats_kept"], NT)
            for b in range(B):
                for j in range(TPB):
                    nc.vector.bn_aggr(mv[:, b, j], st_all[:, b, j]).then_inc(sD["aggr"], 1)

            def normalise4(i, s):
                n = 2 * i + s
                b, j = tile_at(i, s)
                jj = bass.ds(j, 1)
                wait(dve, sD["xT_ps"], n - 1)
                nc.vector.tensor_scalar(xn[:, b], x[:, b, jj, :], mv[:, b, jj, 0:1], rstd[:, b, jj],
                                        ALU.subtract, ALU.mult).then_inc(sD["xn_ready"], 1)

            dve.wait_ge(sD["rstd"], 2)
            dve.wait_ge(sD["w_in"], 48)
            normalise4(0, 0)
            def body(i, u):
                n = 2 * i + u
                v = 1 - u
                step = [0]

                def link(ins):
                    step[0] += 1
                    ins.then_inc(sD["chain"], 1)

                def linked():
                    wait(dve, sD["chain"], LINKS * (n + 1) + step[0])

                def weigh(e):
                    if live(i, u):
                        if e % 2 == 0:
                            wait(dve, sD["e_ps"], 4 * n + e // 2 + 1)
                        wait(dve, sD["acc"], ACCS * n + e + 1)
                        nc.vector.scalar_tensor_tensor(acc[:, u], ps[:, e // 2, D * (e % 2):D * (e % 2) + D], gates[:, u, e:e + 1], acc[:, u],
                                                       ALU.mult, ALU.add).then_inc(sD["acc"], 1)

                ahead = live(i, u + 1)
                if ahead:
                    wait(dve, sD["lg_ps"], n + 2)
                    link(nc.vector.tensor_copy(lt[:, v], ps[:, 5, 0:E]))
                if live(i, u + 2):
                    if ahead:
                        linked()
                    normalise4(i, u + 2)
                elif ahead:
                    linked()
                if ahead:
                    link(nc.vector.max(lmax[:, v], lt[:, v]))
                    linked()
                    nc.vector.tensor_tensor(gd[:, v, 0:1], lmax[:, v, 1:2], lmax[:, v, 0:1], ALU.subtract).then_inc(sD["diff"], 1)
                    link(nc.vector.max_index(lidx[:, v], lmax[:, v], lt[:, v]))
                if live(i, u):
                    b, j = tile_at(i, u)
                    jj = bass.ds(j, 1)
                    wait(dve, sD["be_ps"], n + 1)
                    nc.vector.tensor_tensor(acc[:, u], x[:, b, jj, :].squeeze(1), ps[:, 7, 0:D], ALU.add).then_inc(sD["acc"], 1)
                if ahead:
                    linked()
                    link(nc.vector.tensor_copy(lidf[:, v], lidx[:, v, 0:TOP]))
                weigh(0)
                if ahead:
                    wait(dve, sD["exp"], n + 2)
                    nc.vector.tensor_scalar(gt[:, v, 0:1], gd[:, v, 1:2], 1.0, None, ALU.add).then_inc(sD["chain2"], 1)
                    linked()
                    link(nc.vector.tensor_tensor(goh[:, v], bcast(iot8[:], 1, TOP), bcast(lidf[:, v], 2, E), ALU.is_equal))
                    wait(dve, sD["chain2"], 2 * (n + 1) + 1)
                    nc.vector.reciprocal(gt[:, v, 0:1], gt[:, v, 0:1]).then_inc(sD["chain2"], 1)
                weigh(1)
                if live(i, u - 1):
                    wait(dve, sD["summed"], n)
                    wait(dve, sD["acc"], ACCS * n)
                    wait(dve, written[v], (16 * i - 16) if u == 0 else 16 * i)
                    nc.vector.tensor_tensor(y[:, v], acc[:, v], part[:, v, 0], ALU.add).then_inc(sD["y_ready"], 1)
                if ahead:
                    wait(dve, sD["chain2"], 2 * (n + 1) + 2)
                    link(nc.vector.tensor_tensor(gt[:, v, 1:2], gt[:, v, 0:1], gd[:, v, 1:2], ALU.mult))
                weigh(2)
                if ahead:
                    linked()
                    link(nc.vector.tensor_tensor(goh[:, v], goh[:, v], bcast(gt[:, v], 2, E), ALU.mult))
                weigh(3)
                if ahead:
                    linked()
                    wait(dve, sD["gT_ps"], n)
                    wait(dve, sD["scaled"], n)
                    link(nc.vector.tensor_tensor(gates[:, v], goh[:, v, 0], goh[:, v, 1], ALU.add))
                weigh(4)
                weigh(5)
                if isinstance(i, int) and ahead:
                    assert step[0] == LINKS
                if ahead:
                    linked()

            pipeline(dve, body)

        @block.tensor
        def _(pe):
            pe.wait_ge(c_in, 32)
            for k in range(DK):
                for b in range(B):
                    last = nc.tensor.transpose(ps[:, 6, (2 * k + b) * LK:(2 * k + b + 1) * LK], ctx[:, b, P * k:P * k + P], ident[0:LK, 0:LK])
            last.then_inc(sA["ctxT_ps"], 1)
            pe.wait_ge(sA["ctxT_sb"], 1)
            pe.wait_ge(k_in, 48)
            for c in range(2):
                for k in range(DK):
                    last = nc.tensor.matmul(ps[:, 7, 2 * LK * c:2 * LK * (c + 1)], wk[:, k, P * c:P * c + P], ctxT[:, k],
                                            start=k == 0, stop=k == DK - 1)
            last.then_inc(sA["kv_ps"], 1)
            pe.wait_ge(sA["rep_ready"], 1)
            pe.wait_ge(v_in, 48)
            for g in range(5):
                for q in range(4):
                    b, c, j = v_unit(4 * g + q)
                    for k in range(DK):
                        last = nc.tensor.matmul(ps[0:rows(j), g, P * q:P * q + P],
                                                ctx_rep[:, k, b].rearrange("p h k -> p (h k)")[:, P * j:P * j + rows(j)],
                                                wv[:, k, P * c:P * c + P], start=k == 0, stop=k == DK - 1)
                last.then_inc(sA["kv_ps"], 1)
            pe.wait_ge(q_in, 64)

            def transpose_tile(i, s):
                m = 2 * i + s
                wait(pe, sA["xn_ready"], m + 1)
                wait(pe, sA["oT_sb"], m - 2)
                wait(pe, sA["q_ready"], m)
                for k in range(DK):
                    last = nc.tensor.transpose(XT[:, k], xn[:, s % 2, P * k:P * k + P], ident[:])
                last.then_inc(sA["xT_ps"], 1)

            def queries(i, s):
                wait(pe, sA["xT_sb"], 2 * i + s + 1)
                for c in range(2):
                    for k in range(DK):
                        last = nc.tensor.matmul(QT[:, c], wq[:, k, P * c:P * c + P], xnT[:, s % 2, k, :], start=k == 0, stop=k == DK - 1)
                last.then_inc(sA["q_ps"], 1)

            transpose_tile(0, 0)
            queries(0, 0)
            pe.wait_ge(sA["kbd_ready"], 1)
            pe.wait_ge(sA["kv_sb"], 6)

            def body(i, u):
                n = 2 * i + u

                def transpose_weights(c):
                    flat = pr[:, c].rearrange("p h k -> p (h k)")
                    wait(pe, sA["exp_done"], 2 * n + c + 1)
                    wait(pe, sA["pta_ev"], 2 * n + c)
                    for j in range(3):
                        last = nc.tensor.transpose(PTA[:, j], flat[:, P * j:P * j + P], ident[:])
                    last.then_inc(sA["pta_ps"], 1)
                    wait(pe, sA["ptb_ev"], 2 * n + c)
                    nc.tensor.transpose(PTB[:, 0], flat[:, 3 * P:4 * P], ident[:])
                    nc.tensor.transpose(PTB[0:rows(4), 1], flat[:, 4 * P:UK], ident[:]).then_inc(sA["ptb_ps"], 1)

                def apply_weights(c):
                    wait(pe, sA["ptb_ev"], 2 * n + c + 1)
                    for j in range(NJ):
                        h0, nh = heads_of(j)
                        last = nc.tensor.matmul(O_[:, c, h0:h0 + nh, :].rearrange("p h v -> p (h v)"), prT[0:rows(j), c, j, :],
                                                vbd[0:rows(j), u, c, j, h0:h0 + nh, :].rearrange("p h v -> p (h v)"),
                                                start=j == 0 and c == 0, stop=j == NJ - 1, skip_group_check=True)
                    return last

                def scores(c):
                    wait(pe, sA["sub_done"], 2 * n + c + 1)
                    for a in range(2):
                        last = nc.tensor.matmul(ps[:, 2 * c + a, 0:4 * LK], qT[:, 1 - u, c, :],
                                                kbd[:, 1 - u, c, 4 * a:4 * a + 4, :].rearrange("p h k -> p (h k)"), start=True, stop=True)
                    last.then_inc(sA["s_ps"], 1)

                if live(i, u + 1):
                    wait(pe, sA["q_ready"], n + 2)
                    scores(0)
                if live(i, u):
                    transpose_weights(0)
                if live(i, u - 1):
                    wait(pe, sA["on_ready"], n)
                    for c in range(2):
                        last = nc.tensor.transpose(OT[:, c], on[:, c].rearrange("p h d -> p (h d)"), ident[:])
                    last.then_inc(sA["oT_ps"], 1)
                if live(i, u + 1):
                    scores(1)
                if live(i, u + 2):
                    transpose_tile(i, u + 2)
                if live(i, u - 1):
                    wait(pe, sA["oT_sb"], n)
                    for c in range(2):
                        last = nc.tensor.matmul(OUT, oT[:, c, :], wo[:, c, :], start=c == 0, stop=c == 1)
                    last.then_inc(sA["out_ps"], 1)
                if live(i, u):
                    transpose_weights(1)
                if live(i, u + 2):
                    queries(i, u + 2)
                if isinstance(i, int) and n == 0:
                    pe.wait_ge(sA["vbd_ready"], 5)
                    pe.wait_ge(sA["ones_ready"], 1)
                if live(i, u):
                    wait(pe, sA["x1_ready"], n)
                    apply_weights(0)
                    apply_weights(1).then_inc(sA["o_ps"], 1)

            pipeline(pe, body)

            pe.wait_ge(sA["x1_ready"], NT)
            pe.wait_ge(c_w, 19 * 16)
            for k in range(DK):
                last = nc.tensor.matmul(ps[0:DC, 7, 0:B * LK], wkvc[:, k, :], ctxT[:, k], start=k == 0, stop=k == DK - 1)
            last.then_inc(sC["kvc_ps"], 1)
            pe.wait_ge(sC["kvc_sb"], 1)
            for q in range(NP2):
                last = nc.tensor.matmul(ps[:, q // 3, (q % 3) * B * LK:(q % 3 + 1) * B * LK], wkup[:, P * q:P * q + P], kvcT, start=True, stop=True)
                if q % 3 == 2 or q == NP2 - 1:
                    last.then_inc(sC["kn_ps"], 1)
            for v in range(2):
                last = nc.tensor.matmul(ps[:, 3, v * B * LK:(v + 1) * B * LK], wkr[:, v, :], kvcT, start=True, stop=True)
            last.then_inc(sC["kr_ps"], 1)
            pe.wait_ge(g_in, 32)
            pe.wait_ge(sC["kn_sb"], 3)
            pe.wait_ge(sC["kr_sb"], 1)

            def transpose_tile(i, r):
                n = RING * i + r
                wait(pe, sB["xn_ready"], n + 1)
                wait(pe, sB["xT_sb"], n - RING + 1)
                for k in range(DK):
                    last = nc.tensor.transpose(ps[:, r, P * k:P * k + P], xng[:, r, P * k:P * k + P], ident[:])
                last.then_inc(sB["xT_ps"], 1)

            def gate(i, r):
                n = RING * i + r
                wait(pe, sB["xT_sb"], n + 1)
                wait(pe, sB["lg_sb"], n - 1)
                for k in range(DK):
                    last = nc.tensor.matmul(ps[0:E, 4 + r % 2, 0:P], gw[:, k, :], xnT[:, r % 2, k, :], start=k == 0, stop=k == DK - 1)
                last.then_inc(sB["lg_ps"], 1)

            AHEAD = RING - 2
            for r in range(AHEAD):
                transpose_tile(0, r)

            def body(i, live_next=True):
                for r in range(RING):
                    if r + AHEAD < RING:
                        transpose_tile(i, r + AHEAD)
                    elif live_next:
                        transpose_tile(i + 1, r + AHEAD - RING)
                    gate(i, r)

            body(0)
            with pe.Fori(1, NT // RING - 1) as i:
                body(i)
            body(NT // RING - 1, live_next=False)
            for g in range(6):
                if g >= 2:
                    pe.wait_ge(sC["a_sb"], g - 1)
                r = slice(RD * (g % 2), RD * (g % 2) + RD)
                for q in range(3 * (g // 2), min(3 * (g // 2) + 3, NP2)):
                    last = nc.tensor.matmul(ps[0:DQ, g % 2, (q % 3) * B * LK:(q % 3 + 1) * B * LK], wqupT[r, q, :],
                                            knT[r, q].rearrange("p b k -> p (b k)"), start=True, stop=True)
                last.then_inc(sC["a_ps"], 1)
            pe.wait_ge(sB["chain"], 6)
            for t in range(NT):
                b, j = t // TPB, t % TPB
                last = nc.tensor.transpose(ps[:, 4, E * t:E * t + E], lg[:, b, P * j:P * j + P], ident[0:E, 0:E])
            last.then_inc(sB["pT_ps"], 1)
            for q in range(NP2):
                last = nc.tensor.matmul(ps[:, VBANK[q // 3], (q % 3) * B * LK:(q % 3 + 1) * B * LK], wvup[:, P * q:P * q + P], kvcT, start=True, stop=True)
                if q % 3 == 2 or q == NP2 - 1:
                    last.then_inc(sC["v_ps"], 1)
            pe.wait_ge(sB["route_ready"], 1)
            pe.wait_ge(sB["const"], 96)
            flat = sel[:].rearrange("p t e -> p (t e)")
            nc.tensor.matmul(ps[:, 5, 0:NT * E], tri[:], flat, start=True, stop=False, skip_group_check=True)
            for t in range(NT):
                last = nc.tensor.matmul(ps[:, 5, E * (t + 1):E * (NT + 1)].rearrange("p (a e) -> p a e", e=E), ones[:],
                                        bcast(sel[:, t], 1, NT - t), start=False, stop=t == NT - 1, skip_group_check=True)
            last.then_inc(sB["rank_ps"], 1)

            def output_values(b):
                pe.wait_ge(sC["v_sb"], b + 1)
                for m in range(NJ):
                    if b == 0 and m < 2:
                        pe.wait_ge(sC["a_sb"], 6)
                    wait(pe, sC["vw_sb"], NJ * b + m - 1)
                    for a in range(2):
                        c, j = (2 * m + a) // NJ, (2 * m + a) % NJ
                        pairs = [q for q in range(4) if -rows(j) < P * j - 2 * LK * q < 2 * LK]
                        for q in pairs:
                            w0_ = P + P * j - 2 * LK * q
                            last = nc.tensor.matmul(ps[0:rows(j), m % 2, D * a:D * a + D], vbdT[:, 4 * c + q, w0_:w0_ + rows(j)],
                                                    wout[:, 4 * c + q, :], start=q == pairs[0], stop=q == pairs[-1])
                    last.then_inc(sC["vw_ps"], 1)

            def route(g):
                pe.wait_ge(sB["payload"], 2)
                pe.wait_ge(sB["rowhot"], g + 1)
                for q in range(8 * g, 8 * g + 8):
                    last = nc.tensor.matmul(ps[:, 6, 0:2 * NCH], rowhot[:, g % 2, q % 8], payload[:, q].rearrange("p v c -> p (v c)"),
                                            start=q == 0, stop=q == TOP * NT - 1)
                last.then_inc(sB["rowhot_used"], 1)

            output_values(0)
            route(0)
            output_values(1)
            for g in range(1, 4):
                route(g)
            pe.wait_ge(sC["vw_sb"], 2 * NJ)
            for t in range(NT):
                last = nc.tensor.transpose(ps[0:E, t // 4, P * (t % 4):P * (t % 4) + P], sel[:, t, :], ident[:])
            last.then_inc(sB["ind_ps"], 1)
            pe.wait_ge(sB["route_ready"], 2)
            pe.wait_ge(sB["ind_sb"], 1)
            pe.wait_ge(w0_in, 144)

            def values(it, s):
                pe.wait_ge(sB["y_ready"], NSTR * it + s + 1)
                first = isinstance(it, int) and it == 0 and s == 0
                final = isinstance(it, int) and it == NIT - 1 and s == NSTR - 1
                for m in range(DK):
                    last = nc.tensor.matmul(ps[:, 3 + m, 0:E], y0[:, s, P * m:P * m + P], wexp[:, bass.ds(NSTR * it + s, 1), :].squeeze(1),
                                            start=first, stop=final)
                last.then_inc(sB["v_ps"], 1)

            def expert_of(it, s):
                return nc.tensor.value_load(ce_i[0:1, bass.ds(NSTR * it + s, 1)], min_val=0, max_val=E - 1)

            def transpose_step(it, k):
                s = k % NSTR
                if k < NSTR:
                    pe.wait_ge(gathered[s], 16 * (it + 1))
                    wait(pe, sB["l_sb"], STEPS * (it - 1) + STEPS - NSTR + s + 1)
                else:
                    pe.wait_ge(sB["l_sb"], STEPS * it + k - NSTR + 1)
                src = g0 if k < NSTR else h0
                for m in range(DK):
                    last = nc.tensor.transpose(ps[:, s, P * m:P * m + P], src[:, s, P * m:P * m + P], ident[:])
                last.then_inc(sB["tp_ps"], 1)

            def layer_step(it, k, e):
                l, s = k // NSTR, k % NSTR
                pe.wait_ge(sB["tp_sb"], STEPS * it + k + 1)
                for m in range(DK):
                    last = nc.tensor.matmul(ps[:, s, D:2 * D], hT[:, s, m, :], w0[:, bass.ds(e, 1), l, m, :].squeeze(1),
                                            start=m == 0, stop=m == DK - 1)
                last.then_inc(sB["l_ps"], 1)

            def chunks(it, first=False):
                transpose_step(it, 0)
                e = [expert_of(it, 0)]
                for k in range(1, STEPS):
                    transpose_step(it, k)
                    if k < NSTR:
                        e.append(expert_of(it, k))
                    layer_step(it, k - 1, e[(k - 1) % NSTR])
                if not first:
                    for s in range(NSTR):
                        values(it - 1, s)
                layer_step(it, STEPS - 1, e[NSTR - 1])

            chunks(0, first=True)
            chunks(1)
            with pe.Fori(2, NIT) as it:
                chunks(it)
            for s in range(NSTR):
                values(NIT - 1, s)
            pe.wait_ge(sB["vT_sb"], 1)
            for m in range(DK):
                last = nc.tensor.transpose(ps[0:E, 5, P * m:P * m + P], vT[:, m, :], ident[:])
            last.then_inc(sB["v_tp"], 1)
            pe.wait_ge(sB["v_sb"], 1)
            for m in range(NT // 2):
                if m >= 4:
                    pe.wait_ge(sB["x2_ready"], m - 3)
                for q in range(2):
                    last = nc.tensor.matmul(ps[:, m % 4, D * q:D * q + D], indT[:, 2 * m + q, :], v0[:], start=True, stop=True)
                last.then_inc(sB["o_ps"], 1)
            pe.wait_ge(sB["x2_ready"], NT // 2)

            def transpose_tile(i, s):
                m = 2 * i + s
                wait(pe, sC["xn_ready"], m + 1)
                wait(pe, sC["rot_ready"], 4 * m)
                for k in range(DK):
                    last = nc.tensor.transpose(ps[:, 6, P * k:P * k + P], xn[:, s % 2, P * k:P * k + P], ident[:])
                last.then_inc(sC["xT_ps"], 1)

            def latents(i, s):
                wait(pe, sC["xT_sb"], 2 * i + s + 1)
                for k in range(DK):
                    last = nc.tensor.matmul(ps[0:DQ, 6, D:D + P], wqd[:, k, :], xnT[:, s % 2, k, :], start=k == 0, stop=k == DK - 1)
                last.then_inc(sC["qc_ps"], 1)

            transpose_tile(0, 0)
            latents(0, 0)

            def body(i, u):
                n = 2 * i + u
                v = 1 - u

                def transpose_weights(c):
                    flat = pc[:, c].rearrange("p h k -> p (h k)")
                    wait(pe, sC["norm_done"], 2 * n + c + 1)
                    wait(pe, sC["pta_ev"], 2 * n + c)
                    for j in range(3):
                        last = nc.tensor.transpose(PTA[:, j], flat[:, P * j:P * j + P], ident[:])
                    last.then_inc(sC["pta_ps"], 1)
                    wait(pe, sC["ptb_ev"], 2 * n + c)
                    nc.tensor.transpose(PTB[:, 0], flat[:, 3 * P:4 * P], ident[:])
                    nc.tensor.transpose(PTB[0:rows(4), 1], flat[:, 4 * P:UK], ident[:]).then_inc(sC["ptb_ps"], 1)

                def apply_weights(c):
                    wait(pe, sC["ptb_ev"], 2 * n + c + 1)
                    for j in range(NJ):
                        last = nc.tensor.matmul(ps[:, 7, 0:D], pcT[0:rows(j), c, j, :], vw[0:rows(j), u, c, j, :],
                                                start=c == 0 and j == 0, stop=c == 1 and j == NJ - 1)
                    return last

                def project(g):
                    wait(pe, sC["rot_ready"], 4 * (n + 1) + g)
                    for h in range(4 * g, 4 * g + 4):
                        last = nc.tensor.matmul(ps[:, 6, P * (h % 4):P * (h % 4) + P], wr2[:, h, :], qc[:, v, :], start=True, stop=True)
                    last.then_inc(sC["rope_ps"], 1)

                def nope(g):
                    wait(pe, sC["mask_done"], 2 * n + 1 + g // 2)
                    nc.tensor.matmul(ps[:, g, 0:4 * LK], qc[:, v, :], anope[:, v, 4 * g:4 * g + 4, :].rearrange("p h k -> p (h k)"),
                                     start=True, stop=False, skip_group_check=True)

                def rope(g):
                    wait(pe, sC["rot_ready"], 4 * (n + 1) + g + 1)
                    for h in range(4):
                        last = nc.tensor.matmul(ps[:, g, LK * h:LK * h + LK], rot[:, g, h, :], kr2[:, v, :],
                                                start=False, stop=h == 3, skip_group_check=True)
                    if g % 2:
                        last.then_inc(sC["s_ps"], 1)

                if live(i, u + 1):
                    wait(pe, sC["qc_sb"], n + 2)
                    project(0)
                    nope(0)
                if live(i, u):
                    transpose_weights(0)
                if live(i, u + 1):
                    project(1)
                    nope(1)
                    rope(0)
                    project(2)
                    rope(1)
                    nope(2)
                if live(i, u):
                    transpose_weights(1)
                if live(i, u + 1):
                    project(3)
                    nope(3)
                    rope(2)
                if live(i, u + 2):
                    transpose_tile(i, u + 2)
                if live(i, u + 1):
                    rope(3)
                if live(i, u):
                    wait(pe, sC["x_ready"], n)
                    apply_weights(0)
                if live(i, u + 2):
                    latents(i, u + 2)
                if live(i, u):
                    last = apply_weights(1)
                    last.then_inc(sC["out_ps"], 1)

            pipeline(pe, body)
            pe.wait_ge(sC["x_ready"], NT)
            pe.wait_ge(sC["ptb_ev"], 2 * NT)
            pe.wait_ge(sC["mask_done"], 2 * NT)
            pe.wait_ge(sD["w_in"], 48)
            pe.wait_ge(sD["we_lo"], NT)

            def transpose_tile(i, s):
                m = 2 * i + s
                wait(pe, sD["xn_ready"], m + 1)
                wait(pe, sD["xT_sb"], m)
                for k in range(DK):
                    last = nc.tensor.transpose(ps[:, 4, P * k:P * k + P], xn[:, s % 2, P * k:P * k + P], ident[:])
                last.then_inc(sD["xT_ps"], 1)

            transpose_tile(0, 0)

            def body(i, u):
                n = 2 * i + u
                v = 1 - u

                def experts(g):
                    if g < 3:
                        wait(pe, sD["acc"], ACCS * (n - 1) + 2 * g + 3)
                    else:
                        wait(pe, sD["scaled"], n)
                    if g == 0:
                        wait(pe, sD["lo"], n + 1)
                    terms = [(a, w, k) for a, w in ((xhi, we_hi), (xhi, we_lo), (xlo, we_hi)) for k in range(DK)]
                    for t, (a, w, k) in enumerate(terms):
                        last = nc.tensor.matmul(ps[:, g, :], a[:, u, k, :], by_k(w)[:, k, 2 * D * g:2 * D * g + 2 * D],
                                                start=t == 0, stop=t == len(terms) - 1)
                    last.then_inc(sD["e_ps"], 1)

                if live(i, u + 1):
                    wait(pe, sD["xT_sb"], n + 2)
                    wait(pe, sD["chain"], LINKS * n + 1)
                    for k in range(DK):
                        last = nc.tensor.matmul(ps[:, 5, 0:E], xnT[:, v, k, :], wg[:, k, :], start=k == 0, stop=k == DK - 1)
                    last.then_inc(sD["lg_ps"], 1)
                if live(i, u):
                    experts(0)
                    wait(pe, sD["gT_sb"], n + 1)
                    wait(pe, sD["acc"], ACCS * (n - 1) + 1)
                    nc.tensor.matmul(ps[:, 7, 0:D], gatesT[:, u, :], be[:], start=True, stop=True).then_inc(sD["be_ps"], 1)
                if live(i, u + 2):
                    transpose_tile(i, u + 2)
                if live(i, u):
                    experts(1)
                    experts(2)
                    experts(3)
                if live(i, u + 1):
                    wait(pe, sD["chain"], LINKS * (n + 2))
                    wait(pe, sD["gT_sb"], n + 1)
                    nc.tensor.transpose(ps[0:E, 6, 0:P], gates[:, v, :], ident[:]).then_inc(sD["gT_ps"], 1)

            pipeline(pe, body)


_INS = ['x', 'ctx_1024', 'L0_xattn_Wq', 'L0_xattn_bq', 'L0_xattn_Wk', 'L0_xattn_bk', 'L0_xattn_Wv', 'L0_xattn_bv',
        'L0_xattn_Wo', 'L0_xattn_bo', 'L0_ffn_gate_w', 'L0_ffn_gate_b', 'L0_ffn_w1', 'L0_ffn_b1', 'L0_ffn_w2', 'L0_ffn_b2',
        'L0_ffn_w3', 'L0_ffn_b3', 'itok_BxS_0_511', 'L1_xattn_w_kv_comp', 'L1_xattn_w_q_down', 'L1_xattn_w_q_up', 'L1_xattn_w_q_rope',
        'L1_xattn_w_k_up', 'L1_xattn_w_k_rope', 'L1_xattn_w_v_up', 'L1_xattn_w_out', 'L1_ffn_Wg', 'L1_ffn_We', 'L1_ffn_be']


def constants():
    import numpy as np
    f = np.float32
    row = np.arange(P)
    c = {"c_ident": np.eye(P, dtype=f)}
    c["c_tri"] = (row[:, None] < row[None]).astype(f)
    c["c_ones"] = np.ones((P, P), f)
    c["c_iota"] = np.tile(row.astype(f), (P, 1))
    c["c_rev8"] = np.tile(np.arange(E, 0, -1).astype(f), (P, 1))
    c["c_tri8"] = np.tile(np.tril(np.ones((E, E), f)), (P, 1, 1))
    c["c_tokid"] = (np.arange(NT)[None] * P + row[:, None]).astype(f)
    half = RD // 2
    inv = (f(1.0) / f(10000.0) ** (np.arange(half, dtype=f) / f(half))).astype(f)
    ang = np.arange(S, dtype=f)[None] * inv[:, None]
    cos, sin = np.cos(ang).astype(f), np.sin(ang).astype(f)
    c["c_trig"] = np.concatenate([cos, cos, -sin, sin])
    kc, ks = np.concatenate([cos, cos])[:, :LK], np.concatenate([-sin, sin])[:, :LK]
    c["c_ktrig"] = np.stack([np.concatenate([kc, kc]), np.concatenate([ks, ks])], 1)
    c["c_iok"] = np.tile(np.arange(LK, dtype=f), (P, 1))
    c["c_kmask"] = (row[:, None] // HD == np.arange(HC)[None]).astype(f)
    i = np.arange(NJ)[None, :] * P + row[:, None]
    c["c_vmask"] = ((i // LK)[:, :, None] == np.arange(HC)).astype(f)
    return c


def kernel(**inputs):
    import numpy as np
    import concourse.bacc as bacc
    from concourse import mybir as mb
    from concourse.bass_utils import run_bass_kernel_spmd as run
    nc = bacc.Bacc("TRN2", target_bir_lowering=False, num_devices=1)
    arrays, io = {}, {}
    data = {n: np.ascontiguousarray(inputs[n]) for n in _INS}
    for n in ('L0_xattn_bq', 'L0_xattn_bk'):
        data[n] = np.ascontiguousarray(data[n].reshape(2, P).T)
    data['itok_BxS_0_511'] = np.ascontiguousarray(data['itok_BxS_0_511'].reshape(NT, P).T)
    data['L1_xattn_w_q_up'] = np.ascontiguousarray(data['L1_xattn_w_q_up'].reshape(DQ, NP2, P).transpose(2, 1, 0))
    data['L0_ffn_gate_b'] = data['L0_ffn_gate_b'].reshape(E, 1)
    data.update(constants())
    for name, a in data.items():
        arrays[f"in_{name}"] = a
        io[name] = nc.dram_tensor(f"in_{name}", a.shape, mb.dt.from_np(a.dtype), kind="ExternalInput").ap()
    io["out"] = nc.dram_tensor("out_0", (B, S, D), mb.dt.float32, kind="ExternalOutput").ap()
    io["xn_dram"] = nc.dram_tensor("xn_dram", (B * S, D), mb.dt.float32).ap()
    build(nc, io)
    r = run(nc, [arrays], core_ids=[0])
    return r.results[0]["out_0"]
```

```python
import numpy as np
import concourse.bass as bass
from concourse import mybir
from contextlib import ExitStack

P = 128
B = 2
S = 1024
D = 256
DK = D // P
TPB = S // P
NT = B * TPB
LK = 77
H = 16
HC = H // 2
UK = HC * LK
NJ = -(-UK // P)
HD = D // H
E = 8
EA = 2
LINKS = 8
ACCS = E - EA + 1
NL = 3
TOP = 2
NCH = (TOP * B * S + E * (P - 1)) // P
NSTR = 3
NIT = NCH // NSTR
PAIRS = [NT // 4 * (k % 2) + k // 2 for k in range(NT // 2)]
STEPS = NL * NSTR
RING = 4
DQ = 96
DC = 64
RD = 64
NP2 = H // 2
CW = 17
SCALE = float(np.float32(1.0) / np.float32(np.sqrt(np.float32(2 * RD))))
FMIN = float(np.finfo(np.float32).min)
PAD = P + 2 * LK + P
VW1 = HD + 1


def rows(j):
    return min(P, UK - P * j)


def heads_of(j):
    h0 = P * j // LK
    return h0, (P * j + rows(j) - 1) // LK - h0 + 1


def v_unit(q):
    return q // (2 * NJ), q // NJ % 2, q % NJ


def bcast(ap, axis, n):
    u = ap.unsqueeze(axis)
    shape = list(u.shape)
    shape[axis] = n
    return u.broadcast_to(shape)


def build(nc, io):
    F32 = mybir.dt.float32
    F32R = mybir.dt.float32r
    I32 = mybir.dt.int32
    ALU = mybir.AluOpType
    ACT = mybir.ActivationFunctionType
    AX = mybir.AxisListType

    with ExitStack() as st:
        def sb(name, shape, dt=F32):
            return st.enter_context(nc.sbuf_tensor(name, shape, dt))

        def sem(name):
            return st.enter_context(nc.semaphore(name))

        ps = st.enter_context(nc.psum_tensor("ps", [P, 8, 512], F32))

        x = sb("x", [P, B, TPB, D])
        ident = sb("ident", [P, P])
        stats = sb("stats", [P, 2, 6])
        st_all = sb("st_all", [P, B, TPB, 6])
        xs = sb("xs", [P, 2, D])
        mv = sb("mv", [P, B, TPB, 2])
        rstd = sb("rstd", [P, B, TPB])
        epsv = sb("epsv", [P, B, TPB])
        power = sb("power", [P, B, TPB])
        xn = sb("xn", [P, 2, D])
        xnT = sb("xnT", [P, 2, DK, P])
        wqd = sb("wqd", [P, DK, DQ])
        trig = sb("trig", [P, 2, S])
        negm = sb("negm", [P, NT, LK])
        seg_i = sb("seg_i", [P, NT], I32)
        seg = sb("seg", [P, 2, NT])
        iok = sb("iok", [P, LK])
        krbd = sb("krbd", [P, 2, B, 2, LK])
        gw = sb("gw", [P, DK, E])
        gb = sb("gb", [E, 1])
        ctxT = sb("ctxT", [P, DK, B, LK])
        early = ExitStack()

        def sb(name, shape, dt=F32):
            return early.enter_context(nc.sbuf_tensor(name, shape, dt))

        b0 = sb("b0", [P, NL, E, D])
        wr = sb("wr", [DQ, NP2, P])
        anope = sb("anope", [DQ, B, H, LK])
        vw = sb("vw", [P, B, 2, NJ, D])
        w0 = sb("w0", [P, E, NL, DK, D])
        knT = vw[:].rearrange("p b c j d -> p (b c j d)")[:, 0:NP2 * B * LK].rearrange("p (q b k) -> p q b k", q=NP2, b=B)
        room = b0[:].rearrange("p l e d -> p (l e d)")
        at = [0]

        def carve(cols):
            at[0] += cols
            return room[:, at[0] - cols:at[0]]

        wkup = carve(H * RD)[0:DC]
        wqupT = carve(NP2 * DQ).rearrange("p (q c) -> p q c", q=NP2)
        wkvc = carve(DK * DC).rearrange("p (k c) -> p k c", k=DK)
        assert at[0] <= E * D
        at[0] = E * D
        wvup = carve(H * RD)[0:DC]
        wout = carve(NP2 * D).rearrange("p (q d) -> p q d", q=NP2)
        wkr = carve(2 * 2 * RD).rearrange("p (v r) -> p v r", v=2)[0:DC]
        kvcT = carve(B * LK)[0:DC]
        krt = carve(2 * LK).rearrange("p (v k) -> p v k", v=2)
        kruv = carve(2 * B * LK).rearrange("p (v b k) -> p v b k", v=2, b=B)
        krp = [t[:].rearrange("p t d -> p (t d)")[:, 0:2 * B * LK].rearrange("p (v b k) -> p v b k", v=2, b=B) for t in (xn, xs)]
        phase = ExitStack()

        def sb(name, shape, dt=F32):
            return phase.enter_context(nc.sbuf_tensor(name, shape, dt))

        wq = sb("wq", [P, DK, D])
        wk = sb("wk", [P, DK, D])
        wv = sb("wv", [P, DK, D])
        wo = sb("wo", [P, DK, D])
        bq = sb("bq", [P, 2])
        bk = sb("bk", [P, 2])
        bv = sb("bv", [P, D])
        bo = sb("bo", [P, D])
        kmask = sb("kmask", [P, HC])
        vmask = sb("vmask", [P, NJ, HC])
        ctx = sb("ctx", [LK, B, D])
        ctx_rep = sb("ctx_rep", [P, DK, B, HC, LK])
        kT = sb("kT", [P, 2, B, LK])
        kbd = sb("kbd", [P, B, 2, HC, LK])
        vbd = sb("vbd", [P, B, 2, NJ, HC, VW1])
        vtmp = sb("vtmp", [P, 2, 4, P])
        qT = sb("qT", [P, 2, 2, P])
        pr = sb("pr", [P, 2, HC, LK])
        prT = sb("prT", [P, 2, NJ, P])
        flat_prT = prT[:].rearrange("p c j q -> p (c j q)")
        VTMP = [vtmp[:, 0], vtmp[:, 1]] + [t.rearrange("p (q d) -> p q d", q=4) for t in (
            pr[:, 1].rearrange("p h k -> p (h k)")[:, 0:4 * P], flat_prT[:, 0:4 * P], flat_prT[:, 4 * P:8 * P])]
        nmax = sb("nmax", [P, 2, HC])
        rsum = sb("rsum", [P, 2, HC])
        on = sb("on", [P, 2, HC, HD])
        oT = vtmp[:, 0, 0:2]

        phase.close()
        phase = ExitStack()
        lg_all = sb("lg_all", [P, B, S])
        lg = lg_all[0:E]
        gmax = sb("gmax", [E, B])
        gsum = sb("gsum", [E, B])
        prob = sb("prob", [P, NT, E])
        top = sb("top", [P, TOP, NT])
        key = sb("key", [P, NT, E])
        kmax = sb("kmax", [P, NT])
        oneh = sb("oneh", [P, TOP, NT, E])
        sel = sb("sel", [P, NT, E])
        prob2 = sb("prob2", [P, NT, E])
        cmp16 = sb("cmp16", [P, E, NT])
        nch = sb("nch", [P, E])
        tri8 = sb("tri8", [P, E, E])
        cend = sb("cend", [P, E])
        base = sb("base", [P, E])
        pos = prob2
        slot = sb("slot", [P, TOP * NT])
        slot_i = sb("slot_i", [P, 3, TOP * NT], I32)
        rc = sb("rc", [P, 2, TOP * NT])
        rowhot = sb("rowhot", [P, 2, 8, P])
        chhot = sb("chhot", [P, TOP * NT, NCH])
        payload = sb("payload", [P, TOP * NT, 2, NCH])
        xng = payload[:].rearrange("p t v c -> p (t v c)")[:, 0:RING * D].rearrange("p (r d) -> p r d", r=RING)
        vsum = rowhot[:].rearrange("p g t q -> p (g t q)").rearrange("p (e d) -> p e d", e=E)
        cmp8 = sb("cmp8", [P, NCH, E])
        ce = sb("ce", [P, NCH])
        ce_i = sb("ce_i", [P, NCH], I32)
        tok_i = sb("tok_i", [P, NCH], I32)
        wslot = sb("wslot", [P, NCH])
        unit = sb("unit", [P, 2 * E])
        indT = sb("indT", [E, NT, P], F32R)
        tri = sb("tri", [P, P])
        ones = sb("ones", [P, P])
        iot = sb("iot", [P, P])
        rev8 = sb("rev8", [P, E])
        tokid = sb("tokid", [P, NT])
        rows0 = ExitStack()
        work0 = rows0.enter_context(nc.sbuf_tensor("work0", [P, NP2 * PAD], F32))
        vbdT = work0[:].rearrange("p (q c) -> p q c", q=NP2)
        w_ = lambda q: work0[:, NSTR * D * q:NSTR * D * (q + 1)].rearrange("p (s d) -> p s d", s=NSTR)
        g0 = lg_all[:].rearrange("p b s -> p (b s)")[:, 0:NSTR * D].rearrange("p (s d) -> p s d", s=NSTR)
        hT = w_(1).rearrange("p s (k q) -> p s k q", k=DK)
        h0 = w_(2)
        y0 = w_(3)
        rows0.close()
        v0_hi = sb("v0_hi", [E, D], F32R)
        v0_lo = sb("v0_lo", [E, D], F32R)
        phase.close()
        early.close()
        phase = ExitStack()
        an_hi = sb("an_hi", [DQ, B, H, LK], F32R)
        pcT_lo = sb("pcT_lo", [P, 2, NJ, P], F32R)
        qc = sb("qc", [DQ, 2, P])
        qc_hi = sb("qc_hi", [DQ, 2, P], F32R)
        sb("rest_of_b0", [P, E * NL * D - B * H * LK - 2 * NJ * P - 4 * P])
        sb("place_of_wr", [DQ, NP2, P])
        an_lo = sb("an_lo", [DQ, B, H, LK], F32R)
        vw_lo = sb("vw_lo", [P, B, 2, NJ, D], F32R)
        NW = DK * E * D
        WCOLS = NW // NT
        we = sb("we", [P, NW])
        we_hi = sb("we_hi", [P, NW], F32R)
        we_lo = sb("we_lo", [P, NW], F32R)
        vw_hi = sb("vw_hi", [P, B, 2, NJ, D], F32R)
        qc_lo = sb("qc_lo", [DQ, 2, P], F32R)
        rot = sb("rot", [P, 4, 2, 2, P])
        pc = sb("pc", [P, 2, HC, LK])
        pcT_hi = sb("pcT_hi", [P, 2, NJ, P], F32R)
        pmax = sb("pmax", [P, 2, HC])
        psm = sb("psm", [P, 2, HC])
        wg = sb("wg", [P, DK, E])
        be = sb("be", [E, D])
        lt = sb("lt", [P, 2, E])
        lmax = sb("lmax", [P, 2, E])
        lidx = sb("lidx", [P, 2, E], mybir.dt.uint32)
        lidf = sb("lidf", [P, 2, TOP])
        gt = sb("gt", [P, 2, TOP])
        gd = sb("gd", [P, 2, 2])
        goh = sb("goh", [P, 2, TOP, E])
        gates = sb("gates", [P, 2, E])
        gatesT = sb("gatesT", [E, 2, P])
        acc = sb("acc", [P, 2, D])
        part = sb("part", [P, 2, EA, D])
        xhi = sb("xhi", [P, 2, DK, P], F32R)
        xlo = sb("xlo", [P, 2, DK, P], F32R)
        y = sb("y", [P, 2, D])
        iot8 = sb("iot8", [P, E])
        phase.close()
        by_k = lambda t: t.rearrange("p (k n) -> p k n", k=DK)

        S_ = lambda c: ps[:, 2 * c:2 * c + 2, 0:4 * LK].rearrange("p a (h k) -> p a h k", h=4)
        PTA = ps[:, 4, 0:3 * P].rearrange("p (j q) -> p j q", j=3)
        PTB = ps[:, 5, 0:2 * P].rearrange("p (j q) -> p j q", j=2)
        XT = ps[:, 6, 0:D].rearrange("p (k q) -> p k q", k=DK)
        QT = ps[:, 6, 0:D].rearrange("p (c q) -> p c q", c=2)
        O_ = ps[:, 7, 0:2 * HC * VW1].rearrange("p (c h v) -> p c h v", c=2, h=HC)
        OT = ps[:, 6, D:2 * D].rearrange("p (c q) -> p c q", c=2)
        OUT = ps[:, 7, 0:D]

        x_in = [sem(f"x_in{g}") for g in range(2)]
        k_in = sem("k_in")
        v_in = sem("v_in")
        q_in = sem("q_in")
        g_in = sem("g_in")
        c_in = sem("c_in")
        w0_in = sem("w0_in")
        b0_in = [sem(f"b0_in{l}") for l in range(NL)]
        const_set = sem("const_set")
        sA = {n: sem("a_" + n) for n in (
            "stats aggr rstd ones_ready kv_ps kv_sb kbd_ready vbd_ready ctxT_ps ctxT_sb rep_ready xn_ready xT_ps xT_sb q_ps "
            "q_ready s_ps max_done sub_done exp_done pta_ps ptb_ps pta_ev ptb_ev o_ps rsum_done on_ready oT_ps oT_sb out_ps "
            "x1_ready aggr2 stats2 xo_ready x1_kept stats_kept").split()}

        sB = {n: sem("b_" + n) for n in (
            "const rstd xn_ready xT_ps xT_sb lg_ps lg_sb chain gexp pT_ps ind_ps ind_sb rank_ps payload rowhot rowhot_used "
            "tok_ready route_ready tp_ps tp_sb l_ps l_sb y_ready v_ps v_sb v_done vsum_zero o_ps x2_ready stats aggr").split()}
        stored = [sem(f"b_stored{r}") for r in range(RING)]
        gathered = [sem(f"b_gathered{s}") for s in range(NSTR)]

        sC = {n: sem("c_" + n) for n in (
            "const_hi const_lo vw_lo lo_done qlo kvc_ps kvc_sb kn_ps kn_sb v_ps v_sb a_ps a_sb kr_ps kr_sb kr_mul vw_ps "
            "vw_sb zero rstd xn_ready xT_ps xT_sb qc_ps qc_sb rope_ps rot_ready s_ps mask_done max_done sub_done exp_done "
            "sum_done rsum_done norm_done pta_ps ptb_ps pta_ev ptb_ev out_ps x_ready stats").split()}
        sD = {n: sem("d_" + n) for n in (
            "we_in we_hi we_lo hi lo scaled summed acc w_in aggr rstd xn_ready xT_ps xT_sb lg_ps chain diff exp gT_ps gT_sb "
            "be_ps e_ps chain2 y_ready").split()}
        written = [sem(f"d_written{u}") for u in range(2)]
        c_w = sem("c_w")

        def vw_parts(t, b):
            return t[:, b, :, 0:NJ - 1], t[0:rows(NJ - 1), b, :, NJ - 1]

        ROPE = (ps[:, 6, 0:2 * P], ps[:, 7, D:D + 2 * P])

        VBANK = (2, 3, 7)

        block = st.enter_context(nc.Block())

        def wait(eng, s, n):
            if not isinstance(n, int) or n > 0:
                eng.wait_ge(s, n)

        def tile_at(i, s):
            return s % 2, i + s // 2

        def pipeline(eng, body, first=1):
            body(-1, 1)
            for i in range(first):
                body(i, 0)
                body(i, 1)
            with eng.Fori(first, TPB - 1) as i:
                body(i, 0)
                body(i, 1)
            body(TPB - 1, 0)
            body(TPB - 1, 1)
            body(TPB, 0)

        def live(i, s):
            return not isinstance(i, int) or 0 <= 2 * i + s < NT

        @block.sync
        def _(sp):
            sp.dma_start(ctx[:], io["ctx_1024"].rearrange("b k d -> k b d")).then_inc(c_in, 16)
            sp.dma_start(ident[:], io["c_ident"]).then_inc(c_in, 16)
            sp.dma_start(wk[:], io["L0_xattn_Wk"].rearrange("(k p) n -> p k n", p=P)).then_inc(k_in, 16)
            sp.dma_start(bk[:], io["L0_xattn_bk"]).then_inc(k_in, 16)
            sp.dma_start(kmask[:], io["c_kmask"]).then_inc(k_in, 16)
            sp.dma_start(wv[:], io["L0_xattn_Wv"].rearrange("(k p) n -> p k n", p=P)).then_inc(v_in, 16)
            sp.dma_start(bv[:], io["L0_xattn_bv"].partition_broadcast(P)).then_inc(v_in, 16)
            sp.dma_start(vmask[:], io["c_vmask"]).then_inc(v_in, 16)
            sp.dma_start(wq[:], io["L0_xattn_Wq"].rearrange("(k p) n -> p k n", p=P)).then_inc(q_in, 16)
            sp.dma_start(bq[:], io["L0_xattn_bq"]).then_inc(q_in, 16)
            sp.dma_start(wo[:], io["L0_xattn_Wo"].rearrange("(k p) n -> p k n", p=P)).then_inc(q_in, 16)
            sp.dma_start(bo[:], io["L0_xattn_bo"].partition_broadcast(P)).then_inc(q_in, 16)
            sp.dma_start(gw[:], io["L0_ffn_gate_w"].rearrange("(k p) e -> p k e", p=P)).then_inc(g_in, 16)
            sp.dma_start(gb[:], io["L0_ffn_gate_b"]).then_inc(g_in, 16)
            for l, n in enumerate(("L0_ffn_w1", "L0_ffn_w2", "L0_ffn_w3")):
                for k in range(DK):
                    sp.dma_start(w0[:, :, l, k, :], io[n][:, P * k:P * k + P, :].rearrange("e p o -> p e o")).then_inc(w0_in, 16)
            for dst, n in ((wkup, "L1_xattn_w_k_up"), (wvup, "L1_xattn_w_v_up"), (wqupT, "L1_xattn_w_q_up"), (trig[:], "c_trig"),
                           (seg_i[:], "itok_BxS_0_511"), (krt, "c_ktrig"), (iok[:], "c_iok")):
                sp.dma_start(dst, io[n]).then_inc(c_w, 16)
            sp.dma_start(wout, io["L1_xattn_w_out"].rearrange("(q p) n -> p q n", p=P)).then_inc(c_w, 16)
            sp.dma_start(wkvc, io["L1_xattn_w_kv_comp"].rearrange("(k p) n -> p k n", p=P)).then_inc(c_w, 16)
            sp.dma_start(wqd[:], io["L1_xattn_w_q_down"].rearrange("(k p) n -> p k n", p=P)).then_inc(c_w, 16)
            half = RD // 2
            sp.dma_start(wr[:].rearrange("c q r -> c (q r)"), io["L1_xattn_w_q_rope"]).then_inc(c_w, 16)
            for a in range(2):
                sp.dma_start(wkr[:, 0, RD * a:RD * a + RD], io["L1_xattn_w_k_rope"]).then_inc(c_w, 16)
                sp.dma_start(wkr[:, 1, RD * a:RD * a + half], io["L1_xattn_w_k_rope"][:, half:RD]).then_inc(c_w, 16)
                sp.dma_start(wkr[:, 1, RD * a + half:RD * a + RD], io["L1_xattn_w_k_rope"][:, 0:half]).then_inc(c_w, 16)
            sp.wait_ge(sA["x1_ready"], NT)
            for dst, n in ((tri, "c_tri"), (ones, "c_ones"), (iot, "c_iota"), (rev8, "c_rev8"), (tri8, "c_tri8"), (unit, "c_unit"), (tokid, "c_tokid")):
                sp.dma_start(dst[:], io[n]).then_inc(sB["const"], 16)
            for n in range(NT):
                b, j = tile_at(0, n)
                sp.wait_ge(sB["xn_ready"], n + 1)
                sp.dma_start(io["xn_dram"][P * (TPB * b + j):P * (TPB * b + j + 1), :], xng[:, n % RING, :]).then_inc(stored[n % RING], 16)
            for l, n in enumerate(("L0_ffn_b1", "L0_ffn_b2", "L0_ffn_b3")):
                if l == 0:
                    sp.wait_ge(sC["a_ps"], 6)
                if l == 1:
                    sp.wait_ge(sC["vw_ps"], 2 * NJ)
                    sp.wait_ge(sC["kr_mul"], 9)
                sp.dma_start(b0[:, l], io[n].partition_broadcast(P)).then_inc(b0_in[l], 16)
            sp.wait_ge(sB["l_sb"], NL * NCH)
            for k in range(DK):
                sp.dma_start(by_k(we)[:, k, :].rearrange("p (e d) -> p e d", e=E), io["L1_ffn_We"][:, P * k:P * k + P, :].rearrange("e p d -> p e d")).then_inc(sD["we_in"], 16)
            sp.wait_ge(sB["x2_ready"], NT // 2)
            sp.dma_start(wg[:], io["L1_ffn_Wg"].rearrange("(k p) e -> p k e", p=P)).then_inc(sD["w_in"], 16)
            sp.dma_start(be[:], io["L1_ffn_be"]).then_inc(sD["w_in"], 16)
            sp.dma_start(iot8[:], io["c_iota"][:, 0:E]).then_inc(sD["w_in"], 16)
            for n in range(NT):
                b, j = tile_at(0, n)
                sp.wait_ge(sD["y_ready"], n + 1)
                sp.dma_start(io["out"][b, P * j:P * j + P, :], y[:, b, :]).then_inc(written[b], 16)
            for b in range(B):
                sp.wait_ge(written[b], 16 * TPB)
        @block.gpsimd
        def _(pool):
            nc.gpsimd.memset(epsv[:], 1e-5).then_inc(const_set, 1)
            nc.gpsimd.memset(power[:], -0.5).then_inc(const_set, 1)
            pool.wait_ge(const_set, 2)

            def deviations(aggregated, count, done, before, parts):
                pool.wait_ge(aggregated, count)
                j = slice(parts[0].start, parts[-1].stop)
                nc.gpsimd.tensor_tensor(rstd[:, :, j], mv[:, :, j, 1], epsv[:, :, j], ALU.add).then_inc(done, 1)
                pool.wait_ge(done, before + 1)
                for j in parts:
                    nc.gpsimd.tensor_tensor(rstd[:, :, j], rstd[:, :, j], power[:, :, j], ALU.pow).then_inc(done, 1)

            deviations(sA["aggr"], 1, sA["rstd"], 0, (slice(0, 1), slice(1, TPB // 2)))
            pool.wait_ge(v_in, 48)
            for g in range(5):
                pool.wait_ge(sA["kv_sb"], g + 2)
                for q in range(4):
                    b, c, j = v_unit(4 * g + q)
                    r = rows(j)
                    last = nc.gpsimd.tensor_tensor(vbd[0:r, b, c, j, :, 0:HD], VTMP[g][0:r, q].rearrange("p (h d) -> p h d", h=HC),
                                                   bcast(vmask[0:r, j], 2, HD), ALU.mult)
                last.then_inc(sA["vbd_ready"], 1)
            deviations(sA["aggr"], 2, sA["rstd"], 3, (slice(TPB // 2, TPB),))
            pool.wait_ge(q_in, 64)

            def body(i, u):
                if live(i, u):
                    b, j = tile_at(i, u)
                    jj = bass.ds(j, 1)
                    wait(pool, sA["xn_ready"], 2 * i + u + 1)
                    nc.gpsimd.tensor_tensor(x[:, b, jj, :].squeeze(1), x[:, b, jj, :].squeeze(1), bo[:], ALU.add).then_inc(sA["xo_ready"], 1)

            pipeline(pool, body)

            pool.wait_ge(sA["stats_kept"], NT)
            nc.gpsimd.memset(work0[:], 0.0).then_inc(sC["zero"], 1)
            deviations(sA["aggr2"], NT, sB["rstd"], 0, (slice(0, 1), slice(1, TPB)))
            nc.gpsimd.memset(krbd[:], 0.0).then_inc(sC["kr_mul"], 1)
            pool.wait_ge(sC["kr_sb"], 1)
            for w in range(2):
                for v in range(2):
                    nc.gpsimd.tensor_tensor(krp[w][:, v], kruv[:, v if w == 0 else 1 - v], bcast(krt[:, v], 1, B), ALU.mult).then_inc(sC["kr_mul"], 1)
            pool.wait_ge(sC["kr_mul"], 5)
            for w, op in enumerate((ALU.add, ALU.subtract)):
                for a in range(2):
                    r = slice(RD * a, RD * a + RD)
                    nc.gpsimd.tensor_tensor(krbd[r, w, :, a, :], krp[w][r, 0], krp[w][r, 1], op).then_inc(sC["kr_mul"], 1)
                    pool.wait_ge(sC["kr_mul"], 6 + 2 * w + a)
            for r in range(RING):
                pool.wait_ge(stored[r], 16 * NT // RING)
            pool.wait_ge(sB["tok_ready"], 1)
            for c in range(NCH):
                it, s = c // NSTR, c % NSTR
                if c == NSTR:
                    pool.wait_ge(sB["rowhot_used"], 4)
                    nc.gpsimd.memset(vsum, 0.0).then_inc(sB["vsum_zero"], 1)
                if it:
                    pool.wait_ge(sB["tp_ps"], NL * NSTR * (it - 1) + s + 1)
                pool.indirect_dma_start(out=g0[:, s, :], out_offset=None, in_=io["xn_dram"],
                                        in_offset=bass.IndirectOffsetOnAxis(ap=tok_i[:, c:c + 1], axis=0)).then_inc(gathered[s], 16)
            def latents_lo(i, s):
                m = 2 * i + s
                wait(pool, sC["qc_sb"], m + 1)
                wait(pool, sC["s_ps"], 2 * m - 2)
                nc.gpsimd.tensor_tensor(qc_lo[:, s % 2, :], qc[:, s % 2, :], qc_hi[:, s % 2, :], ALU.subtract).then_inc(sC["qlo"], 1)

            deviations(sB["aggr"], 1, sC["rstd"], 0, (slice(0, 1),))
            pool.wait_ge(sC["const_hi"], 1)
            nc.gpsimd.tensor_tensor(an_lo[:, 0], anope[:, 0], an_hi[:, 0], ALU.subtract).then_inc(sC["const_lo"], 1)
            latents_lo(0, 0)
            nc.gpsimd.tensor_tensor(an_lo[:, 1], anope[:, 1], an_hi[:, 1], ALU.subtract).then_inc(sC["const_lo"], 1)
            deviations(sB["aggr"], 2, sC["rstd"], 2, (slice(1, TPB),))

            def body(i, u):
                n = 2 * i + u

                def norm(m, c):
                    wait(pool, sC["rsum_done"], 2 * m + c + 1)
                    nc.gpsimd.tensor_tensor(pc[:, c], pc[:, c], bcast(psm[:, c], 2, LK), ALU.mult).then_inc(sC["norm_done"], 1)

                def sub(m, c):
                    wait(pool, sC["max_done"], 2 * m + c + 1)
                    nc.gpsimd.tensor_tensor(pc[:, c], pc[:, c], bcast(pmax[:, c], 2, LK), ALU.subtract).then_inc(sC["sub_done"], 1)

                if live(i, u):
                    norm(n, 1)
                if live(i, u + 1):
                    sub(n + 1, 0)
                    norm(n + 1, 0)
                    sub(n + 1, 1)
                if live(i, u + 2):
                    latents_lo(i, u + 2)
                if isinstance(i, int) and n == NT - 1:
                    deviations(sD["aggr"], NT - 2, sD["rstd"], 0, (slice(0, 1), slice(1, TPB - 1)))
                if live(i, u):
                    wait(pool, sD["we_hi"], n + 1)
                    cols = bass.ds(2 * WCOLS * i + WCOLS * u, WCOLS)
                    nc.gpsimd.tensor_tensor(we_lo[:, cols], we[:, cols], we_hi[:, cols], ALU.subtract).then_inc(sD["we_lo"], 1)

            pipeline(pool, body)
            deviations(sD["aggr"], NT, sD["rstd"], 3, (slice(TPB - 1, TPB),))

            def split_tile(i, s):
                m = 2 * i + s
                wait(pool, sD["hi"], m + 1)
                wait(pool, sD["e_ps"], 4 * m - 4)
                nc.gpsimd.tensor_tensor(xlo[:, s % 2], xnT[:, s % 2], xhi[:, s % 2], ALU.subtract).then_inc(sD["lo"], 1)

            def body(i, u):
                n = 2 * i + u
                if live(i, u + 2):
                    split_tile(i, u + 2)
                if live(i, u):
                    wait(pool, sD["scaled"], n + 1)
                    wait(pool, sD["y_ready"], n - 1)
                    nc.gpsimd.tensor_tensor(part[:, u, 0], part[:, u, 0], part[:, u, 1], ALU.add).then_inc(sD["summed"], 1)

            split_tile(0, 0)
            pipeline(pool, body)

        @block.scalar
        def _(act):
            for g in range(2):
                for b in range(B):
                    if g == 0 and b == 0:
                        act.wait_ge(k_in, 48)
                    act.dma_start(x[:, b, 4 * g:4 * g + 4, :], io["x"][b, 512 * g:512 * g + 512, :].rearrange("(j p) d -> p j d", p=P)).then_inc(x_in[g], 16)
            act.wait_ge(v_in, 48)
            for b in range(B):
                for c in range(2):
                    last = nc.scalar.activation(vbd[:, b, c, :, :, HD], vmask[:], ACT.Copy)
            last.then_inc(sA["ones_ready"], 1)
            act.wait_ge(q_in, 64)

            def evac_xT(i, s):
                m = 2 * i + s
                wait(act, sA["xT_ps"], m + 1)
                wait(act, sA["q_ps"], m - 1)
                nc.scalar.activation(xnT[:, s % 2], XT, ACT.Copy).then_inc(sA["xT_sb"], 1)

            def evac_q(i, s):
                m = 2 * i + s
                wait(act, sA["q_ps"], m + 1)
                wait(act, sA["s_ps"], 2 * m - 2)
                for c in range(2):
                    last = nc.scalar.activation(qT[:, s % 2, c, :], QT[:, c], ACT.Identity, bias=bq[:, c:c + 1])
                last.then_inc(sA["q_ready"], 1)

            evac_xT(0, 0)
            evac_q(0, 0)

            def body(i, u):
                n = 2 * i + u
                if isinstance(i, int) and n == 0:
                    act.wait_ge(sA["vbd_ready"], 5)

                def weights(c):
                    wait(act, sA["pta_ps"], 2 * n + c + 1)
                    wait(act, sA["o_ps"], n)
                    nc.scalar.activation(prT[:, c, 0:3, :], PTA, ACT.Copy).then_inc(sA["pta_ev"], 1)
                    wait(act, sA["ptb_ps"], 2 * n + c + 1)
                    nc.scalar.activation(prT[:, c, 3, :], PTB[:, 0], ACT.Copy)
                    nc.scalar.activation(prT[0:rows(4), c, 4, :], PTB[0:rows(4), 1], ACT.Copy).then_inc(sA["ptb_ev"], 1)

                def exponentials(c):
                    wait(act, sA["sub_done"], 2 * n + 3 + c)
                    nc.scalar.activation(pr[:, c], pr[:, c], ACT.Exp).then_inc(sA["exp_done"], 1)

                if live(i, u):
                    weights(0)
                if live(i, u - 1):
                    wait(act, sA["oT_ps"], n)
                    wait(act, sA["out_ps"], n - 1)
                    nc.scalar.activation(oT, OT, ACT.Copy).then_inc(sA["oT_sb"], 1)
                if live(i, u + 2):
                    evac_xT(i, u + 2)
                if live(i, u + 1):
                    exponentials(0)
                if live(i, u):
                    weights(1)
                if live(i, u + 1):
                    exponentials(1)
                if live(i, u + 2):
                    evac_q(i, u + 2)

            pipeline(act, body)

            def copies(ps_sem, k, dst, src, sb_sem, scale=1.0):
                act.wait_ge(ps_sem, k)
                nc.scalar.activation(dst, src, ACT.Copy, scale=scale).then_inc(sb_sem, 1)

            copies(sC["kvc_ps"], 1, kvcT, ps[0:DC, 7, 0:B * LK], sC["kvc_sb"])
            for g, (q0, nq) in enumerate(((0, 3), (3, 3), (6, 2))):
                copies(sC["kn_ps"], g + 1, knT[:, q0:q0 + nq].rearrange("p q b k -> p (q b k)"), ps[:, g, 0:nq * B * LK], sC["kn_sb"])
            copies(sC["kr_ps"], 1, kruv.rearrange("p v b k -> p (v b k)"), ps[:, 3, 0:2 * B * LK], sC["kr_sb"], scale=SCALE)
            def body(i):
                for r in range(RING):
                    n = RING * i + r
                    act.wait_ge(sB["xT_ps"], n + 1)
                    wait(act, sB["lg_ps"], n - 1)
                    nc.scalar.activation(xnT[:, r % 2], ps[:, r, 0:D].rearrange("p (k q) -> p k q", k=DK), ACT.Copy).then_inc(sB["xT_sb"], 1)

            body(0)
            with act.Fori(1, NT // RING) as i:
                body(i)
            for g in range(6):
                if g == 3:
                    act.wait_ge(sB["chain"], 3)
                    for b in range(B):
                        nc.scalar.activation(lg[:, b], lg[:, b], ACT.Exp, bias=gmax[:, b:b + 1], accum_out=gsum[:, b:b + 1]).then_inc(sB["gexp"], 1)
                q0, a = 3 * (g // 2), g % 2
                nh = min(3, NP2 - q0)
                copies(sC["a_ps"], g + 1, anope[:].rearrange("p b (q a) k -> p a q b k", a=2)[:, a, q0:q0 + nh],
                       ps[0:DQ, g % 2, 0:nh * B * LK].rearrange("p (h b k) -> p h b k", h=nh, b=B), sC["a_sb"], scale=SCALE)
            act.wait_ge(sC["zero"], 1)
            for b in range(B):
                if b:
                    act.wait_ge(sC["vw_ps"], NJ)
                act.wait_ge(sC["v_ps"], 3)
                for q in range(NP2):
                    for a in range(2):
                        r = slice(RD * a, RD * a + RD)
                        last = nc.scalar.activation(vbdT[r, q, P + LK * a:P + LK * a + LK], ps[r, VBANK[q // 3], (q % 3) * B * LK + b * LK:(q % 3) * B * LK + (b + 1) * LK], ACT.Copy)
                last.then_inc(sC["v_sb"], 1)
                for m in range(NJ):
                    act.wait_ge(sC["vw_ps"], NJ * b + m + 1)
                    for a in range(2):
                        c, j = (2 * m + a) // NJ, (2 * m + a) % NJ
                        last = nc.scalar.activation(vw[0:rows(j), b, c, j, :], ps[0:rows(j), m % 2, D * a:D * a + D], ACT.Copy)
                    last.then_inc(sC["vw_sb"], 1)
            act.wait_ge(sB["ind_ps"], 1)
            for g in range(4):
                last = nc.scalar.activation(indT[:, 4 * g:4 * g + 4, :], ps[0:E, g, :].rearrange("e (t q) -> e t q", q=P), ACT.Copy)
            last.then_inc(sB["ind_sb"], 1)

            def evac(it, k):
                l, s = k // NSTR, k % NSTR
                act.wait_ge(sB["tp_ps"], STEPS * it + k + 1)
                nc.scalar.activation(hT[:, s], ps[:, s, 0:D].rearrange("p (k q) -> p k q", k=DK),
                                     ACT.Relu if l else ACT.Copy).then_inc(sB["tp_sb"], 1)

            def chunks(it):
                for k in range(STEPS):
                    evac(it, k)

            chunks(0)
            with act.Fori(1, NIT) as it:
                chunks(it)
            act.wait_ge(sB["v_ps"], 1)
            nc.scalar.activation(v0_hi[:], ps[0:E, 5, 0:D], ACT.Copy).then_inc(sB["v_sb"], 1)
            act.wait_ge(sB["l_sb"], NL * NCH)
            act.wait_ge(c_w, CW * 16)
            act.wait_ge(sC["a_sb"], 6)
            act.wait_ge(sC["vw_sb"], 2 * NJ)
            nc.scalar.activation(an_hi[:], anope[:], ACT.Copy).then_inc(sC["const_hi"], 1)
            for b in range(B):
                for hi, whole in zip(vw_parts(vw_hi, b), vw_parts(vw, b)):
                    last = nc.scalar.activation(hi, whole, ACT.Copy)
                last.then_inc(sC["const_hi"], 1)

            def evac_xT(i, s):
                m = 2 * i + s
                wait(act, sC["xT_ps"], m + 1)
                nc.scalar.activation(xnT[:, s % 2], ps[:, 6, 0:D].rearrange("p (k q) -> p k q", k=DK), ACT.Copy).then_inc(sC["xT_sb"], 1)

            def evac_qc(i, s):
                m = 2 * i + s
                wait(act, sC["qc_ps"], m + 1)
                wait(act, sC["s_ps"], 2 * m - 2)
                nc.scalar.activation(qc[:, s % 2, :], ps[0:DQ, 6, D:D + P], ACT.Copy)
                nc.scalar.activation(qc_hi[:, s % 2, :], ps[0:DQ, 6, D:D + P], ACT.Copy).then_inc(sC["qc_sb"], 1)

            evac_xT(0, 0)
            evac_qc(0, 0)

            def body(i, u):
                n = 2 * i + u

                def weights(c):
                    wait(act, sC["pta_ps"], 2 * n + c + 1)
                    wait(act, sC["out_ps"], n)
                    nc.scalar.activation(pcT_hi[:, c, 0:3, :], PTA, ACT.Copy).then_inc(sC["pta_ev"], 1)
                    wait(act, sC["ptb_ps"], 2 * n + c + 1)
                    nc.scalar.activation(pcT_hi[:, c, 3, :], PTB[:, 0], ACT.Copy)
                    nc.scalar.activation(pcT_hi[0:rows(4), c, 4, :], PTB[0:rows(4), 1], ACT.Copy).then_inc(sC["ptb_ev"], 1)

                def exponentials(c):
                    wait(act, sC["sub_done"], 2 * n + 3 + c)
                    nc.scalar.activation(pc[:, c], pc[:, c], ACT.Exp).then_inc(sC["exp_done"], 1)

                if live(i, u):
                    weights(0)
                    weights(1)
                if live(i, u + 1):
                    exponentials(0)
                if live(i, u + 2):
                    evac_xT(i, u + 2)
                    evac_qc(i, u + 2)
                if live(i, u + 1):
                    exponentials(1)
                if isinstance(i, int) and n == 0:
                    act.wait_ge(sD["we_in"], 32)
                if live(i, u):
                    cols = bass.ds(2 * WCOLS * i + WCOLS * u, WCOLS)
                    nc.scalar.activation(we_hi[:, cols], we[:, cols], ACT.Copy).then_inc(sD["we_hi"], 1)

            pipeline(act, body)

            def evac_xT(i, s):
                m = 2 * i + s
                wait(act, sD["xT_ps"], m + 1)
                wait(act, sD["lg_ps"], m - 1)
                wait(act, sD["lo"], m - 1)
                nc.scalar.activation(xnT[:, s % 2], ps[:, 4, 0:D].rearrange("p (k q) -> p k q", k=DK), ACT.Copy).then_inc(sD["xT_sb"], 1)
                wait(act, sD["xT_sb"], m + 1)
                wait(act, sD["e_ps"], 4 * m - 4)
                nc.scalar.activation(xhi[:, s % 2], xnT[:, s % 2], ACT.Copy).then_inc(sD["hi"], 1)

            evac_xT(0, 0)

            def body(i, u):
                n = 2 * i + u
                if live(i, u + 1):
                    wait(act, sD["diff"], n + 2)
                    nc.scalar.activation(gd[:, 1 - u, 1:2], gd[:, 1 - u, 0:1], ACT.Exp).then_inc(sD["exp"], 1)
                if live(i, u + 2):
                    evac_xT(i, u + 2)
                if live(i, u):
                    wait(act, sD["e_ps"], 4 * n + 4)
                    wait(act, sD["y_ready"], n - 1)
                    for a in range(EA):
                        e = E - EA + a
                        last = nc.scalar.activation(part[:, u, a], ps[:, e // 2, D * (e % 2):D * (e % 2) + D], ACT.Copy, scale=gates[:, u, e:e + 1])
                    last.then_inc(sD["scaled"], 1)
                if live(i, u + 1):
                    wait(act, sD["gT_ps"], n + 2)
                    wait(act, sD["be_ps"], n)
                    nc.scalar.activation(gatesT[:, 1 - u, :], ps[0:E, 6, 0:P], ACT.Copy).then_inc(sD["gT_sb"], 1)

            pipeline(act, body)

        @block.vector
        def _(dve):
            dve.wait_ge(sA["ctxT_ps"], 1)
            nc.vector.tensor_copy(ctxT[:], ps[:, 6, 0:DK * B * LK].rearrange("p (k b q) -> p k b q", k=DK, b=B)).then_inc(sA["ctxT_sb"], 1)
            dve.wait_ge(sA["ctxT_sb"], 1)
            for k in range(DK):
                last = nc.vector.tensor_copy(ctx_rep[:, k], bcast(ctxT[:, k], 2, HC))
            last.then_inc(sA["rep_ready"], 1)
            def normalise(i, s):
                b, j = tile_at(i, s)
                n = 2 * i + s
                wait(dve, sA["xT_ps"], n - 1)
                jj = bass.ds(j, 1)
                nc.vector.tensor_scalar(xn[:, b], x[:, b, jj, :], mv[:, b, jj, 0:1], rstd[:, b, jj],
                                        ALU.subtract, ALU.mult).then_inc(sA["xn_ready"], 1)

            def keep_stats(i, s):
                b, j = tile_at(i, s)
                nc.vector.tensor_copy(st_all[:, b, bass.ds(j, 1), :].squeeze(1), stats[:, b]).then_inc(sA["stats_kept"], 1)

            def input_stats(g):
                dve.wait_ge(x_in[g], 32)
                for j in range(4 * g, 4 * g + 4):
                    for b in range(B):
                        last = nc.vector.bn_stats(st_all[:, b, j], x[:, b, j, :])
                last.then_inc(sA["stats"], 1)

            def input_means(g):
                dve.wait_ge(sA["stats"], g + 1)
                for j in range(4 * g, 4 * g + 4):
                    for b in range(B):
                        last = nc.vector.bn_aggr(mv[:, b, j], st_all[:, b, j])
                last.then_inc(sA["aggr"], 1)

            def add_value_bias(g):
                dve.wait_ge(sA["kv_ps"], g + 2)
                for q in range(4):
                    b, c, j = v_unit(4 * g + q)
                    last = nc.vector.tensor_tensor(VTMP[g][0:rows(j), q], ps[0:rows(j), g, P * q:P * q + P], bv[0:rows(j), P * c:P * c + P], ALU.add)
                last.then_inc(sA["kv_sb"], 1)

            dve.wait_ge(k_in, 48)
            dve.wait_ge(sA["kv_ps"], 1)
            for c in range(2):
                last = nc.vector.tensor_scalar(kT[:, c], ps[:, 7, 2 * LK * c:2 * LK * (c + 1)].rearrange("p (b k) -> p b k", b=B),
                                               bk[:, c:c + 1], HD ** -0.5, ALU.add, ALU.mult)
            last.then_inc(sA["kv_sb"], 1)
            dve.wait_ge(sA["kv_sb"], 1)
            for c in range(2):
                for b in range(B):
                    last = nc.vector.tensor_tensor(kbd[:, b, c], bcast(kT[:, c, b], 1, HC), bcast(kmask[:], 2, LK), ALU.mult)
            last.then_inc(sA["kbd_ready"], 1)
            input_stats(0)
            input_means(0)
            dve.wait_ge(v_in, 48)
            add_value_bias(0)
            add_value_bias(1)
            dve.wait_ge(sA["rstd"], 2)
            normalise(0, 0)
            for g in range(2, 5):
                add_value_bias(g)
            dve.wait_ge(sA["vbd_ready"], 3)

            def body(i, u):
                n = 2 * i + u
                def maximum(c):
                    wait(dve, sA["s_ps"], 2 * n + 3 + c)
                    nc.vector.tensor_reduce(nmax[:, c], S_(c), AX.X, ALU.max).then_inc(sA["max_done"], 1)

                def subtract(c):
                    wait(dve, sA["max_done"], 2 * n + 3 + c)
                    wait(dve, sA["ptb_ps"], 2 * n + 1 + c)
                    nc.vector.tensor_tensor(pr[:, c].rearrange("p (a h) k -> p a h k", a=2), S_(c),
                                            bcast(nmax[:, c].rearrange("p (a h) -> p a h", a=2), 3, LK),
                                            ALU.subtract).then_inc(sA["sub_done"], 1)

                if live(i, u - 1):
                    wait(dve, sA["o_ps"], n)
                    wait(dve, sA["stats2"], n - 1)
                    nc.vector.reciprocal(rsum[:], O_[:, :, :, HD]).then_inc(sA["rsum_done"], 1)
                    wait(dve, sA["rsum_done"], n)
                    wait(dve, sA["oT_ps"], n - 1)
                    nc.vector.tensor_tensor(on[:], O_[:, :, :, 0:HD], bcast(rsum[:], 3, HD), ALU.mult).then_inc(sA["on_ready"], 1)
                if live(i, u - 2):
                    keep_stats(i, u - 2)
                if isinstance(i, int) and n == 0:
                    dve.wait_ge(sA["rstd"], 3)
                    input_means(1)
                if isinstance(i, int) and n == 1:
                    dve.wait_ge(sA["rstd"], 5)
                if live(i, u + 2):
                    normalise(i, u + 2)
                if live(i, u + 1):
                    maximum(0)
                    subtract(0)
                    maximum(1)
                if live(i, u - 1):
                    b, j = tile_at(i, u - 1)
                    jj = bass.ds(j, 1)
                    wait(dve, sA["out_ps"], n)
                    wait(dve, sA["xo_ready"], n)
                    wait(dve, sA["x1_kept"], n - 1)
                    nc.vector.tensor_tensor(xs[:, b], x[:, b, jj, :].squeeze(1), OUT, ALU.add).then_inc(sA["x1_ready"], 1)
                if live(i, u + 1):
                    subtract(1)
                if live(i, u - 1):
                    wait(dve, sA["x1_ready"], n)
                    wait(dve, sA["stats_kept"], n - 1)
                    nc.vector.bn_stats(stats[:, b], xs[:, b]).then_inc(sA["stats2"], 1)
                    nc.vector.tensor_copy(x[:, b, jj, :].squeeze(1), xs[:, b]).then_inc(sA["x1_kept"], 1)
                if isinstance(i, int) and n == -1:
                    input_stats(1)

            pipeline(dve, body)

            dve.wait_ge(sA["stats2"], NT)
            keep_stats(TPB - 1, 1)
            dve.wait_ge(sA["stats_kept"], NT)
            for b in range(B):
                for j in range(TPB):
                    nc.vector.bn_aggr(mv[:, b, j], st_all[:, b, j]).then_inc(sA["aggr2"], 1)

            links = [0]

            def then(ins):
                links[0] += 1
                ins.then_inc(sB["chain"], 1)
                dve.wait_ge(sB["chain"], links[0])

            dve.wait_ge(c_w, CW * 16)
            tmp = chhot[:].rearrange("p t c -> p (t c)")[:, 0:NT * LK].rearrange("p (t k) -> p t k", t=NT)
            then(nc.vector.tensor_copy(seg[:, 0], seg_i[:]))
            nc.vector.tensor_tensor(negm[:], bcast(iok[:], 1, NT), bcast(seg[:, 0], 2, LK), ALU.is_gt)
            then(nc.vector.tensor_scalar(seg[:, 1], seg[:, 0], 2.0, None, ALU.subtract))

            def normalise2(i, r):
                n = RING * i + r
                u, j = r % 2, (RING // 2) * i + r // 2
                jj = bass.ds(j, 1)
                wait(dve, sB["xT_ps"], n - RING + 1)
                wait(dve, stored[r], 16 * i)
                nc.vector.tensor_scalar(xng[:, r], x[:, u, jj, :], mv[:, u, jj, 0:1], rstd[:, u, jj],
                                        ALU.subtract, ALU.mult).then_inc(sB["xn_ready"], 1)

            def logits(i, r):
                n = RING * i + r
                u, j = r % 2, (RING // 2) * i + r // 2
                wait(dve, sB["lg_ps"], n + 1)
                nc.vector.tensor_scalar(lg[:, u, bass.ds(P * j, P)], ps[0:E, 4 + u, 0:P], gb[:, 0:1], None, ALU.add).then_inc(sB["lg_sb"], 1)

            dve.wait_ge(g_in, 32)
            dve.wait_ge(sB["rstd"], 2)
            for r in range(RING):
                if r == B:
                    dve.wait_ge(sB["rstd"], 3)
                normalise2(0, r)
            with dve.Fori(1, NT // RING) as i:
                for r in range(RING):
                    logits(i - 1, r)
                    normalise2(i, r)
            for r in range(RING):
                logits(NT // RING - 1, r)
            dve.wait_ge(sB["lg_sb"], NT)
            then(nc.vector.tensor_reduce(gmax[:], lg[:], AX.X, ALU.max, negate=True))
            then(nc.vector.tensor_tensor(tmp, bcast(iok[:], 1, NT), bcast(seg[:, 1], 2, LK), ALU.is_lt))
            dve.wait_ge(sB["gexp"], 2)
            then(nc.vector.reciprocal(gsum[:], gsum[:]))
            for b in range(B):
                last = nc.vector.tensor_scalar(lg[:, b], lg[:, b], gsum[:, b:b + 1], None, ALU.mult)
            then(last)
            dve.wait_ge(sB["const"], 112)
            dve.wait_ge(sB["pT_ps"], 1)
            then(nc.vector.tensor_copy(prob[:], ps[:, 4, 0:NT * E].rearrange("p (t e) -> p t e", e=E)))
            src = prob
            for k in range(TOP):
                then(nc.vector.tensor_reduce(top[:, k], src[:], AX.X, ALU.max))
                then(nc.vector.tensor_tensor(key[:], src[:], bcast(top[:, k], 2, E), ALU.is_equal))
                then(nc.vector.tensor_tensor(key[:], key[:], bcast(rev8[:], 1, NT), ALU.mult))
                then(nc.vector.tensor_reduce(kmax[:], key[:], AX.X, ALU.max))
                then(nc.vector.tensor_tensor(oneh[:, k], bcast(rev8[:], 1, NT), bcast(kmax[:], 2, E), ALU.is_equal))
                if k == 0:
                    then(nc.vector.scalar_tensor_tensor(prob2[:], oneh[:, 0], -2.0, prob[:], ALU.mult, ALU.add))
                    src = prob2
            nc.vector.tensor_tensor(sel[:], oneh[:, 0], oneh[:, 1], ALU.add).then_inc(sB["route_ready"], 1)
            then(nc.vector.tensor_tensor(negm[:], negm[:], tmp, ALU.add))
            nc.vector.tensor_scalar(negm[:], negm[:], FMIN, None, ALU.mult)
            dve.wait_ge(sB["rank_ps"], 1)
            rank = ps[:, 5, 0:(NT + 1) * E].rearrange("p (t e) -> p t e", e=E)
            then(nc.vector.tensor_copy(base[:], rank[:, NT, :]))
            then(nc.vector.tensor_scalar(cmp16[:, 0], iot[:, 0:NT], float(P), None, ALU.mult))
            then(nc.vector.tensor_copy(kmax[:], cmp16[:, 0]))
            then(nc.vector.tensor_tensor(cmp16[:], bcast(base[:], 2, NT), bcast(kmax[:], 1, E), ALU.is_gt))
            then(nc.vector.tensor_reduce(nch[:], cmp16[:], AX.X, ALU.add))
            then(nc.vector.tensor_tensor(tri8[:], tri8[:], bcast(nch[:], 1, E), ALU.mult))
            then(nc.vector.tensor_reduce(cend[:], tri8[:], AX.X, ALU.add))
            then(nc.vector.tensor_tensor(base[:], cend[:], nch[:], ALU.subtract))
            then(nc.vector.tensor_scalar(base[:], base[:], float(P), None, ALU.mult))
            then(nc.vector.tensor_tensor(pos[:], rank[:, 0:NT, :], bcast(base[:], 1, NT), ALU.add))
            for k in range(TOP):
                then(nc.vector.tensor_tensor(key[:], oneh[:, k], pos[:], ALU.mult))
                then(nc.vector.tensor_reduce(slot[:, NT * k:NT * k + NT], key[:], AX.X, ALU.add))
            then(nc.vector.tensor_copy(slot_i[:, 0], slot[:]))
            nc.vector.tensor_scalar(slot_i[:, 1], slot_i[:, 0], P - 1, None, ALU.bitwise_and)
            then(nc.vector.tensor_scalar(slot_i[:, 2], slot_i[:, 0], P.bit_length() - 1, None, ALU.logical_shift_right))
            then(nc.vector.tensor_copy(rc[:], slot_i[:, 1:3]))
            then(nc.vector.tensor_tensor(chhot[:], bcast(rc[:, 1], 2, NCH), bcast(iot[:, 0:NCH], 1, TOP * NT), ALU.is_equal))
            hot = chhot[:].rearrange("p (k t) c -> p k t c", k=TOP)
            pay = payload[:].rearrange("p (k t) v c -> p k t v c", k=TOP)
            for r in range(RING):
                dve.wait_ge(stored[r], 16 * NT // RING)
            for k in range(TOP):
                nc.vector.tensor_tensor(pay[:, k, :, 0, :], hot[:, k], bcast(tokid[:], 2, NCH), ALU.mult)
                nc.vector.tensor_tensor(pay[:, k, :, 1, :], hot[:, k], bcast(top[:, k], 2, NCH), ALU.mult).then_inc(sB["payload"], 1)
            for g in range(4):
                a = slice(8 * g, 8 * g + 8)
                if g >= 2:
                    dve.wait_ge(sB["rowhot_used"], g - 1)
                nc.vector.tensor_tensor(rowhot[:, g % 2], bcast(rc[:, 0, a], 2, P), bcast(iot[:], 1, 8), ALU.is_equal).then_inc(sB["rowhot"], 1)
            then(nc.vector.tensor_tensor(cmp8[:], bcast(iot[:, 0:NCH], 2, E), bcast(cend[:], 1, NCH), ALU.is_ge))
            then(nc.vector.tensor_reduce(ce[:], cmp8[:], AX.X, ALU.add))
            then(nc.vector.tensor_scalar(ce[:], ce[:], float(E - 1), None, ALU.min))
            then(nc.vector.tensor_copy(ce_i[:], ce[:]))
            dve.wait_ge(sB["rowhot_used"], 4)
            nc.vector.tensor_copy(tok_i[:], ps[:, 6, 0:NCH]).then_inc(sB["tok_ready"], 1)
            nc.vector.tensor_copy(wslot[:], ps[:, 6, NCH:2 * NCH]).then_inc(sB["route_ready"], 1)
            dve.wait_ge(sB["route_ready"], 2)

            def expert_of(it, s):
                return nc.vector.value_load(ce_i[0:1, bass.ds(NSTR * it + s, 1)], min_val=0, max_val=E - 1)

            def add_bias(it, k, e):
                l, s = k // NSTR, k % NSTR
                dve.wait_ge(sB["l_ps"], STEPS * it + k + 1)
                nc.vector.tensor_tensor(h0[:, s], ps[:, s, D:2 * D], b0[:, l, bass.ds(e, 1), :].squeeze(1), ALU.add).then_inc(sB["l_sb"], 1)

            def weigh(it, s):
                dve.wait_ge(sB["l_sb"], STEPS * it + STEPS - NSTR + s + 1)
                nc.vector.tensor_scalar(y0[:, s], h0[:, s], 0.0, wslot[:, bass.ds(NSTR * it + s, 1)], ALU.max, ALU.mult).then_inc(sB["y_ready"], 1)

            def gather_sum(it, s, e):
                dve.wait_ge(sB["y_ready"], NSTR * it + s + 1)
                wait(dve, sB["v_done"], NSTR * it + s)
                at_e = vsum[:, bass.ds(e[s], 1), :].squeeze(1)
                nc.vector.tensor_tensor(at_e, at_e, y0[:, s], ALU.add).then_inc(sB["v_done"], 1)

            def chunks(it):
                if isinstance(it, int):
                    dve.wait_ge(sB["vsum_zero"], 1)
                e = []
                for k in range(STEPS):
                    if k < NSTR:
                        e.append(expert_of(it, k))
                    if isinstance(it, int) and k % NSTR == 0:
                        dve.wait_ge(b0_in[k // NSTR], 16)
                    add_bias(it, k, e[k % NSTR])
                    if k > STEPS - NSTR:
                        gather_sum(it, k - 1 - (STEPS - NSTR), e)
                    if k >= STEPS - NSTR:
                        weigh(it, k - (STEPS - NSTR))
                gather_sum(it, NSTR - 1, e)

            chunks(0)
            with dve.Fori(1, NIT) as it:
                chunks(it)
            dve.wait_ge(sB["v_sb"], 1)
            nc.vector.tensor_tensor(v0_lo[:], ps[0:E, 5, 0:D], v0_hi[:], ALU.subtract).then_inc(sB["v_sb"], 1)

            def pair_stats(m):
                b, j = 2 * m // TPB, 2 * m % TPB
                for q in range(2):
                    last = nc.vector.bn_stats(st_all[:, b, j + q], x[:, b, j + q, :])
                last.then_inc(sB["stats"], 1)

            def means(js, count):
                dve.wait_ge(sB["stats"], count)
                for j in js:
                    for b in range(B):
                        last = nc.vector.bn_aggr(mv[:, b, j], st_all[:, b, j])
                last.then_inc(sB["aggr"], 1)

            def normalise3(i, s):
                n = 2 * i + s
                b, j = tile_at(i, s)
                jj = bass.ds(j, 1)
                wait(dve, sC["xT_ps"], n - 1)
                nc.vector.tensor_scalar(xn[:, b], x[:, b, jj, :], mv[:, b, jj, 0:1], rstd[:, b, jj],
                                        ALU.subtract, ALU.mult).then_inc(sC["xn_ready"], 1)

            for k, m in enumerate(PAIRS):
                b, j = 2 * m // TPB, 2 * m % TPB
                dve.wait_ge(sB["o_ps"], k + 1)
                nc.vector.tensor_tensor(x[:, b, j:j + 2, :], x[:, b, j:j + 2, :], ps[:, k % 4, :].rearrange("p (t d) -> p t d", t=2), ALU.add).then_inc(sB["x2_ready"], 1)
                if k:
                    dve.wait_ge(sB["x2_ready"], k)
                    pair_stats(PAIRS[k - 1])
                if k == 2:
                    means((0, 1), 2)
                if k == 4:
                    dve.wait_ge(sC["rstd"], 2)
                    normalise3(0, 0)
            dve.wait_ge(sB["x2_ready"], NT // 2)
            pair_stats(PAIRS[-1])
            means(range(2, TPB), NT // 2)

            def normalise4(i, s):
                n = 2 * i + s
                b, j = tile_at(i, s)
                jj = bass.ds(j, 1)
                wait(dve, sD["xT_ps"], n - 1)
                nc.vector.tensor_scalar(xn[:, b], x[:, b, jj, :], mv[:, b, jj, 0:1], rstd[:, b, jj],
                                        ALU.subtract, ALU.mult).then_inc(sD["xn_ready"], 1)

            EARLY = 2

            def aggregate(n0, n1):
                for n in range(n0, n1):
                    nc.vector.bn_aggr(mv[:, n % 2, n // 2], st_all[:, n % 2, n // 2]).then_inc(sD["aggr"], 1)

            def body(i, u):
                n = 2 * i + u

                def rotate(g):
                    b, j = tile_at(i, u + 1)
                    wait(dve, sC["rope_ps"], 4 * (n + 1) + g + 1)
                    wait(dve, sC["s_ps"], 2 * n + 1 + g // 2)
                    nc.vector.tensor_tensor(rot[:, g], bcast(ROPE[g % 2].rearrange("p (h q) -> p h q", h=2), 1, 2),
                                            bcast(trig[:, :, bass.ds(P * j, P)], 2, 2), ALU.mult).then_inc(sC["rot_ready"], 1)

                def mask(c):
                    b, j = tile_at(i, u + 1)
                    m = 2 * (n + 1) + c + 1
                    wait(dve, sC["s_ps"], m)
                    wait(dve, sC["ptb_ps"], m - 2)
                    nc.vector.tensor_tensor(pc[:, c].rearrange("p (a h) k -> p a h k", a=2), S_(c),
                                            negm[:, bass.ds(TPB * b + j, 1), :].unsqueeze(1).broadcast_to([P, 2, 4, LK]),
                                            ALU.add).then_inc(sC["mask_done"], 1)
                    wait(dve, sC["mask_done"], m)
                    nc.vector.tensor_reduce(pmax[:, c], pc[:, c], AX.X, ALU.max).then_inc(sC["max_done"], 1)

                def total(m, c):
                    k = 2 * m + c + 1
                    wait(dve, sC["exp_done"], k)
                    wait(dve, sC["norm_done"], k - 2)
                    nc.vector.tensor_reduce(psm[:, c], pc[:, c], AX.X, ALU.add).then_inc(sC["sum_done"], 1)
                    wait(dve, sC["sum_done"], k)
                    nc.vector.reciprocal(psm[:, c], psm[:, c]).then_inc(sC["rsum_done"], 1)

                def weights_lo(c):
                    m = 2 * n + c + 1
                    wait(dve, sC["pta_ev"], m)
                    nc.vector.tensor_tensor(pcT_lo[:, c, 0:3, :], PTA, pcT_hi[:, c, 0:3, :], ALU.subtract)
                    wait(dve, sC["ptb_ev"], m)
                    nc.vector.tensor_tensor(pcT_lo[:, c, 3, :], PTB[:, 0], pcT_hi[:, c, 3, :], ALU.subtract)
                    r = rows(4)
                    nc.vector.tensor_tensor(pcT_lo[0:r, c, 4, :], PTB[0:r, 1], pcT_hi[0:r, c, 4, :], ALU.subtract).then_inc(sC["lo_done"], 1)

                if isinstance(i, int) and n == NT - 1:
                    dve.wait_ge(sC["stats"], NT - EARLY)
                    aggregate(0, NT - EARLY)
                if live(i, u + 1):
                    rotate(0)
                if live(i, u):
                    total(n, 1)
                if isinstance(i, int) and n == 0:
                    dve.wait_ge(sC["rstd"], 4)
                if live(i, u + 2):
                    normalise3(i, u + 2)
                if live(i, u + 1):
                    rotate(1)
                if live(i, u):
                    weights_lo(0)
                if isinstance(i, int) and n in (-1, 0):
                    dve.wait_ge(sC["const_hi"], n + 3)
                    for lo, whole, hi in zip(vw_parts(vw_lo, n + 1), vw_parts(vw, n + 1), vw_parts(vw_hi, n + 1)):
                        last = nc.vector.tensor_tensor(lo, whole, hi, ALU.subtract)
                    last.then_inc(sC["vw_lo"], 1)
                if live(i, u + 1):
                    rotate(2)
                    mask(0)
                    rotate(3)
                if live(i, u):
                    weights_lo(1)
                if live(i, u + 1):
                    total(n + 1, 0)
                    if live(i, u - 1):
                        wait(dve, sC["x_ready"], n)
                    mask(1)
                if live(i, u - 1):
                    if not live(i, u + 1):
                        wait(dve, sC["x_ready"], n)
                    bb, j = tile_at(i, u - 1)
                    jb = bass.ds(j, 1)
                    nc.vector.bn_stats(st_all[:, bb, jb, :].squeeze(1), x[:, bb, jb, :].squeeze(1)).then_inc(sC["stats"], 1)
                if isinstance(i, int) and n == NT - 1:
                    dve.wait_ge(sD["rstd"], 2)
                    normalise4(0, 0)
                if live(i, u):
                    b, j = tile_at(i, u)
                    jj = bass.ds(j, 1)
                    wait(dve, sC["out_ps"], n + 1)
                    nc.vector.tensor_tensor(x[:, b, jj, :].squeeze(1), x[:, b, jj, :].squeeze(1), ps[:, 7, 0:D], ALU.add).then_inc(sC["x_ready"], 1)

            pipeline(dve, body)
            dve.wait_ge(sC["stats"], NT)
            aggregate(NT - EARLY, NT)

            dve.wait_ge(sD["w_in"], 48)
            def body(i, u):
                n = 2 * i + u
                v = 1 - u
                step = [0]

                def link(ins):
                    step[0] += 1
                    ins.then_inc(sD["chain"], 1)

                def linked():
                    wait(dve, sD["chain"], LINKS * (n + 1) + step[0])

                def weigh(e):
                    if live(i, u):
                        if e % 2 == 0:
                            wait(dve, sD["e_ps"], 4 * n + e // 2 + 1)
                        wait(dve, sD["acc"], ACCS * n + e + 1)
                        nc.vector.scalar_tensor_tensor(acc[:, u], ps[:, e // 2, D * (e % 2):D * (e % 2) + D], gates[:, u, e:e + 1], acc[:, u],
                                                       ALU.mult, ALU.add).then_inc(sD["acc"], 1)

                ahead = live(i, u + 1)
                if isinstance(i, int) and n == 0:
                    dve.wait_ge(sD["rstd"], 3)
                if isinstance(i, int) and n == 1:
                    dve.wait_ge(sD["rstd"], 5)
                if ahead:
                    wait(dve, sD["lg_ps"], n + 2)
                    link(nc.vector.tensor_copy(lt[:, v], ps[:, 5, 0:E]))
                if live(i, u + 2):
                    if ahead:
                        linked()
                    normalise4(i, u + 2)
                elif ahead:
                    linked()
                if ahead:
                    link(nc.vector.max(lmax[:, v], lt[:, v]))
                    linked()
                    nc.vector.tensor_tensor(gd[:, v, 0:1], lmax[:, v, 1:2], lmax[:, v, 0:1], ALU.subtract).then_inc(sD["diff"], 1)
                    link(nc.vector.max_index(lidx[:, v], lmax[:, v], lt[:, v]))
                if live(i, u):
                    b, j = tile_at(i, u)
                    jj = bass.ds(j, 1)
                    wait(dve, sD["be_ps"], n + 1)
                    nc.vector.tensor_tensor(acc[:, u], x[:, b, jj, :].squeeze(1), ps[:, 7, 0:D], ALU.add).then_inc(sD["acc"], 1)
                if ahead:
                    linked()
                    link(nc.vector.tensor_copy(lidf[:, v], lidx[:, v, 0:TOP]))
                weigh(0)
                if ahead:
                    wait(dve, sD["exp"], n + 2)
                    nc.vector.tensor_scalar(gt[:, v, 0:1], gd[:, v, 1:2], 1.0, None, ALU.add).then_inc(sD["chain2"], 1)
                    linked()
                    link(nc.vector.tensor_tensor(goh[:, v], bcast(iot8[:], 1, TOP), bcast(lidf[:, v], 2, E), ALU.is_equal))
                    wait(dve, sD["chain2"], 2 * (n + 1) + 1)
                    nc.vector.reciprocal(gt[:, v, 0:1], gt[:, v, 0:1]).then_inc(sD["chain2"], 1)
                weigh(1)
                if live(i, u - 1):
                    wait(dve, sD["summed"], n)
                    wait(dve, sD["acc"], ACCS * n)
                    wait(dve, written[v], (16 * i - 16) if u == 0 else 16 * i)
                    nc.vector.tensor_tensor(y[:, v], acc[:, v], part[:, v, 0], ALU.add).then_inc(sD["y_ready"], 1)
                if ahead:
                    wait(dve, sD["chain2"], 2 * (n + 1) + 2)
                    link(nc.vector.tensor_tensor(gt[:, v, 1:2], gt[:, v, 0:1], gd[:, v, 1:2], ALU.mult))
                weigh(2)
                if ahead:
                    linked()
                    link(nc.vector.tensor_tensor(goh[:, v], goh[:, v], bcast(gt[:, v], 2, E), ALU.mult))
                weigh(3)
                if ahead:
                    linked()
                    wait(dve, sD["gT_ps"], n)
                    wait(dve, sD["scaled"], n)
                    link(nc.vector.tensor_tensor(gates[:, v], goh[:, v, 0], goh[:, v, 1], ALU.add))
                weigh(4)
                weigh(5)
                if isinstance(i, int) and ahead:
                    assert step[0] == LINKS
                if ahead:
                    linked()

            pipeline(dve, body, first=2)

        @block.tensor
        def _(pe):
            pe.wait_ge(c_in, 32)
            for k in range(DK):
                for b in range(B):
                    last = nc.tensor.transpose(ps[:, 6, (2 * k + b) * LK:(2 * k + b + 1) * LK], ctx[:, b, P * k:P * k + P], ident[0:LK, 0:LK])
            last.then_inc(sA["ctxT_ps"], 1)
            pe.wait_ge(sA["ctxT_sb"], 1)
            pe.wait_ge(k_in, 48)
            for c in range(2):
                for k in range(DK):
                    last = nc.tensor.matmul(ps[:, 7, 2 * LK * c:2 * LK * (c + 1)], wk[:, k, P * c:P * c + P], ctxT[:, k],
                                            start=k == 0, stop=k == DK - 1)
            last.then_inc(sA["kv_ps"], 1)
            pe.wait_ge(sA["rep_ready"], 1)
            pe.wait_ge(v_in, 48)
            for g in range(5):
                for q in range(4):
                    b, c, j = v_unit(4 * g + q)
                    for k in range(DK):
                        last = nc.tensor.matmul(ps[0:rows(j), g, P * q:P * q + P],
                                                ctx_rep[:, k, b].rearrange("p h k -> p (h k)")[:, P * j:P * j + rows(j)],
                                                wv[:, k, P * c:P * c + P], start=k == 0, stop=k == DK - 1)
                last.then_inc(sA["kv_ps"], 1)
            pe.wait_ge(q_in, 64)

            def transpose_tile(i, s):
                m = 2 * i + s
                wait(pe, sA["xn_ready"], m + 1)
                wait(pe, sA["oT_sb"], m - 2)
                wait(pe, sA["q_ready"], m)
                for k in range(DK):
                    last = nc.tensor.transpose(XT[:, k], xn[:, s % 2, P * k:P * k + P], ident[:])
                last.then_inc(sA["xT_ps"], 1)

            def queries(i, s):
                wait(pe, sA["xT_sb"], 2 * i + s + 1)
                for c in range(2):
                    for k in range(DK):
                        last = nc.tensor.matmul(QT[:, c], wq[:, k, P * c:P * c + P], xnT[:, s % 2, k, :], start=k == 0, stop=k == DK - 1)
                last.then_inc(sA["q_ps"], 1)

            transpose_tile(0, 0)
            queries(0, 0)
            pe.wait_ge(sA["kbd_ready"], 1)
            pe.wait_ge(sA["kv_sb"], 6)

            def body(i, u):
                n = 2 * i + u

                def transpose_weights(c):
                    flat = pr[:, c].rearrange("p h k -> p (h k)")
                    wait(pe, sA["exp_done"], 2 * n + c + 1)
                    wait(pe, sA["pta_ev"], 2 * n + c)
                    for j in range(3):
                        last = nc.tensor.transpose(PTA[:, j], flat[:, P * j:P * j + P], ident[:])
                    last.then_inc(sA["pta_ps"], 1)
                    wait(pe, sA["ptb_ev"], 2 * n + c)
                    nc.tensor.transpose(PTB[:, 0], flat[:, 3 * P:4 * P], ident[:])
                    nc.tensor.transpose(PTB[0:rows(4), 1], flat[:, 4 * P:UK], ident[:]).then_inc(sA["ptb_ps"], 1)

                def apply_weights(c):
                    wait(pe, sA["ptb_ev"], 2 * n + c + 1)
                    for j in range(NJ):
                        h0, nh = heads_of(j)
                        last = nc.tensor.matmul(O_[:, c, h0:h0 + nh, :].rearrange("p h v -> p (h v)"), prT[0:rows(j), c, j, :],
                                                vbd[0:rows(j), u, c, j, h0:h0 + nh, :].rearrange("p h v -> p (h v)"),
                                                start=j == 0 and c == 0, stop=j == NJ - 1, skip_group_check=True)
                    return last

                def scores(c):
                    wait(pe, sA["sub_done"], 2 * n + c + 1)
                    for a in range(2):
                        last = nc.tensor.matmul(ps[:, 2 * c + a, 0:4 * LK], qT[:, 1 - u, c, :],
                                                kbd[:, 1 - u, c, 4 * a:4 * a + 4, :].rearrange("p h k -> p (h k)"), start=True, stop=True)
                    last.then_inc(sA["s_ps"], 1)

                if live(i, u + 1):
                    wait(pe, sA["q_ready"], n + 2)
                    scores(0)
                if live(i, u):
                    transpose_weights(0)
                if live(i, u - 1):
                    wait(pe, sA["on_ready"], n)
                    for c in range(2):
                        last = nc.tensor.transpose(OT[:, c], on[:, c].rearrange("p h d -> p (h d)"), ident[:])
                    last.then_inc(sA["oT_ps"], 1)
                if live(i, u + 1):
                    scores(1)
                if live(i, u + 2):
                    transpose_tile(i, u + 2)
                if live(i, u - 1):
                    wait(pe, sA["oT_sb"], n)
                    for c in range(2):
                        last = nc.tensor.matmul(OUT, oT[:, c, :], wo[:, c, :], start=c == 0, stop=c == 1)
                    last.then_inc(sA["out_ps"], 1)
                if live(i, u):
                    transpose_weights(1)
                if live(i, u + 2):
                    queries(i, u + 2)
                if isinstance(i, int) and n == 0:
                    pe.wait_ge(sA["vbd_ready"], 5)
                    pe.wait_ge(sA["ones_ready"], 1)
                if live(i, u):
                    wait(pe, sA["x1_ready"], n)
                    apply_weights(0)
                    apply_weights(1).then_inc(sA["o_ps"], 1)

            pipeline(pe, body)

            pe.wait_ge(sA["x1_ready"], NT)
            pe.wait_ge(c_w, CW * 16)
            for k in range(DK):
                last = nc.tensor.matmul(ps[0:DC, 7, 0:B * LK], wkvc[:, k, :], ctxT[:, k], start=k == 0, stop=k == DK - 1)
            last.then_inc(sC["kvc_ps"], 1)
            pe.wait_ge(sC["kvc_sb"], 1)
            for q in range(NP2):
                last = nc.tensor.matmul(ps[:, q // 3, (q % 3) * B * LK:(q % 3 + 1) * B * LK], wkup[:, P * q:P * q + P], kvcT, start=True, stop=True)
                if q % 3 == 2 or q == NP2 - 1:
                    last.then_inc(sC["kn_ps"], 1)
            for v in range(2):
                last = nc.tensor.matmul(ps[:, 3, v * B * LK:(v + 1) * B * LK], wkr[:, v, :], kvcT, start=True, stop=True)
            last.then_inc(sC["kr_ps"], 1)
            pe.wait_ge(g_in, 32)
            pe.wait_ge(sC["kn_sb"], 3)
            pe.wait_ge(sC["kr_sb"], 1)

            def transpose_tile(i, r):
                n = RING * i + r
                wait(pe, sB["xn_ready"], n + 1)
                wait(pe, sB["xT_sb"], n - RING + 1)
                for k in range(DK):
                    last = nc.tensor.transpose(ps[:, r, P * k:P * k + P], xng[:, r, P * k:P * k + P], ident[:])
                last.then_inc(sB["xT_ps"], 1)

            def gate(i, r):
                n = RING * i + r
                wait(pe, sB["xT_sb"], n + 1)
                wait(pe, sB["lg_sb"], n - 1)
                for k in range(DK):
                    last = nc.tensor.matmul(ps[0:E, 4 + r % 2, 0:P], gw[:, k, :], xnT[:, r % 2, k, :], start=k == 0, stop=k == DK - 1)
                last.then_inc(sB["lg_ps"], 1)

            AHEAD = RING - 2
            for r in range(AHEAD):
                transpose_tile(0, r)

            def body(i, live_next=True):
                for r in range(RING):
                    if r + AHEAD < RING:
                        transpose_tile(i, r + AHEAD)
                    elif live_next:
                        transpose_tile(i + 1, r + AHEAD - RING)
                    gate(i, r)

            body(0)
            with pe.Fori(1, NT // RING - 1) as i:
                body(i)
            body(NT // RING - 1, live_next=False)
            for g in range(6):
                if g >= 2:
                    pe.wait_ge(sC["a_sb"], g - 1)
                r = slice(RD * (g % 2), RD * (g % 2) + RD)
                for q in range(3 * (g // 2), min(3 * (g // 2) + 3, NP2)):
                    last = nc.tensor.matmul(ps[0:DQ, g % 2, (q % 3) * B * LK:(q % 3 + 1) * B * LK], wqupT[r, q, :],
                                            knT[r, q].rearrange("p b k -> p (b k)"), start=True, stop=True)
                last.then_inc(sC["a_ps"], 1)
            pe.wait_ge(sB["chain"], 6)
            for t in range(NT):
                b, j = t // TPB, t % TPB
                last = nc.tensor.transpose(ps[:, 4, E * t:E * t + E], lg[:, b, P * j:P * j + P], ident[0:E, 0:E])
            last.then_inc(sB["pT_ps"], 1)
            for q in range(NP2):
                last = nc.tensor.matmul(ps[:, VBANK[q // 3], (q % 3) * B * LK:(q % 3 + 1) * B * LK], wvup[:, P * q:P * q + P], kvcT, start=True, stop=True)
                if q % 3 == 2 or q == NP2 - 1:
                    last.then_inc(sC["v_ps"], 1)
            pe.wait_ge(sB["route_ready"], 1)
            pe.wait_ge(sB["const"], 112)
            flat = sel[:].rearrange("p t e -> p (t e)")
            nc.tensor.matmul(ps[:, 5, 0:NT * E], tri[:], flat, start=True, stop=False, skip_group_check=True)
            for t in range(NT):
                last = nc.tensor.matmul(ps[:, 5, E * (t + 1):E * (NT + 1)].rearrange("p (a e) -> p a e", e=E), ones[:],
                                        bcast(sel[:, t], 1, NT - t), start=False, stop=t == NT - 1, skip_group_check=True)
            last.then_inc(sB["rank_ps"], 1)

            def output_values(b):
                pe.wait_ge(sC["v_sb"], b + 1)
                for m in range(NJ):
                    if b == 0 and m < 2:
                        pe.wait_ge(sC["a_sb"], 6)
                    wait(pe, sC["vw_sb"], NJ * b + m - 1)
                    for a in range(2):
                        c, j = (2 * m + a) // NJ, (2 * m + a) % NJ
                        pairs = [q for q in range(4) if -rows(j) < P * j - 2 * LK * q < 2 * LK]
                        for q in pairs:
                            w0_ = P + P * j - 2 * LK * q
                            last = nc.tensor.matmul(ps[0:rows(j), m % 2, D * a:D * a + D], vbdT[:, 4 * c + q, w0_:w0_ + rows(j)],
                                                    wout[:, 4 * c + q, :], start=q == pairs[0], stop=q == pairs[-1])
                    last.then_inc(sC["vw_ps"], 1)

            def route(g):
                pe.wait_ge(sB["payload"], 2)
                pe.wait_ge(sB["rowhot"], g + 1)
                for q in range(8 * g, 8 * g + 8):
                    last = nc.tensor.matmul(ps[:, 6, 0:2 * NCH], rowhot[:, g % 2, q % 8], payload[:, q].rearrange("p v c -> p (v c)"),
                                            start=q == 0, stop=q == TOP * NT - 1)
                last.then_inc(sB["rowhot_used"], 1)

            output_values(0)
            route(0)
            output_values(1)
            for g in range(1, 4):
                route(g)
            pe.wait_ge(sC["vw_sb"], 2 * NJ)
            for t in range(NT):
                last = nc.tensor.transpose(ps[0:E, t // 4, P * (t % 4):P * (t % 4) + P], sel[:, t, :], ident[:])
            last.then_inc(sB["ind_ps"], 1)
            pe.wait_ge(sB["route_ready"], 2)
            pe.wait_ge(sB["ind_sb"], 1)
            pe.wait_ge(w0_in, 96)

            def expert_of(it, s):
                return nc.tensor.value_load(ce_i[0:1, bass.ds(NSTR * it + s, 1)], min_val=0, max_val=E - 1)

            def transpose_step(it, k):
                s = k % NSTR
                if k < NSTR:
                    pe.wait_ge(gathered[s], 16 * (it + 1))
                    wait(pe, sB["l_sb"], STEPS * (it - 1) + STEPS - NSTR + s + 1)
                else:
                    pe.wait_ge(sB["l_sb"], STEPS * it + k - NSTR + 1)
                src = g0 if k < NSTR else h0
                for m in range(DK):
                    last = nc.tensor.transpose(ps[:, s, P * m:P * m + P], src[:, s, P * m:P * m + P], ident[:])
                last.then_inc(sB["tp_ps"], 1)

            def layer_step(it, k, e):
                l, s = k // NSTR, k % NSTR
                pe.wait_ge(sB["tp_sb"], STEPS * it + k + 1)
                for m in range(DK):
                    last = nc.tensor.matmul(ps[:, s, D:2 * D], hT[:, s, m, :], w0[:, bass.ds(e, 1), l, m, :].squeeze(1),
                                            start=m == 0, stop=m == DK - 1)
                last.then_inc(sB["l_ps"], 1)

            def chunks(it):
                transpose_step(it, 0)
                e = [expert_of(it, 0)]
                for k in range(1, STEPS):
                    transpose_step(it, k)
                    if k < NSTR:
                        e.append(expert_of(it, k))
                    layer_step(it, k - 1, e[(k - 1) % NSTR])
                layer_step(it, STEPS - 1, e[NSTR - 1])

            chunks(0)
            with pe.Fori(1, NIT) as it:
                chunks(it)
            pe.wait_ge(sB["v_done"], NCH)
            for e in range(E):
                last = nc.tensor.matmul(ps[0:E, 5, 0:D], unit[:, E - e:2 * E - e], vsum[:, e, :], start=e == 0, stop=e == E - 1)
            last.then_inc(sB["v_ps"], 1)
            pe.wait_ge(sB["v_sb"], 2)
            for k, m in enumerate(PAIRS):
                if k >= 4:
                    pe.wait_ge(sB["x2_ready"], k - 3)
                for q in range(2):
                    for t, v in enumerate((v0_hi, v0_lo)):
                        last = nc.tensor.matmul(ps[:, k % 4, D * q:D * q + D], indT[:, 2 * m + q, :], v[:], start=t == 0, stop=t == 1)
                last.then_inc(sB["o_ps"], 1)
            def transpose_tile(i, s):
                m = 2 * i + s
                wait(pe, sC["xn_ready"], m + 1)
                wait(pe, sC["rot_ready"], 4 * m - 1)
                for k in range(DK):
                    last = nc.tensor.transpose(ps[:, 6, P * k:P * k + P], xn[:, s % 2, P * k:P * k + P], ident[:])
                last.then_inc(sC["xT_ps"], 1)

            def latents(i, s):
                wait(pe, sC["xT_sb"], 2 * i + s + 1)
                for k in range(DK):
                    last = nc.tensor.matmul(ps[0:DQ, 6, D:D + P], wqd[:, k, :], xnT[:, s % 2, k, :], start=k == 0, stop=k == DK - 1)
                last.then_inc(sC["qc_ps"], 1)

            transpose_tile(0, 0)
            latents(0, 0)
            pe.wait_ge(sB["x2_ready"], NT // 2)
            pe.wait_ge(sC["const_lo"], 1)

            def body(i, u):
                n = 2 * i + u
                v = 1 - u

                def transpose_weights(c):
                    flat = pc[:, c].rearrange("p h k -> p (h k)")
                    wait(pe, sC["norm_done"], 2 * n + c + 1)
                    wait(pe, sC["lo_done"], 2 * n + c)
                    for j in range(3):
                        last = nc.tensor.transpose(PTA[:, j], flat[:, P * j:P * j + P], ident[:])
                    last.then_inc(sC["pta_ps"], 1)
                    nc.tensor.transpose(PTB[:, 0], flat[:, 3 * P:4 * P], ident[:])
                    nc.tensor.transpose(PTB[0:rows(4), 1], flat[:, 4 * P:UK], ident[:]).then_inc(sC["ptb_ps"], 1)

                def apply_weights(c):
                    wait(pe, sC["lo_done"], 2 * n + c + 1)
                    for j in range(NJ):
                        r = slice(0, rows(j))
                        for t, (a, w) in enumerate(((pcT_hi, vw_hi), (pcT_hi, vw_lo), (pcT_lo, vw_hi))):
                            last = nc.tensor.matmul(ps[:, 7, 0:D], a[r, c, j, :], w[r, u, c, j, :],
                                                    start=c == 0 and j == 0 and t == 0, stop=c == 1 and j == NJ - 1 and t == 2)
                    return last

                def project(g):
                    wait(pe, sC["rot_ready"], 4 * (n + 1) + g - 1)
                    if g == 1:
                        wait(pe, sC["x_ready"], n)
                    for q in range(2):
                        last = nc.tensor.matmul(ROPE[g % 2][:, P * q:P * q + P], wr[:, 2 * g + q, :], qc[:, v, :], start=True, stop=True)
                    last.then_inc(sC["rope_ps"], 1)

                def nope(g):
                    wait(pe, sC["mask_done"], 2 * n + 1 + g // 2)
                    for t, (q, w) in enumerate(((qc_hi, an_hi), (qc_hi, an_lo), (qc_lo, an_hi))):
                        nc.tensor.matmul(ps[:, g, 0:4 * LK], q[:, v, :], w[:, v, 4 * g:4 * g + 4, :].rearrange("p h k -> p (h k)"),
                                         start=t == 0, stop=False, skip_group_check=True)

                def rope(g):
                    wait(pe, sC["rot_ready"], 4 * (n + 1) + g + 1)
                    for q in range(2):
                        for w in range(2):
                            last = nc.tensor.matmul(ps[:, g, 2 * LK * q:2 * LK * (q + 1)], rot[:, g, w, q, :],
                                                    krbd[:, w, v].rearrange("p a k -> p (a k)"),
                                                    start=False, stop=q == 1 and w == 1, skip_group_check=True)
                    if g % 2:
                        last.then_inc(sC["s_ps"], 1)

                if live(i, u + 1):
                    wait(pe, sC["qc_sb"], n + 2)
                    project(0)
                if live(i, u):
                    transpose_weights(0)
                if isinstance(i, int) and n == 0:
                    pe.wait_ge(sC["const_lo"], 2)
                if live(i, u + 1):
                    wait(pe, sC["qlo"], n + 2)
                    nope(0)
                    project(1)
                    nope(1)
                    rope(0)
                    project(2)
                    rope(1)
                    nope(2)
                if live(i, u):
                    transpose_weights(1)
                if live(i, u + 1):
                    project(3)
                    nope(3)
                    rope(2)
                if live(i, u + 2):
                    transpose_tile(i, u + 2)
                if live(i, u + 1):
                    rope(3)
                if live(i, u):
                    if isinstance(i, int) and n in (0, 1):
                        pe.wait_ge(sC["vw_lo"], n + 1)
                    wait(pe, sC["x_ready"], n)
                    apply_weights(0)
                if live(i, u + 2):
                    latents(i, u + 2)
                if live(i, u):
                    last = apply_weights(1)
                    last.then_inc(sC["out_ps"], 1)

            pipeline(pe, body)
            pe.wait_ge(sC["lo_done"], 2 * NT)
            pe.wait_ge(sC["mask_done"], 2 * NT)

            def transpose_tile(i, s):
                m = 2 * i + s
                wait(pe, sD["xn_ready"], m + 1)
                wait(pe, sD["xT_sb"], m)
                for k in range(DK):
                    last = nc.tensor.transpose(ps[:, 4, P * k:P * k + P], xn[:, s % 2, P * k:P * k + P], ident[:])
                last.then_inc(sD["xT_ps"], 1)

            transpose_tile(0, 0)
            pe.wait_ge(sC["x_ready"], NT)
            pe.wait_ge(sD["w_in"], 48)
            pe.wait_ge(sD["we_lo"], NT)

            def body(i, u):
                n = 2 * i + u
                v = 1 - u

                def experts(g):
                    if g < 3:
                        wait(pe, sD["acc"], ACCS * (n - 1) + 2 * g + 3)
                    else:
                        wait(pe, sD["scaled"], n)
                    if g == 0:
                        wait(pe, sD["lo"], n + 1)
                    terms = [(a, w, k) for a, w in ((xhi, we_hi), (xhi, we_lo), (xlo, we_hi)) for k in range(DK)]
                    for t, (a, w, k) in enumerate(terms):
                        last = nc.tensor.matmul(ps[:, g, :], a[:, u, k, :], by_k(w)[:, k, 2 * D * g:2 * D * g + 2 * D],
                                                start=t == 0, stop=t == len(terms) - 1)
                    last.then_inc(sD["e_ps"], 1)

                if live(i, u + 1):
                    wait(pe, sD["xT_sb"], n + 2)
                    wait(pe, sD["chain"], LINKS * n + 1)
                    for k in range(DK):
                        last = nc.tensor.matmul(ps[:, 5, 0:E], xnT[:, v, k, :], wg[:, k, :], start=k == 0, stop=k == DK - 1)
                    last.then_inc(sD["lg_ps"], 1)
                if live(i, u):
                    experts(0)
                    wait(pe, sD["gT_sb"], n + 1)
                    wait(pe, sD["acc"], ACCS * (n - 1) + 1)
                    nc.tensor.matmul(ps[:, 7, 0:D], gatesT[:, u, :], be[:], start=True, stop=True).then_inc(sD["be_ps"], 1)
                if live(i, u + 2):
                    transpose_tile(i, u + 2)
                if live(i, u):
                    experts(1)
                    experts(2)
                    experts(3)
                if live(i, u + 1):
                    wait(pe, sD["chain"], LINKS * (n + 2))
                    wait(pe, sD["gT_sb"], n + 1)
                    nc.tensor.transpose(ps[0:E, 6, 0:P], gates[:, v, :], ident[:]).then_inc(sD["gT_ps"], 1)

            pipeline(pe, body)


_INS = ['x', 'ctx_1024', 'L0_xattn_Wq', 'L0_xattn_bq', 'L0_xattn_Wk', 'L0_xattn_bk', 'L0_xattn_Wv', 'L0_xattn_bv',
        'L0_xattn_Wo', 'L0_xattn_bo', 'L0_ffn_gate_w', 'L0_ffn_gate_b', 'L0_ffn_w1', 'L0_ffn_b1', 'L0_ffn_w2', 'L0_ffn_b2',
        'L0_ffn_w3', 'L0_ffn_b3', 'itok_BxS_0_511', 'L1_xattn_w_kv_comp', 'L1_xattn_w_q_down', 'L1_xattn_w_q_up', 'L1_xattn_w_q_rope',
        'L1_xattn_w_k_up', 'L1_xattn_w_k_rope', 'L1_xattn_w_v_up', 'L1_xattn_w_out', 'L1_ffn_Wg', 'L1_ffn_We', 'L1_ffn_be']


def constants():
    import numpy as np
    f = np.float32
    row = np.arange(P)
    c = {"c_ident": np.eye(P, dtype=f)}
    c["c_tri"] = (row[:, None] < row[None]).astype(f)
    c["c_ones"] = np.ones((P, P), f)
    c["c_iota"] = np.tile(row.astype(f), (P, 1))
    c["c_rev8"] = np.tile(np.arange(E, 0, -1).astype(f), (P, 1))
    c["c_tri8"] = np.tile(np.tril(np.ones((E, E), f)), (P, 1, 1))
    c["c_unit"] = np.zeros((P, 2 * E), f)
    c["c_unit"][:, E] = 1
    c["c_tokid"] = (np.arange(NT)[None] * P + row[:, None]).astype(f)
    half = RD // 2
    inv = (f(1.0) / f(10000.0) ** (np.arange(half, dtype=f) / f(half))).astype(f)
    ang = np.arange(S, dtype=f)[None] * inv[:, None]
    cos, sin = np.cos(ang).astype(f), np.sin(ang).astype(f)
    c["c_trig"] = np.stack([np.concatenate([cos] * 4), np.concatenate([sin, -sin] * 2)], 1)
    kc, ks = np.concatenate([cos, cos])[:, :LK], np.concatenate([-sin, sin])[:, :LK]
    c["c_ktrig"] = np.stack([np.concatenate([kc, kc]), np.concatenate([ks, ks])], 1)
    c["c_iok"] = np.tile(np.arange(LK, dtype=f), (P, 1))
    c["c_kmask"] = (row[:, None] // HD == np.arange(HC)[None]).astype(f)
    i = np.arange(NJ)[None, :] * P + row[:, None]
    c["c_vmask"] = ((i // LK)[:, :, None] == np.arange(HC)).astype(f)
    return c


def kernel(**inputs):
    import numpy as np
    import concourse.bacc as bacc
    from concourse import mybir as mb
    from concourse.bass_utils import run_bass_kernel_spmd as run
    nc = bacc.Bacc("TRN2", target_bir_lowering=False, num_devices=1)
    arrays, io = {}, {}
    data = {n: np.ascontiguousarray(inputs[n]) for n in _INS}
    for n in ('L0_xattn_bq', 'L0_xattn_bk'):
        data[n] = np.ascontiguousarray(data[n].reshape(2, P).T)
    data['itok_BxS_0_511'] = np.ascontiguousarray(data['itok_BxS_0_511'].reshape(NT, P).T)
    data['L1_xattn_w_q_up'] = np.ascontiguousarray(data['L1_xattn_w_q_up'].reshape(DQ, NP2, P).transpose(2, 1, 0))
    data['L0_ffn_gate_b'] = data['L0_ffn_gate_b'].reshape(E, 1)
    data.update(constants())
    for name, a in data.items():
        arrays[f"in_{name}"] = a
        io[name] = nc.dram_tensor(f"in_{name}", a.shape, mb.dt.from_np(a.dtype), kind="ExternalInput").ap()
    io["out"] = nc.dram_tensor("out_0", (B, S, D), mb.dt.float32, kind="ExternalOutput").ap()
    io["xn_dram"] = nc.dram_tensor("xn_dram", (B * S, D), mb.dt.float32).ap()
    build(nc, io)
    r = run(nc, [arrays], core_ids=[0])
    return r.results[0]["out_0"]
```
